# Optimizing a Trainium2 kernel written in Bass

```python
import numpy as np
import jax
import jax.numpy as jnp

def _softmax(x, axis=-1):
    return jax.nn.softmax(x, axis=axis)

def _gelu(x):
    return jax.nn.gelu(x, approximate=True)

def _silu(x):
    return jax.nn.silu(x)

def _sigmoid(x):
    return jax.nn.sigmoid(x)

def _layernorm(x, axis=-1, eps=1e-05):
    m = jnp.mean(x, axis=axis, keepdims=True)
    v = jnp.var(x, axis=axis, keepdims=True)
    return (x - m) / jnp.sqrt(v + eps)

def _scatter_add(tgt, idx, src, axis=0):
    return tgt.at[idx].add(src)

def _segment_sum(src, seg, n):
    return jax.ops.segment_sum(src, seg, n)
kernel_name = 'mk_decoder_postln_d1_seqx_r4_80c8ec'

def setup_inputs(seed: int=0):
    np.random.seed(seed)
    _w = jnp.asarray

    def _rec_inputs():
        import jax
        import jax.numpy as jnp
        _rk = jax.random.key(seed)
        x = -0.000125 + 0.9999 * jax.random.normal(jax.random.fold_in(_rk, 1), (2, 512, 1024), jnp.float32)
        _lenS = 512 - jax.random.randint(jax.random.fold_in(_rk, 7), (2,), 0, max(1, 512 // 4) + 1, jnp.int32)
        _lenS2 = 1024 - jax.random.randint(jax.random.fold_in(_rk, 8), (2,), 0, max(1, 1024 // 4) + 1, jnp.int32)
        _ctx_4096P = jax.random.normal(jax.random.fold_in(_rk, 11), (2, 16, 1024), jnp.float32)
        _ctx_4096c = jax.random.dirichlet(jax.random.fold_in(_rk, 511), 0.3 * jnp.ones((16,), jnp.float32), (2, 1024))
        _ctx_4096t = jnp.einsum('bsk,bkd->bsd', _ctx_4096c, _ctx_4096P)
        _ctx_4096t = _ctx_4096t * jax.lax.rsqrt(jnp.mean(jnp.square(_ctx_4096t)) + 1e-12) * 0.953939
        ctx_4096 = -5.72187e-05 + 0.999849 * (_ctx_4096t + 0.3 * jax.random.normal(jax.random.fold_in(_rk, 611), (2, 1024, 1024), jnp.float32))
        return (x, ctx_4096)
    x, ctx_4096 = _rec_inputs()

    def _L0_attn_setup():
        import jax, jax.numpy as jnp
        import numpy as np
        EMB = 1024
        HEADS = 32
        SCALE = 4
        D = EMB // HEADS
        HKV = HEADS // SCALE
        B, S = (2, 512)
        key = jax.random.key(seed)
        ks = jax.random.split(key, 7)
        std = 0.02
        return {'x': jax.random.normal(ks[0], (B, S, EMB), jnp.float32), 'Wq': jax.random.normal(ks[1], (EMB, D, HEADS), jnp.float32) * std, 'bq': jnp.zeros((D, HEADS), jnp.float32), 'Wk': jax.random.normal(ks[2], (EMB, D, HKV), jnp.float32) * std, 'bk': jnp.zeros((D, HKV), jnp.float32), 'Wv': jax.random.normal(ks[3], (EMB, D, HKV), jnp.float32) * std, 'bv': jnp.zeros((D, HKV), jnp.float32)}
    _L0_attn_all = _L0_attn_setup()
    _L0_attn_in = {k: v for k, v in _L0_attn_all.items() if k in ('Wq', 'bq', 'Wk', 'bk', 'Wv', 'bv')}
    del _L0_attn_all

    def _L0_xattn_setup():
        import jax, jax.numpy as jnp
        import numpy as np
        QMIN = 0.0
        QMAX = 255.0

        def fake_quant(x, scale, zp):
            s = scale.reshape(())
            z = zp.reshape(())
            q = jnp.clip(jnp.round(x / s + z), QMIN, QMAX)
            return (q - z) * s
        key = jax.random.key(seed)
        k1, k2 = jax.random.split(key)
        B, M, K, N = (4, 512, 1024, 1024)
        x1 = jax.random.normal(k1, (B, M, K), dtype=jnp.float32)
        x2 = jax.random.normal(k2, (B, K, N), dtype=jnp.float32)
        x1_scale = jnp.full((1,), 8.0 / 255.0, dtype=jnp.float32)
        x1_zp = jnp.full((1,), 128.0, dtype=jnp.float32)
        x2_scale = jnp.full((1,), 8.0 / 255.0, dtype=jnp.float32)
        x2_zp = jnp.full((1,), 128.0, dtype=jnp.float32)
        return {'x1': x1, 'x2': x2, 'x1_scale': x1_scale, 'x1_zp': x1_zp, 'x2_scale': x2_scale, 'x2_zp': x2_zp}
    _L0_xattn_all = _L0_xattn_setup()
    _L0_xattn_in = {k: v for k, v in _L0_xattn_all.items() if k in ('x1_scale', 'x1_zp', 'x2_scale', 'x2_zp')}
    del _L0_xattn_all

    def _L0_ffn_setup():
        import jax, jax.numpy as jnp
        import numpy as np
        HID, INT, LAT, NE, K = (1024, 2048, 512, 8, 2)
        LN_EPS = 1e-05

        def _layernorm(x, gamma, beta):
            mu = jnp.mean(x, axis=-1, keepdims=True)
            var = jnp.var(x, axis=-1, keepdims=True)
            return (x - mu) * jax.lax.rsqrt(var + LN_EPS) * gamma + beta
        key = jax.random.key(seed)
        ks = jax.random.split(key, 8)
        s = lambda d: 1.0 / np.sqrt(d)
        return {'hidden_states': jax.random.normal(ks[0], (4, 512, HID), jnp.float32), 'gate_w': jax.random.normal(ks[1], (HID, NE), jnp.float32) * s(HID), 'up_w': jax.random.normal(ks[2], (HID, INT), jnp.float32) * s(HID), 'down_w': jax.random.normal(ks[3], (INT, HID), jnp.float32) * s(INT), 'fc1_w': jax.random.normal(ks[4], (HID, LAT), jnp.float32) * s(HID), 'fc2_w': jax.random.normal(ks[5], (LAT, HID), jnp.float32) * s(LAT), 'expert_w': jax.random.normal(ks[6], (LAT, LAT), jnp.float32), 'ln_gamma': jnp.ones((HID,), jnp.float32), 'ln_beta': jnp.zeros((HID,), jnp.float32)}
    _L0_ffn_all = _L0_ffn_setup()
    _L0_ffn_in = {k: v for k, v in _L0_ffn_all.items() if k in ('gate_w', 'up_w', 'down_w', 'fc1_w', 'fc2_w', 'expert_w', 'ln_gamma', 'ln_beta')}
    del _L0_ffn_all
    return {'x': x, 'ctx_4096': ctx_4096, 'L0_attn_Wq': _L0_attn_in['Wq'], 'L0_attn_bq': _L0_attn_in['bq'], 'L0_attn_Wk': _L0_attn_in['Wk'], 'L0_attn_bk': _L0_attn_in['bk'], 'L0_attn_Wv': _L0_attn_in['Wv'], 'L0_attn_bv': _L0_attn_in['bv'], 'L0_xattn_x1_scale': _L0_xattn_in['x1_scale'], 'L0_xattn_x1_zp': _L0_xattn_in['x1_zp'], 'L0_xattn_x2_scale': _L0_xattn_in['x2_scale'], 'L0_xattn_x2_zp': _L0_xattn_in['x2_zp'], 'L0_ffn_gate_w': _L0_ffn_in['gate_w'], 'L0_ffn_up_w': _L0_ffn_in['up_w'], 'L0_ffn_down_w': _L0_ffn_in['down_w'], 'L0_ffn_fc1_w': _L0_ffn_in['fc1_w'], 'L0_ffn_fc2_w': _L0_ffn_in['fc2_w'], 'L0_ffn_expert_w': _L0_ffn_in['expert_w'], 'L0_ffn_ln_gamma': _L0_ffn_in['ln_gamma'], 'L0_ffn_ln_beta': _L0_ffn_in['ln_beta']}

def reference(x, ctx_4096, L0_attn_Wq, L0_attn_bq, L0_attn_Wk, L0_attn_bk, L0_attn_Wv, L0_attn_bv, L0_xattn_x1_scale, L0_xattn_x1_zp, L0_xattn_x2_scale, L0_xattn_x2_zp, L0_ffn_gate_w, L0_ffn_up_w, L0_ffn_down_w, L0_ffn_fc1_w, L0_ffn_fc2_w, L0_ffn_expert_w, L0_ffn_ln_gamma, L0_ffn_ln_beta):
    import jax
    import jax.numpy as jnp

    def _L0_attn_ref(x, Wq, bq, Wk, bk, Wv, bv):
        import jax, jax.numpy as jnp
        import numpy as np
        EMB = 1024
        HEADS = 32
        SCALE = 4
        D = EMB // HEADS
        HKV = HEADS // SCALE
        B, S = (2, 512)
        q = jnp.einsum('bse,edh->bsdh', x, Wq) + bq
        k = jnp.einsum('bse,edh->bsdh', x, Wk) + bk
        v = jnp.einsum('bse,edh->bsdh', x, Wv) + bv
        k = jnp.repeat(k, SCALE, axis=-1)
        v = jnp.repeat(v, SCALE, axis=-1)
        scores = jnp.einsum('bsdh,bseh->bsde', q, k) / np.float32(np.sqrt(D))
        attn = jax.nn.softmax(scores, axis=-1)
        out = jnp.einsum('bsde,bseh->bsdh', attn, v)
        return out.reshape(x.shape[:-1] + (EMB,))

    def _L0_xattn_ref(x1, x2, x1_scale, x1_zp, x2_scale, x2_zp):
        import jax, jax.numpy as jnp
        import numpy as np
        QMIN = 0.0
        QMAX = 255.0

        def fake_quant(x, scale, zp):
            s = scale.reshape(())
            z = zp.reshape(())
            q = jnp.clip(jnp.round(x / s + z), QMIN, QMAX)
            return (q - z) * s
        q1 = fake_quant(x1, x1_scale, x1_zp)
        q2 = fake_quant(x2, x2_scale, x2_zp)
        return jnp.matmul(q1, q2)

    def _L0_ffn_ref(hidden_states, gate_w, up_w, down_w, fc1_w, fc2_w, expert_w, ln_gamma, ln_beta):
        import jax, jax.numpy as jnp
        import numpy as np
        HID, INT, LAT, NE, K = (1024, 2048, 512, 8, 2)
        LN_EPS = 1e-05

        def _layernorm(x, gamma, beta):
            mu = jnp.mean(x, axis=-1, keepdims=True)
            var = jnp.var(x, axis=-1, keepdims=True)
            return (x - mu) * jax.lax.rsqrt(var + LN_EPS) * gamma + beta
        logits = jnp.einsum('bsh,he->bse', hidden_states, gate_w)
        routing_weights, selected_experts = jax.lax.top_k(logits, K)
        h = jax.nn.relu(jnp.einsum('bsh,hi->bsi', hidden_states, up_w)) ** 2
        shared_out = jnp.einsum('bsi,ih->bsh', h, down_w)
        x_latent = jnp.einsum('bsh,hl->bsl', hidden_states, fc1_w)
        expert_out = jnp.einsum('bsl,lm->bsm', x_latent, expert_w)
        moe_out = expert_out * jnp.sum(routing_weights, axis=-1, keepdims=True)
        routed_out = jnp.einsum('bsl,lh->bsh', moe_out, fc2_w)
        return _layernorm(shared_out + routed_out, ln_gamma, ln_beta)
    x = _layernorm(x + _L0_attn_ref(x, L0_attn_Wq, L0_attn_bq, L0_attn_Wk, L0_attn_bk, L0_attn_Wv, L0_attn_bv), axis=-1)
    x = _layernorm(x + _L0_xattn_ref(x, ctx_4096, L0_xattn_x1_scale, L0_xattn_x1_zp, L0_xattn_x2_scale, L0_xattn_x2_zp), axis=-1)
    x = _layernorm(x + _L0_ffn_ref(x, L0_ffn_gate_w, L0_ffn_up_w, L0_ffn_down_w, L0_ffn_fc1_w, L0_ffn_fc2_w, L0_ffn_expert_w, L0_ffn_ln_gamma, L0_ffn_ln_beta), axis=-1)
    return x

_drawn_inputs = setup_inputs


def setup_inputs(seed=0):
    import zlib

    import numpy as np

    out = dict(_drawn_inputs(seed))
    spreads = {'L0_attn_bq': (0.0, 0.506),
     'L0_attn_bk': (0.0, 0.517),
     'L0_attn_bv': (0.0, 0.331),
     'L0_ffn_ln_gamma': (1.0, 0.2),
     'L0_ffn_ln_beta': (0.0, 0.1)}
    factors = {}
    for name, (base, spread) in spreads.items():
        noise = np.random.default_rng([zlib.crc32(name.encode()), seed]).standard_normal(out[name].shape)
        drawn = base * np.exp(spread * noise) if base else spread * noise
        out[name] = jnp.asarray(drawn.astype(out[name].dtype))
    for name, factor in factors.items():
        out[name] = (out[name] * factor).astype(out[name].dtype)
    return out
```

```python
from contextlib import ExitStack

import concourse.bass as bass
from concourse import mybir

F32 = mybir.dt.float32
F32R = mybir.dt.float32r
BF16 = mybir.dt.bfloat16
ALU = mybir.AluOpType
ACT = mybir.ActivationFunctionType
AX = mybir.AxisListType

P = 128
BATCH, SEQ, EMB = 2, 512, 1024
TOKENS = BATCH * SEQ
TILES = TOKENS // P
HEADS, GROUPS = 32, 8
REP = HEADS // GROUPS
HD = EMB // HEADS
GD = GROUPS * HD
QKV = 3 * GD
KT = EMB // P
CTX = 1024
HID, LAT, EXPERTS = 2048, 512, 8
BANK = 512
NH = EMB // BANK
NG = P // 16
JQ = 4
TQ = 4
BT = SEQ // P
EPS = 1e-5
QMAX, QMID = 255.0, 128.0
MAGIC = 1.5 * 2.0 ** 23


def split_products(stationary, moving):
    (s_hi, s_lo), (m_hi, m_lo) = stationary, moving
    return ((s_hi, m_hi), (s_hi, m_lo), (s_lo, m_hi))


def prepare_weights(nc, sb_outer, args, w2_dram):
    w_hi, w_lo, bias = sb_outer["w_hi"], sb_outer["w_lo"], sb_outer["bias"]
    ident, maskj, maskt = sb_outer["ident"], sb_outer["maskj"], sb_outer["maskt"]
    MT = LAT // P
    with ExitStack() as ctx:
        sb = lambda name, shape, dt: ctx.enter_context(nc.sbuf_tensor(name, shape, dt))
        ps = lambda name, shape, dt: ctx.enter_context(nc.psum_tensor(name, shape, dt))
        sem = lambda name: ctx.enter_context(nc.semaphore(name))
        ex_raw = sb("ex_raw", [P, MT, LAT], F32)
        exT_hi, exT_lo = sb("exT_hi", [P, MT, LAT], F32R), sb("exT_lo", [P, MT, LAT], F32R)
        fc2_raw = sb("fc2_raw", [P, MT, EMB], F32)
        fc2_hi, fc2_lo = sb("fc2_hi", [P, MT, EMB], F32R), sb("fc2_lo", [P, MT, EMB], F32R)
        w2_sb = sb("w2_sb", [P, MT, EMB], F32)
        wq_raw = sb("wq_raw", [P, 2, EMB], F32)
        wkv_raw = sb("wkv_raw", [P, 2, 2, GD], F32)
        wq_sum = sb("wq_sum", [P, 2, GD], F32)
        bq_raw = sb("bq_raw", [P, EMB], F32)
        bkv_raw = sb("bkv_raw", [P, 2, GD], F32)
        exT_ps = ps("exT_ps", [P, 2, BANK], F32)
        w2_ps = ps("w2_ps", [P, 2, BANK], F32)

        ex_in, fc2_in, bias_in = sem("ex_in"), sem("fc2_in"), sem("bias_in")
        wraw_in = [sem("wraw_in0"), sem("wraw_in1")]
        ident_zero, ident_done = sem("ident_zero"), sem("ident_done")
        exT_ready, exT_hi_done, exT_lo_done = sem("exT_ready"), sem("exT_hi_done"), sem("exT_lo_done")
        fc2_hi_done, fc2_lo_done = sem("fc2_hi_done"), sem("fc2_lo_done")
        w2_ready, w2_evac = sem("w2_ready"), sem("w2_evac")
        w2_stored = sem("w2_stored")
        wq_summed, w_hi_done, w_lo_done = sem("wq_summed"), sem("w_hi_done"), sem("w_lo_done")
        masks_done, bias_done = sem("masks_done"), sem("bias_done")
        block = ctx.enter_context(nc.Block())

        @block.sync
        def _(sp):
            sp.dma_start(ex_raw[:], args["expert_w"].rearrange("(l p) m -> p l m", p=P)).then_inc(ex_in, 16)
            sp.dma_start(fc2_raw[:], args["fc2_w"].rearrange("(m p) n -> p m n", p=P)).then_inc(fc2_in, 16)
            wq = args["Wq"].rearrange("(k p) d h -> k p (d h)", p=P)
            wk = args["Wk"].rearrange("(k p) d h -> k p (d h)", p=P)
            wv = args["Wv"].rearrange("(k p) d h -> k p (d h)", p=P)
            for k in range(KT):
                if k >= 2:
                    sp.wait_ge(w_lo_done, k - 1)
                sp.dma_start(wq_raw[:, k % 2], wq[k]).then_inc(wraw_in[k % 2], 16)
                sp.dma_start(wkv_raw[:, k % 2, 0], wk[k]).then_inc(wraw_in[k % 2], 16)
                sp.dma_start(wkv_raw[:, k % 2, 1], wv[k]).then_inc(wraw_in[k % 2], 16)
            row = lambda a: a.rearrange("d h -> (d h)").partition_broadcast(P)
            sp.dma_start(bq_raw[:], row(args["bq"])).then_inc(bias_in, 16)
            sp.dma_start(bkv_raw[:, 0], row(args["bk"])).then_inc(bias_in, 16)
            sp.dma_start(bkv_raw[:, 1], row(args["bv"])).then_inc(bias_in, 16)
            for i, name in enumerate(("x1_scale", "x1_zp", "x2_scale", "x2_zp")):
                sp.dma_start(sb_outer["quant"][:, i:i + 1], args[name].partition_broadcast(P)).then_inc(bias_in, 16)
            for l in range(MT):
                sp.wait_ge(w2_evac, 2 * (l + 1))
                sp.dma_start(w2_dram[l * P:(l + 1) * P, :], w2_sb[:, l]).then_inc(w2_stored, 16)
            sp.wait_ge(w2_stored, 16 * MT)
            sp.wait_ge(bias_in, 16 * 7)

        @block.gpsimd
        def _(pool):
            pool.memset(ident[:], 0.0).then_inc(ident_zero, 1)
            pool.wait_ge(ident_zero, 1)
            pool.affine_select(out=ident[:], in_=ident[:], compare_op=ALU.not_equal, fill=1.0, base=0,
                               pattern=[[-1, P]], channel_multiplier=1).then_inc(ident_done, 1)
            pool.memset(sb_outer["ones_bf"][:], 1.0)
            pool.memset(sb_outer["neg_half"][:], -0.5)
            pool.memset(sb_outer["unmagic"][:], -(MAGIC + QMID))

        @block.tensor
        def _(pe):
            pe.wait_ge(ident_done, 1)
            pe.wait_ge(ex_in, 16)
            for m in range(MT):
                if m >= 2:
                    pe.wait_ge(exT_lo_done, m - 1)
                for l in range(MT):
                    mm = pe.transpose(exT_ps[:, m % 2, l * P:(l + 1) * P], ex_raw[:, l, m * P:(m + 1) * P], ident[:])
                mm.then_inc(exT_ready, 1)
            for l in range(MT):
                for n in range(NH):
                    q = l * NH + n
                    if q >= 2:
                        pe.wait_ge(w2_evac, q - 1)
                    for m in range(MT):
                        pe.wait_ge(exT_lo_done, m + 1)
                        pe.wait_ge(fc2_lo_done, m + 1)
                        st = [e[:, m, l * P:(l + 1) * P] for e in (exT_hi, exT_lo)]
                        mv = [f[:, m, n * BANK:(n + 1) * BANK] for f in (fc2_hi, fc2_lo)]
                        for i, (s, v) in enumerate(split_products(st, mv)):
                            mm = pe.matmul(w2_ps[:, q % 2], s, v, start=(m == 0 and i == 0), stop=(m == MT - 1 and i == 2))
                    mm.then_inc(w2_ready, 1)

        @block.scalar
        def _(act):
            act.wait_ge(fc2_in, 16)
            for m in range(MT):
                act.wait_ge(exT_ready, m + 1)
                act.activation(exT_hi[:, m], exT_ps[:, m % 2], ACT.Copy).then_inc(exT_hi_done, 1)
                act.activation(fc2_hi[:, m], fc2_raw[:, m], ACT.Copy).then_inc(fc2_hi_done, 1)

            def split_w(k):
                act.wait_ge(wq_summed, k + 1)
                act.activation(w_hi[:, k, 0:GD], wq_sum[:, k % 2], ACT.Copy)
                act.activation(w_hi[:, k, GD:QKV].rearrange("p (c g d) -> p c g d", c=2, g=GROUPS),
                               wkv_raw[:, k % 2].rearrange("p c (d g) -> p c g d", g=GROUPS),
                               ACT.Copy).then_inc(w_hi_done, 1)

            for q in range(MT * NH):
                split_w(q)
                act.wait_ge(w2_ready, q + 1)
                act.activation(w2_sb[:, q // NH, (q % NH) * BANK:(q % NH + 1) * BANK], w2_ps[:, q % 2],
                               ACT.Copy).then_inc(w2_evac, 1)

        @block.vector
        def _(dve):
            dve.wait_ge(ident_done, 1)
            dve.tensor_reduce(maskj[:], ident[:].rearrange("p (j r) -> p j r", j=JQ), AX.X, ALU.add).then_inc(masks_done, 1)
            dve.tensor_reduce(maskt[:], ident[:].rearrange("p (j t g) -> p t j g", j=JQ, t=TQ), AX.XY, ALU.add).then_inc(masks_done, 1)
            dve.tensor_copy(sb_outer["ident_bf"][:], ident[:])
            for m in range(MT):
                dve.wait_ge(exT_hi_done, m + 1)
                dve.tensor_tensor(exT_lo[:, m], exT_ps[:, m % 2], exT_hi[:, m].bitcast(F32), ALU.subtract).then_inc(exT_lo_done, 1)
                dve.wait_ge(fc2_hi_done, m + 1)
                dve.tensor_tensor(fc2_lo[:, m], fc2_raw[:, m], fc2_hi[:, m].bitcast(F32), ALU.subtract).then_inc(fc2_lo_done, 1)
            for k in range(KT):
                dve.wait_ge(wraw_in[k % 2], 48 * (k // 2 + 1))
                dve.tensor_reduce(wq_sum[:, k % 2].rearrange("p (g d) -> p g d", g=GROUPS),
                                  wq_raw[:, k % 2].rearrange("p (d g r) -> p g d r", g=GROUPS, r=REP),
                                  AX.X, ALU.add).then_inc(wq_summed, 1)
                dve.wait_ge(w_hi_done, k + 1)
                dve.wait_ge(wq_summed, k + 1)
                dve.tensor_tensor(w_lo[:, k, 0:GD], wq_sum[:, k % 2], w_hi[:, k, 0:GD].bitcast(F32), ALU.subtract)
                for c in range(2):
                    cols = slice((1 + c) * GD, (2 + c) * GD)
                    ins = dve.tensor_tensor(w_lo[:, k, cols].rearrange("p (g d) -> p g d", g=GROUPS),
                                            wkv_raw[:, k % 2, c].rearrange("p (d g) -> p g d", g=GROUPS),
                                            w_hi[:, k, cols].bitcast(F32).rearrange("p (g d) -> p g d", g=GROUPS),
                                            ALU.subtract)
                ins.then_inc(w_lo_done, 1)
            dve.wait_ge(bias_in, 16 * 7)
            dve.tensor_reduce(bias[:, 0:GD].rearrange("p (g d) -> p g d", g=GROUPS),
                              bq_raw[:].rearrange("p (d g r) -> p g d r", g=GROUPS, r=REP), AX.X, ALU.add)
            dve.tensor_copy(bias[:, GD:QKV].rearrange("p (c g d) -> p c g d", c=2, g=GROUPS),
                            bkv_raw[:].rearrange("p c (d g) -> p c g d", g=GROUPS))
            qp = sb_outer["quant"]
            dve.reciprocal(qp[:, 4:5], qp[:, 0:1])
            dve.reciprocal(qp[:, 5:6], qp[:, 2:3])
            dve.tensor_tensor(qp[:, 6:7], qp[:, 0:1], qp[:, 2:3], ALU.mult)
            dve.tensor_scalar(qp[:, 7:8], qp[:, 1:2], -1.0, QMID, ALU.mult, ALU.add)
            dve.tensor_scalar(qp[:, 8:9], qp[:, 3:4], -1.0, QMID, ALU.mult, ALU.add).then_inc(bias_done, 1)
            dve.wait_ge(bias_done, 1)
            dve.tensor_scalar(qp[:, 9:10], qp[:, 8:9], float(CTX), None, ALU.mult)


def attention_and_cross(nc, so, args, qkv_dram, o_dram, x2_dram):
    w_hi, w_lo, bias, ident = so["w_hi"], so["w_lo"], so["bias"], so["ident"]
    maskj, maskt, qp = so["maskj"], so["maskt"], so["quant"]
    CK = CTX // P
    XR = 3
    with ExitStack() as ctx:
        sb = lambda name, shape, dt: ctx.enter_context(nc.sbuf_tensor(name, shape, dt))
        ps = lambda name, shape, dt: ctx.enter_context(nc.psum_tensor(name, shape, dt))
        sem = lambda name: ctx.enter_context(nc.semaphore(name))
        x_sb = sb("x_sb", [P, 2, EMB], F32)
        xT_hi, xT_lo = sb("xT_hi", [P, 2, KT, P], F32R), sb("xT_lo", [P, 2, KT, P], F32R)
        qkv_sb = sb("qkv_sb", [P, 2, 3, GD], F32)
        pg = sb("pg", [P, 2, 3, NG, HD], F32)
        q_bd, k_bd = sb("q_bd", [P, 2, NG, JQ, HD], F32), sb("k_bd", [P, 2, NG, TQ, HD], F32)
        vT, v_bd = sb("vT", [P, 2, NG, HD], F32), sb("v_bd", [P, 2, NG, JQ, HD], F32)
        sm = sb("sm", [P, 2, NG * TQ, HD], F32)
        smT = sb("smT", [P, 2, NG, TQ * HD], F32)
        s_max, s_sum = sb("s_max", [P, 2, NG * TQ], F32), sb("s_sum", [P, 2, NG * TQ], F32)
        s_rec = sb("s_rec", [P, 2, NG * TQ], F32)
        o_sb = sb("o_sb", [P, 2, NG, HD], F32)
        o_tok = sb("o_tok", [P, 2, GD], F32)
        res = sb("res", [P, XR, EMB], F32)
        y_sb = sb("y_sb", [P, EMB], F32)
        q1 = sb("q1", [P, 2, EMB], BF16)
        q1T = sb("q1T", [P, 2, KT, P], BF16)
        q2 = sb("q2", [P, BATCH, CK, EMB], BF16)
        c_sb = sb("c_sb", [P, 2, EMB], F32)
        col = sb("col", [P, EMB], F32)
        xa_out = sb("xa_out", [P, EMB], F32)
        stat, mv = sb("stat", [P, 4, NH, 6], F32), sb("mv", [P, 4, 2], F32)
        veps, rstd = sb("veps", [P, 4], F32), sb("rstd", [P, 4], F32)
        rowsum, rowterm = sb("rowsum", [P, 4], F32), sb("rowterm", [P, 4], F32)
        tr_ps = ps("tr_ps", [P, KT, P], F32)
        qkv_ps = ps("qkv_ps", [P, 2 * BANK], F32)
        sc_ps = ps("sc_ps", [P, NG * TQ, HD], F32)
        xa_ps = ps("xa_ps", [P, EMB], F32)
        q1T_ps = tr_ps[:, 0:KT // 2, :].rearrange("p k c -> p (k c)").bitcast(BF16).rearrange("p (k c) -> p k c", k=KT)
        av_ps = qkv_ps[:].rearrange("p (n t d) -> p n t d", n=NG, t=TQ)

        x_in = [sem("x_in0"), sem("x_in1")]
        c_in = [sem("c_in0"), sem("c_in1")]
        pg_in = [sem("pg_in0"), sem("pg_in1")]
        o_in = [sem("o_in0"), sem("o_in1")]
        res_in = [sem(f"res_in{i}") for i in range(XR)]
        qkv_st = [sem("qkv_st0"), sem("qkv_st1")]
        o_st = [sem("o_st0"), sem("o_st1")]
        x2_st = [sem(f"x2_st{i}") for i in range(XR)]
        names = """xT_ready xT_hi_done xT_lo_done qkv_ready qkv_evac q_bd_done k_bd_done vT_done v_bd_done
            scores_ready max_done sub_done exp_done sum_done rec_done norm_done smT_done av_ready o_part o_done
            pre_done st1_done mv1_done ve1_done rstd1_done x1_done relu_done magic_done q1_done q1T_ready q1T_done
            xa_ready xa_add rowterm_done x2pre_done st2_done mv2_done ve2_done rstd2_done x2_done
            c_relu c_magic c_done col_ready col_done""".split()
        S = {n: sem(n) for n in names}
        block = ctx.enter_context(nc.Block())
        steps = range(-1, TILES + 6)
        in_range = lambda t: 0 <= t < TILES

        x_tiles = args["x"].rearrange("b (t p) e -> (b t) p e", p=P)
        c_tiles = args["ctx"].rearrange("b (k p) e -> (b k) p e", p=P)
        by_group = lambda d, t: d[t * P:(t + 1) * P, :].rearrange("(n a) (g d) -> (a g) n d", n=NG, g=GROUPS)

        @block.sync
        def _(sp):
            def load_x(t):
                if t >= 2:
                    sp.wait_ge(S["xT_ready"], t - 1)
                sp.dma_start(x_sb[:, t % 2], x_tiles[t]).then_inc(x_in[t % 2], 16)

            def load_ctx(c):
                if c >= 2:
                    sp.wait_ge(S["c_done"], c - 1)
                sp.dma_start(c_sb[:, c % 2], c_tiles[c]).then_inc(c_in[c % 2], 16)

            load_x(0)
            load_x(1)
            for s in range(TILES + 7):
                if in_range(s - 6):
                    t = s - 6
                    sp.wait_ge(S["x2_done"], t + 1)
                    sp.dma_start(x2_dram[t * P:(t + 1) * P, :], res[:, t % XR]).then_inc(x2_st[t % XR], 16)
                if in_range(s):
                    if s + 2 < TILES:
                        load_x(s + 2)
                    load_ctx(2 * s)
                    load_ctx(2 * s + 1)
                if in_range(s - 3):
                    t = s - 3
                    sp.wait_ge(S["o_done"], t + 1)
                    sp.dma_start(by_group(o_dram, t), o_sb[:, t % 2]).then_inc(o_st[t % 2], 16)
                    if t >= XR:
                        sp.wait_ge(x2_st[t % XR], 16 * (t // XR))
                    sp.dma_start(res[:, t % XR], x_tiles[t]).then_inc(res_in[t % XR], 16)
                    sp.wait_ge(o_st[t % 2], 16 * (t // 2 + 1))
                    if t >= 2:
                        sp.wait_ge(S["pre_done"], t - 1)
                    sp.dma_start(o_tok[:, t % 2], o_dram[t * P:(t + 1) * P, :]).then_inc(o_in[t % 2], 16)
                if in_range(s):
                    sp.wait_ge(S["qkv_evac"], s + 1)
                    sp.dma_start(qkv_dram[:, s * P:(s + 1) * P, :].rearrange("c t x -> t c x"),
                                 qkv_sb[:, s % 2]).then_inc(qkv_st[s % 2], 16)
                    sp.wait_ge(qkv_st[s % 2], 16 * (s // 2 + 1))
                    if s >= 2:
                        sp.wait_ge(S["q_bd_done"], s - 1)
                        sp.wait_ge(S["k_bd_done"], s - 1)
                        sp.wait_ge(S["vT_done"], s - 1)
                    for c in range(3):
                        sp.dma_start(pg[:, s % 2, c], by_group(qkv_dram[c], s)).then_inc(pg_in[s % 2], 16)
            for i in range(XR):
                sp.wait_ge(x2_st[i], 16 * len(range(i, TILES, XR)))

        @block.tensor
        def _(pe):
            def transpose_x(t):
                pe.wait_ge(x_in[t % 2], 16 * (t // 2 + 1))
                if t >= 1:
                    pe.wait_ge(S["xT_lo_done"], t)
                if in_range(t - 6):
                    pe.wait_ge(S["q1T_done"], t - 5)
                for k in range(KT):
                    mm = pe.transpose(tr_ps[:, k], x_sb[:, t % 2, k * P:(k + 1) * P], ident[:])
                mm.then_inc(S["xT_ready"], 1)

            def project(t):
                pe.wait_ge(S["xT_lo_done"], t + 1)
                if t >= 1:
                    pe.wait_ge(S["qkv_evac"], t)
                if t >= 3:
                    pe.wait_ge(S["o_done"], t - 2)
                for k in range(KT):
                    st = [x[:, t % 2, k] for x in (xT_hi, xT_lo)]
                    for i in range(3):
                        for c0, c1 in ((0, BANK), (BANK, QKV)):
                            s, v = split_products(st, [w[:, k, c0:c1] for w in (w_hi, w_lo)])[i]
                            mm = pe.matmul(qkv_ps[:, c0:c1], s, v, start=(k == 0 and i == 0), stop=(k == KT - 1 and i == 2))
                mm.then_inc(S["qkv_ready"], 1)

            def scores(t):
                pe.wait_ge(S["q_bd_done"], t + 1)
                pe.wait_ge(S["k_bd_done"], t + 1)
                if t >= 1:
                    pe.wait_ge(S["sub_done"], t)
                for n in range(NG):
                    mm = pe.matmul(sc_ps[:, n * TQ:(n + 1) * TQ, :], q_bd[:, t % 2, n], k_bd[:, t % 2, n], start=True, stop=True)
                mm.then_inc(S["scores_ready"], 1)

            def values(t):
                pe.wait_ge(S["smT_done"], t + 1)
                pe.wait_ge(S["v_bd_done"], t + 1)
                pe.wait_ge(S["qkv_evac"], min(t + 3, TILES))
                for n in range(NG):
                    mm = pe.matmul(av_ps[:, n], v_bd[:, t % 2, n], smT[:, t % 2, n], start=True, stop=True)
                mm.then_inc(S["av_ready"], 1)

            def transpose_q1(t):
                pe.wait_ge(S["q1_done"], t + 1)
                pe.wait_ge(S["xT_lo_done"], min(t + 6, TILES))
                if t >= 1:
                    pe.wait_ge(S["q1T_done"], t)
                for k in range(KT):
                    mm = pe.transpose(q1T_ps[:, k], q1[:, t % 2, k * P:(k + 1) * P], so["ident_bf"][:])
                mm.then_inc(S["q1T_ready"], 1)

            def cross(t):
                pe.wait_ge(S["q1T_done"], t + 1)
                b = t // BT
                pe.wait_ge(S["c_done"], (b + 1) * CK)
                if t >= 1:
                    pe.wait_ge(S["xa_add"], t)
                if t % BT == 0:
                    for n in range(NH):
                        for k in range(CK):
                            mm = pe.matmul(xa_ps[:, n * BANK:(n + 1) * BANK], so["ones_bf"][:], q2[:, b, k, n * BANK:(n + 1) * BANK],
                                           start=(k == 0), stop=(k == CK - 1))
                    mm.then_inc(S["col_ready"], 1)
                    pe.wait_ge(S["col_done"], b + 1)
                for k in range(CK):
                    for n in range(NH):
                        mm = pe.matmul(xa_ps[:, n * BANK:(n + 1) * BANK], q1T[:, t % 2, k], q2[:, b, k, n * BANK:(n + 1) * BANK],
                                       start=(k == 0), stop=(k == CK - 1))
                mm.then_inc(S["xa_ready"], 1)

            for s in steps:
                if in_range(s - 3):
                    values(s - 3)
                if in_range(s - 5):
                    transpose_q1(s - 5)
                if in_range(s):
                    project(s)
                if in_range(s - 1):
                    scores(s - 1)
                if in_range(s + 1):
                    transpose_x(s + 1)
                if in_range(s - 5):
                    cross(s - 5)

        @block.scalar
        def _(act):
            def softmax_exp(t):
                act.wait_ge(S["sub_done"], t + 1)
                act.activation(sm[:, t % 2], sm[:, t % 2], ACT.Exp, scale=float(HD) ** -0.5).then_inc(S["exp_done"], 1)

            def query_diagonal(t):
                act.wait_ge(pg_in[t % 2], 48 * (t // 2 + 1))
                if t >= 2:
                    act.wait_ge(S["scores_ready"], t - 1)
                for j in range(JQ):
                    ins = act.activation(q_bd[:, t % 2, :, j, :], pg[:, t % 2, 0], ACT.Copy, scale=maskj[:, j:j + 1])
                ins.then_inc(S["q_bd_done"], 1)

            def q1T_out(t):
                act.wait_ge(S["q1T_ready"], t + 1)
                if t >= 2:
                    act.wait_ge(S["xa_ready"], t - 1)
                act.activation(q1T[:, t % 2], q1T_ps, ACT.Copy).then_inc(S["q1T_done"], 1)

            def quantise_a(t):
                act.wait_ge(S["x1_done"], t + 1)
                if t >= 1:
                    act.wait_ge(S["q1_done"], t)
                act.activation(y_sb[:], res[:, t % XR], ACT.Relu, bias=qp[:, 1:2], scale=qp[:, 4:5]).then_inc(S["relu_done"], 1)

            def quantise_b(t):
                act.wait_ge(S["magic_done"], t + 1)
                if t >= 2:
                    act.wait_ge(S["q1T_ready"], t - 1)
                act.activation(q1[:, t % 2], y_sb[:], ACT.Identity, bias=so["unmagic"][:], accum_out=rowsum[:, t % 4:t % 4 + 1]).then_inc(S["q1_done"], 1)

            def xT_hi_out(t):
                act.wait_ge(S["xT_ready"], t + 1)
                if t >= 2:
                    act.wait_ge(S["qkv_ready"], t - 1)
                act.activation(xT_hi[:, t % 2], tr_ps[:], ACT.Copy).then_inc(S["xT_hi_done"], 1)

            def ctx_a(c):
                act.wait_ge(c_in[c % 2], 16 * (c // 2 + 1))
                act.activation(c_sb[:, c % 2], c_sb[:, c % 2], ACT.Relu, bias=qp[:, 3:4], scale=qp[:, 5:6]).then_inc(S["c_relu"], 1)

            def ctx_b(c):
                act.wait_ge(S["c_magic"], c + 1)
                act.activation(q2[:, c // CK, c % CK], c_sb[:, c % 2], ACT.Identity, bias=so["unmagic"][:]).then_inc(S["c_done"], 1)

            for s in steps:
                if in_range(s - 2):
                    softmax_exp(s - 2)
                if in_range(s - 1):
                    query_diagonal(s - 1)
                if in_range(s - 5):
                    q1T_out(s - 5)
                if in_range(s):
                    ctx_a(2 * s)
                    ctx_a(2 * s + 1)
                if in_range(s - 4):
                    quantise_a(s - 4)
                if in_range(s + 1):
                    xT_hi_out(s + 1)
                if in_range(s):
                    ctx_b(2 * s)
                    ctx_b(2 * s + 1)
                if in_range(s - 4):
                    quantise_b(s - 4)

        @block.vector
        def _(dve):
            def stats(t, first, st_done, mv_done):
                slot = t % 2 + (0 if first else 2)
                for n in range(NH):
                    ins = dve.bn_stats(stat[:, slot, n], res[:, t % XR, n * BANK:(n + 1) * BANK])
                ins.then_inc(st_done, 1)
                dve.wait_ge(st_done, t + 1)
                dve.bn_aggr(mv[:, slot], stat[:, slot].rearrange("p n s -> p (n s)")).then_inc(mv_done, 1)

            def normalise(t, first, rstd_done, done):
                slot = t % 2 + (0 if first else 2)
                dve.wait_ge(rstd_done, t + 1)
                dve.tensor_scalar(res[:, t % XR], res[:, t % XR], mv[:, slot, 0:1], rstd[:, slot:slot + 1],
                                  ALU.subtract, ALU.mult).then_inc(done, 1)

            def cross_residual(t):
                b = t // BT
                dve.wait_ge(S["xa_ready"], t + 1)
                dve.wait_ge(S["rowterm_done"], t + 1)
                dve.scalar_tensor_tensor(out=xa_out[:], in0=xa_ps[:], scalar=rowterm[:, t % 4:t % 4 + 1], in1=col[:],
                                         op0=ALU.add, op1=ALU.add).then_inc(S["xa_add"], 1)
                dve.wait_ge(S["xa_add"], t + 1)
                dve.scalar_tensor_tensor(out=res[:, t % XR], in0=xa_out[:], scalar=qp[:, 6:7], in1=res[:, t % XR],
                                         op0=ALU.mult, op1=ALU.add).then_inc(S["x2pre_done"], 1)
                dve.wait_ge(S["x2pre_done"], t + 1)
                stats(t, False, S["st2_done"], S["mv2_done"])

            def softmax_max(t):
                dve.wait_ge(S["scores_ready"], t + 1)
                dve.tensor_reduce(s_max[:, t % 2], sc_ps[:], AX.X, ALU.max).then_inc(S["max_done"], 1)
                dve.wait_ge(S["max_done"], t + 1)
                if t >= 2:
                    dve.wait_ge(S["smT_done"], t - 1)
                dve.tensor_tensor(sm[:, t % 2], sc_ps[:], s_max[:, t % 2].unsqueeze(2).to_broadcast([P, NG * TQ, HD]),
                                  ALU.subtract).then_inc(S["sub_done"], 1)

            def diagonals(t):
                dve.wait_ge(pg_in[t % 2], 48 * (t // 2 + 1))
                if t >= 2:
                    dve.wait_ge(S["v_bd_done"], t - 1)
                    dve.wait_ge(S["scores_ready"], t - 1)
                dve.transpose(vT[:, t % 2].rearrange("p n c -> p (n c)"), pg[:, t % 2, 2].rearrange("p n c -> p (n c)")).then_inc(S["vT_done"], 1)
                for q in range(TQ):
                    ins = dve.tensor_scalar(k_bd[:, t % 2, :, q, :], pg[:, t % 2, 1], maskt[:, q:q + 1], None, ALU.mult)
                ins.then_inc(S["k_bd_done"], 1)

            def collect(t):
                dve.wait_ge(S["av_ready"], t + 1)
                if t >= 2:
                    dve.wait_ge(o_st[t % 2], 16 * (t // 2))
                dve.tensor_scalar(o_sb[:, t % 2], av_ps[:, :, 0, :], maskt[:, 0:1], None, ALU.mult).then_inc(S["o_part"], 1)
                for q in range(1, TQ):
                    dve.wait_ge(S["o_part"], (TQ - 1) * t + q)
                    ins = dve.scalar_tensor_tensor(out=o_sb[:, t % 2], in0=av_ps[:, :, q, :], scalar=maskt[:, q:q + 1],
                                                   in1=o_sb[:, t % 2], op0=ALU.mult, op1=ALU.add)
                    ins.then_inc(S["o_part"] if q < TQ - 1 else S["o_done"], 1)

            def residual(t):
                dve.wait_ge(res_in[t % XR], 16 * (t // XR + 1))
                dve.wait_ge(o_in[t % 2], 16 * (t // 2 + 1))
                x = res[:, t % XR].rearrange("p (d g r) -> p d g r", g=GROUPS, r=REP)
                o = o_tok[:, t % 2].rearrange("p (g d) -> p d g", g=GROUPS).unsqueeze(3).to_broadcast([P, HD, GROUPS, REP])
                dve.tensor_tensor(x, x, o, ALU.add).then_inc(S["pre_done"], 1)
                dve.wait_ge(S["pre_done"], t + 1)
                stats(t, True, S["st1_done"], S["mv1_done"])

            def softmax_sum(t):
                dve.wait_ge(S["exp_done"], t + 1)
                dve.tensor_reduce(s_sum[:, t % 2], sm[:, t % 2], AX.X, ALU.add).then_inc(S["sum_done"], 1)
                dve.wait_ge(S["sum_done"], t + 1)
                dve.reciprocal(s_rec[:, t % 2], s_sum[:, t % 2]).then_inc(S["rec_done"], 1)

            def magic(t):
                dve.wait_ge(S["relu_done"], t + 1)
                dve.tensor_scalar(y_sb[:], y_sb[:], QMAX, MAGIC, ALU.min, ALU.add).then_inc(S["magic_done"], 1)

            def ctx_magic(c):
                dve.wait_ge(S["c_relu"], c + 1)
                dve.tensor_scalar(c_sb[:, c % 2], c_sb[:, c % 2], QMAX, MAGIC, ALU.min, ALU.add).then_inc(S["c_magic"], 1)

            def qkv_out(t):
                dve.wait_ge(S["qkv_ready"], t + 1)
                if t >= 2:
                    dve.wait_ge(qkv_st[t % 2], 16 * (t // 2))
                dve.tensor_tensor(qkv_sb[:, t % 2].rearrange("p c x -> p (c x)"), qkv_ps[:, 0:QKV], bias[:], ALU.add).then_inc(S["qkv_evac"], 1)

            def xT_lo_out(t):
                dve.wait_ge(S["xT_hi_done"], t + 1)
                dve.tensor_tensor(xT_lo[:, t % 2], tr_ps[:], xT_hi[:, t % 2].bitcast(F32), ALU.subtract).then_inc(S["xT_lo_done"], 1)

            def softmax_transpose(t):
                dve.wait_ge(S["norm_done"], t + 1)
                if t >= 2:
                    dve.wait_ge(S["av_ready"], t - 1)
                dve.transpose(smT[:, t % 2].rearrange("p n c -> p (n c)"), sm[:, t % 2].rearrange("p n c -> p (n c)")).then_inc(S["smT_done"], 1)

            for s in steps:
                if in_range(s - 6):
                    cross_residual(s - 6)
                if in_range(s - 2):
                    softmax_max(s - 2)
                if in_range(s - 1):
                    diagonals(s - 1)
                if in_range(s - 3):
                    collect(s - 3)
                if in_range(s - 4):
                    residual(s - 4)
                if in_range(s - 6):
                    normalise(s - 6, False, S["rstd2_done"], S["x2_done"])
                if in_range(s - 2):
                    softmax_sum(s - 2)
                if in_range(s):
                    ctx_magic(2 * s)
                    ctx_magic(2 * s + 1)
                if in_range(s - 4):
                    normalise(s - 4, True, S["rstd1_done"], S["x1_done"])
                    magic(s - 4)
                if in_range(s):
                    qkv_out(s)
                if in_range(s + 1):
                    xT_lo_out(s + 1)
                if in_range(s - 2):
                    softmax_transpose(s - 2)
                if in_range(s - 5) and (s - 5) % BT == 0:
                    dve.wait_ge(S["col_ready"], (s - 5) // BT + 1)
                    dve.tensor_scalar(col[:], xa_ps[:], qp[:, 9:10], qp[:, 7:8], ALU.add, ALU.mult).then_inc(S["col_done"], 1)

        @block.gpsimd
        def _(pool):
            def values_diagonal(t):
                pool.wait_ge(S["vT_done"], t + 1)
                if t >= 2:
                    pool.wait_ge(S["av_ready"], t - 1)
                for j in range(JQ):
                    ins = pool.tensor_scalar(v_bd[:, t % 2, :, j, :], vT[:, t % 2], maskj[:, j:j + 1], 1.0, ALU.mult, ALU.mult)
                ins.then_inc(S["v_bd_done"], 1)

            def inverse_deviation(t, first, mv_done, ve_done, rstd_done):
                slot = t % 2 + (0 if first else 2)
                pool.wait_ge(mv_done, t + 1)
                pool.tensor_scalar(veps[:, slot:slot + 1], mv[:, slot, 1:2], EPS, 1.0, ALU.add, ALU.mult).then_inc(ve_done, 1)
                pool.wait_ge(ve_done, t + 1)
                pool.tensor_tensor(rstd[:, slot:slot + 1], veps[:, slot:slot + 1], so["neg_half"][:], ALU.pow).then_inc(rstd_done, 1)

            def softmax_scale(t):
                pool.wait_ge(S["rec_done"], t + 1)
                pool.tensor_tensor(sm[:, t % 2], sm[:, t % 2], s_rec[:, t % 2].unsqueeze(2).to_broadcast([P, NG * TQ, HD]),
                                   ALU.mult).then_inc(S["norm_done"], 1)

            def row_term(t):
                pool.wait_ge(S["q1_done"], t + 1)
                pool.tensor_scalar(rowterm[:, t % 4:t % 4 + 1], rowsum[:, t % 4:t % 4 + 1], qp[:, 8:9], 1.0, ALU.mult, ALU.mult).then_inc(S["rowterm_done"], 1)

            for s in steps:
                if in_range(s - 6):
                    inverse_deviation(s - 6, False, S["mv2_done"], S["ve2_done"], S["rstd2_done"])
                if in_range(s - 1):
                    values_diagonal(s - 1)
                if in_range(s - 4):
                    inverse_deviation(s - 4, True, S["mv1_done"], S["ve1_done"], S["rstd1_done"])
                if in_range(s - 2):
                    softmax_scale(s - 2)
                if in_range(s - 5):
                    row_term(s - 5)


KH = HID // P
KL = LAT // P
KD = KH + KL
WT = KL + KH


def feed_forward(nc, so, args, x2_dram, w2_dram, out):
    ident = so["ident"]
    with ExitStack() as ctx:
        sb = lambda name, shape, dt: ctx.enter_context(nc.sbuf_tensor(name, shape, dt))
        ps = lambda name, shape, dt: ctx.enter_context(nc.psum_tensor(name, shape, dt))
        sem = lambda name: ctx.enter_context(nc.semaphore(name))
        XS = 4
        xk = sb("xk", [P, XS, BT, P], F32)
        x2T_hi, x2T_lo = sb("x2T_hi", [P, KT, SEQ], F32R), sb("x2T_lo", [P, KT, SEQ], F32R)
        h_hi, h_lo = sb("h_hi", [P, KD, SEQ], F32R), sb("h_lo", [P, KD, SEQ], F32R)
        u_raw = sb("u_raw", [P, 2, KT, P], F32)
        u_hi, u_lo = sb("u_hi", [P, 2, KT, P], F32R), sb("u_lo", [P, 2, KT, P], F32R)
        d_raw = sb("d_raw", [P, 2, BANK], F32)
        d_hi, d_lo = sb("d_hi", [P, 2, BANK], F32R), sb("d_lo", [P, 2, BANK], F32R)
        act_sb = sb("act_sb", [P, 2, SEQ], F32)
        rT = sb("rT", [P, SEQ], F32)
        gate_raw = sb("gate_raw", [P, KT, EXPERTS], F32)
        gate_hi, gate_lo = sb("gate_hi", [P, KT, EXPERTS], F32R), sb("gate_lo", [P, KT, EXPERTS], F32R)
        top = sb("top", [P, BT, 8], F32)
        r_tok, r_diag = sb("r_tok", [P, BT], F32), sb("r_diag", [P, BT, P], F32)
        ones = sb("ones", [P, P], F32)
        ffn = sb("ffn", [P, BT, EMB], F32)
        x2r = sb("x2r", [P, 2, EMB], F32)
        gamma, beta = sb("gamma", [P, EMB], F32), sb("beta", [P, EMB], F32)
        stat, mv = sb("stat_f", [P, 2, NH, 6], F32), sb("mv_f", [P, 2, 2], F32)
        veps, rstd = sb("veps_f", [P, 2], F32), sb("rstd_f", [P, 2], F32)
        acc = ps("acc", [P, BT, BANK], F32)
        u_ps = ps("u_ps", [P, 2, BANK], F32)
        t_ps = ps("t_ps", [P, 2, BANK], F32)

        xk_in = [sem(f"xk_in{i}") for i in range(XS)]
        u_in, d_in = [sem("u_in0"), sem("u_in1")], [sem("d_in0"), sem("d_in1")]
        x2r_in = [sem("x2r_in0"), sem("x2r_in1")]
        const_in, gate_in, out_st = sem("const_in"), sem("gate_in"), sem("out_st")
        names = """ones_done gate_hi_done gate_lo_done x2T_ready x2T_hi_done x2T_lo_done logits_ready top_done
            r_done rdiag_done rT_ready rT_done u_hi_done u_lo_done u_ready lat_scaled act_done h_hi_done sq_done
            h_lo_done d_hi_done d_lo_done d_used acc_ready acc_evac stA_done mvA_done veA_done rsA_done
            nA_done gam_done bet_done res_done stB_done mvB_done veB_done rsB_done out_done""".split()
        S = {n: sem("f_" + n) for n in names}
        block = ctx.enter_context(nc.Block())

        u_src = [args["fc1_w"].rearrange("(k p) (m c) -> m p k c", p=P, c=P),
                 args["up_w"].rearrange("(k p) (m c) -> m p k c", p=P, c=P)]
        out_rows = out.rearrange("b s e -> (b s) e")
        NB = NH * KD

        @block.sync
        def _(sp):
            def load_xk(b, k):
                i = b * KT + k
                if i >= XS:
                    sp.wait_ge(S["x2T_ready"], i - XS + 1)
                src = x2_dram[b * SEQ:(b + 1) * SEQ, k * P:(k + 1) * P].rearrange("(t p) c -> p t c", p=P)
                sp.dma_start(xk[:, i % XS], src).then_inc(xk_in[i % XS], 16)

            def load_u(b, m):
                i = b * WT + m
                if i >= 2:
                    sp.wait_ge(S["u_lo_done"], i - 1)
                sp.dma_start(u_raw[:, i % 2], u_src[0][m] if m < KL else u_src[1][m - KL]).then_inc(u_in[i % 2], 16)

            def load_d(b, n, k):
                i = b * NB + n * KD + k
                if i >= 2:
                    sp.wait_ge(S["d_lo_done"], i - 1)
                rows = args["down_w"][k * P:(k + 1) * P] if k < KH else w2_dram[(k - KH) * P:(k - KH + 1) * P]
                sp.dma_start(d_raw[:, i % 2], rows[:, n * BANK:(n + 1) * BANK]).then_inc(d_in[i % 2], 16)

            def load_x2r(t):
                if t >= 2:
                    sp.wait_ge(S["res_done"], t - 1)
                sp.dma_start(x2r[:, t % 2], x2_dram[t * P:(t + 1) * P, :]).then_inc(x2r_in[t % 2], 16)

            def store(t):
                sp.wait_ge(S["out_done"], t + 1)
                sp.dma_start(out_rows[t * P:(t + 1) * P, :], ffn[:, t % BT]).then_inc(out_st, 16)

            sp.dma_start(gate_raw[:], args["gate_w"].rearrange("(k p) e -> p k e", p=P)).then_inc(gate_in, 16)
            for k in range(XS):
                load_xk(0, k)
            load_u(0, 0)
            load_u(0, 1)
            for k in range(XS, KT):
                load_xk(0, k)
            sp.dma_start(gamma[:], args["ln_gamma"].partition_broadcast(P)).then_inc(const_in, 16)
            sp.dma_start(beta[:], args["ln_beta"].partition_broadcast(P)).then_inc(const_in, 16)
            for b in range(BATCH):
                for m in range(WT):
                    if m == WT - 2:
                        load_d(b, 0, 0)
                        load_d(b, 0, 1)
                    if b == 0 and m >= 2 or b > 0:
                        load_u(b, m)
                    if b > 0 and m >= KL and (m - KL) % 4 == 3:
                        t = (b - 1) * BT + (m - KL) // 4
                        store(t)
                        if t + 2 < b * BT:
                            load_x2r(t + 2)
                for n in range(NH):
                    for k in range(KD):
                        if n or k >= 2:
                            load_d(b, n, k)
                        if b + 1 < BATCH and n == NH - 1 and k >= KD - KT:
                            load_xk(b + 1, k - (KD - KT))
                load_x2r(b * BT)
                load_x2r(b * BT + 1)
            b = BATCH - 1
            for t in range(b * BT, (b + 1) * BT):
                store(t)
                if t + 2 < (b + 1) * BT:
                    load_x2r(t + 2)
            sp.wait_ge(out_st, 16 * TILES)

        @block.tensor
        def _(pe):
            def transpose_x2(b, k):
                i = b * KT + k
                pe.wait_ge(xk_in[i % XS], 16 * (i // XS + 1))
                if i >= 2:
                    pe.wait_ge(S["x2T_lo_done"], i - 1)
                if b and k < 2:
                    pe.wait_ge(S["rT_done"], b)
                    pe.wait_ge(S["r_done"], b * BT)
                for t in range(BT):
                    mm = pe.transpose(t_ps[:, i % 2, t * P:(t + 1) * P], xk[:, i % XS, t], ident[:])
                mm.then_inc(S["x2T_ready"], 1)

            def routing(b):
                pe.wait_ge(S["x2T_lo_done"], (b + 1) * KT)
                pe.wait_ge(S["gate_lo_done"], 1)
                for t in range(BT):
                    for k in range(KT):
                        st = [x[:, k, t * P:(t + 1) * P] for x in (x2T_hi, x2T_lo)]
                        for i, (s, v) in enumerate(split_products(st, [g[:, k] for g in (gate_hi, gate_lo)])):
                            mm = pe.matmul(t_ps[:, 0, t * EXPERTS:(t + 1) * EXPERTS], s, v, start=(k == 0 and i == 0), stop=(k == KT - 1 and i == 2))
                mm.then_inc(S["logits_ready"], 1)

            def spread_r(b):
                for t in range(BT):
                    pe.wait_ge(S["rdiag_done"], b * BT + t + 1)
                    mm = pe.matmul(t_ps[:, 1, t * P:(t + 1) * P], ones[:], r_diag[:, t], start=True, stop=True)
                mm.then_inc(S["rT_ready"], 1)

            def first_product(i, slot):
                pe.wait_ge(S["u_lo_done"], i + 1)
                for k in range(KT):
                    st = [u[:, slot, k] for u in (u_hi, u_lo)]
                    for j, (s, v) in enumerate(split_products(st, [x[:, k] for x in (x2T_hi, x2T_lo)])):
                        mm = pe.matmul(u_ps[:, slot], s, v, start=(k == 0 and j == 0), stop=(k == KT - 1 and j == 2))
                mm.then_inc(S["u_ready"], 1)

            def second_product(b, n, k):
                i = b * NB + n * KD + k
                pe.wait_ge(S["d_lo_done"], i + 1)
                for t in range(BT):
                    if k == 0 and b + n:
                        pe.wait_ge(S["acc_evac"], (b * NH + n - 1) * BT + t + 1)
                    st = [h[:, k, t * P:(t + 1) * P] for h in (h_hi, h_lo)]
                    for j, (s, v) in enumerate(split_products(st, [d[:, i % 2] for d in (d_hi, d_lo)])):
                        mm = pe.matmul(acc[:, t], s, v, start=(k == 0 and j == 0), stop=(k == KD - 1 and j == 2))
                    if k == KD - 1:
                        mm.then_inc(S["acc_ready"], 1)
                    elif t == BT - 1:
                        mm.then_inc(S["d_used"], 1)

            pe.wait_ge(S["ones_done"], 1)
            for k in range(KT):
                transpose_x2(0, k)
            for b in range(BATCH):
                routing(b)
                for m in range(KL):
                    if b or m >= 2:
                        if m >= 2:
                            pe.wait_ge(S["lat_scaled"], b * KL + m - 1)
                        else:
                            pe.wait_ge(S["act_done"], b * KH)
                    first_product(b * WT + m, m % 2)
                    if m == 0:
                        spread_r(b)
                pe.wait_ge(S["lat_scaled"], (b + 1) * KL)
                first_product(b * WT + KL, 0)
                first_product(b * WT + KL + 1, 1)
                with pe.Fori(1, KH // 2) as p:
                    for slot in range(2):
                        pe.wait_ge(S["act_done"], 2 * p + (b * KH + slot - 1))
                        first_product(2 * p + (b * WT + KL + slot), slot)
                pe.wait_ge(S["h_lo_done"], (b + 1) * KD)
                for n in range(NH):
                    for k in range(KD):
                        second_product(b, n, k)
                        if b + 1 < BATCH and n == NH - 1 and k >= KD - KT:
                            transpose_x2(b + 1, k - (KD - KT))

        def d_step(eng, b, n, k, which):
            i = b * NB + n * KD + k
            if which == "hi":
                eng.wait_ge(d_in[i % 2], 16 * (i // 2 + 1))
                if i >= 2:
                    j = i - 2
                    last = j // KD
                    if j % KD == KD - 1:
                        eng.wait_ge(S["acc_ready"], (last + 1) * BT)
                    else:
                        eng.wait_ge(S["d_used"], last * (KD - 1) + j % KD + 1)
                eng.activation(d_hi[:, i % 2], d_raw[:, i % 2], ACT.Copy).then_inc(S["d_hi_done"], 1)
            else:
                eng.wait_ge(S["d_hi_done"], i + 1)
                eng.tensor_tensor(d_lo[:, i % 2], d_raw[:, i % 2], d_hi[:, i % 2].bitcast(F32), ALU.subtract).then_inc(S["d_lo_done"], 1)

        @block.scalar
        def _(act):
            def x2T_hi_out(b, k):
                i = b * KT + k
                act.wait_ge(S["x2T_ready"], i + 1)
                if b and k == 0:
                    act.wait_ge(S["u_ready"], b * WT)
                act.activation(x2T_hi[:, k], t_ps[:, i % 2], ACT.Copy).then_inc(S["x2T_hi_done"], 1)

            def split_u(i, slot, in_count):
                act.wait_ge(u_in[slot], in_count)
                if isinstance(i, int) and i < 2:
                    pass
                else:
                    act.wait_ge(S["u_ready"], i - 1)
                act.activation(u_hi[:, slot], u_raw[:, slot], ACT.Copy).then_inc(S["u_hi_done"], 1)

            def hidden(m, slot, i, count):
                act.wait_ge(S["u_ready"], i + 1)
                if not (isinstance(count, int) and count < 2):
                    act.wait_ge(S["h_lo_done"], h_done(count - 2, i))
                act.activation(act_sb[:, slot], u_ps[:, slot], ACT.Relu).then_inc(S["act_done"], 1)
                act.wait_ge(S["act_done"], count + 1)
                act.activation(h_hi[:, m], act_sb[:, slot], ACT.Square).then_inc(S["h_hi_done"], 1)

            def h_done(count, i):
                return i - 1

            def latent_hi(b, m):
                i = b * KL + m
                act.wait_ge(S["lat_scaled"], i + 1)
                act.activation(h_hi[:, KH + m], act_sb[:, m % 2], ACT.Copy).then_inc(S["h_hi_done"], 1)

            act.wait_ge(gate_in, 16)
            act.activation(gate_hi[:], gate_raw[:], ACT.Copy).then_inc(S["gate_hi_done"], 1)
            for k in range(KT):
                x2T_hi_out(0, k)
            for b in range(BATCH):
                w0 = b * WT
                split_u(w0, 0, 16 * (w0 // 2 + 1))
                split_u(w0 + 1, 1, 16 * (w0 // 2 + 1))
                act.wait_ge(S["rT_ready"], b + 1)
                if b:
                    act.wait_ge(S["acc_ready"], b * NH * BT)
                act.activation(rT[:], t_ps[:, 1], ACT.Copy).then_inc(S["rT_done"], 1)
                for m in range(KL):
                    latent_hi(b, m)
                    split_u(w0 + m + 2, m % 2, 16 * ((w0 + m) // 2 + 2))
                with act.Fori(0, KH // 2 - 1) as p:
                    for slot in range(2):
                        i = 2 * p + (w0 + KL + slot)
                        hidden(2 * p + slot, slot, i, 2 * p + (b * KH + slot))
                        split_u(i + 2, slot, 16 * (p + (w0 + KL) // 2 + 2))
                for slot in range(2):
                    m = KH - 2 + slot
                    if slot == 0:
                        d_step(act, b, 0, 0, "hi")
                    hidden(m, slot, w0 + KL + m, b * KH + m)
                d_step(act, b, 0, 1, "hi")
                for n in range(NH):
                    for k in range(2, KD + 2):
                        if k < KD:
                            d_step(act, b, n, k, "hi")
                        elif n + 1 < NH:
                            d_step(act, b, n + 1, k - KD, "hi")
                        if b + 1 < BATCH and n == NH - 1 and KD - KT <= k < KD:
                            x2T_hi_out(b + 1, k - (KD - KT))
                    for t in range(BT):
                        act.wait_ge(S["acc_ready"], (b * NH + n) * BT + t + 1)
                        if b:
                            act.wait_ge(out_st, 16 * b * BT)
                        act.activation(ffn[:, t, n * BANK:(n + 1) * BANK], acc[:, t], ACT.Copy).then_inc(S["acc_evac"], 1)

        @block.vector
        def _(dve):
            def x2T_lo_out(b, k):
                i = b * KT + k
                dve.wait_ge(S["x2T_hi_done"], i + 1)
                dve.tensor_tensor(x2T_lo[:, k], t_ps[:, i % 2], x2T_hi[:, k].bitcast(F32), ALU.subtract).then_inc(S["x2T_lo_done"], 1)

            def split_u(i, slot):
                dve.wait_ge(S["u_hi_done"], i + 1)
                dve.tensor_tensor(u_lo[:, slot], u_raw[:, slot], u_hi[:, slot].bitcast(F32), ALU.subtract).then_inc(S["u_lo_done"], 1)

            def hidden(m, slot, count, done):
                dve.wait_ge(S["h_hi_done"], done + 1)
                dve.tensor_tensor(act_sb[:, slot], act_sb[:, slot], act_sb[:, slot], ALU.mult).then_inc(S["sq_done"], 1)
                dve.wait_ge(S["sq_done"], count + 1)
                dve.tensor_tensor(h_lo[:, m], act_sb[:, slot], h_hi[:, m].bitcast(F32), ALU.subtract).then_inc(S["h_lo_done"], 1)

            def route(b):
                dve.wait_ge(S["logits_ready"], b + 1)
                for t in range(BT):
                    ins = dve.max(top[:, t], t_ps[:, 0, t * EXPERTS:(t + 1) * EXPERTS])
                ins.then_inc(S["top_done"], 1)
                dve.wait_ge(S["top_done"], b + 1)
                for t in range(BT):
                    dve.tensor_tensor(r_tok[:, t:t + 1], top[:, t, 0:1], top[:, t, 1:2], ALU.add).then_inc(S["r_done"], 1)
                dve.wait_ge(S["r_done"], (b + 1) * BT)
                for t in range(BT):
                    dve.tensor_scalar(r_diag[:, t], ident[:], r_tok[:, t:t + 1], None, ALU.mult).then_inc(S["rdiag_done"], 1)

            def latent(b, m):
                dve.wait_ge(S["u_ready"], b * WT + m + 1)
                dve.wait_ge(S["rT_done"], b + 1)
                if b or m >= 2:
                    dve.wait_ge(S["h_lo_done"], b * KD + m - 1 if m >= 2 else b * KD)
                dve.tensor_tensor(act_sb[:, m % 2], u_ps[:, m % 2], rT[:], ALU.mult).then_inc(S["lat_scaled"], 1)
                dve.wait_ge(S["h_hi_done"], b * KD + m + 1)
                dve.tensor_tensor(h_lo[:, KH + m], act_sb[:, m % 2], h_hi[:, KH + m].bitcast(F32), ALU.subtract).then_inc(S["h_lo_done"], 1)

            def stats(t, slot, st_done, mv_done, i):
                for n in range(NH):
                    ins = dve.bn_stats(stat[:, slot, n], ffn[:, t, n * BANK:(n + 1) * BANK])
                ins.then_inc(st_done, 1)
                dve.wait_ge(st_done, i + 1)
                dve.bn_aggr(mv[:, slot], stat[:, slot].rearrange("p n s -> p (n s)")).then_inc(mv_done, 1)

            def finish(i):
                t = i % BT
                dve.wait_ge(S["acc_evac"], (i // BT * NH + NH - 1) * BT + t + 1)
                stats(t, 0, S["stA_done"], S["mvA_done"], i)
                dve.wait_ge(S["rsA_done"], i + 1)
                dve.tensor_scalar(ffn[:, t], ffn[:, t], mv[:, 0, 0:1], rstd[:, 0:1], ALU.subtract, ALU.mult).then_inc(S["nA_done"], 1)
                dve.wait_ge(S["nA_done"], i + 1)
                dve.tensor_tensor(ffn[:, t], ffn[:, t], gamma[:], ALU.mult).then_inc(S["gam_done"], 1)
                dve.wait_ge(S["gam_done"], i + 1)
                dve.tensor_tensor(ffn[:, t], ffn[:, t], beta[:], ALU.add).then_inc(S["bet_done"], 1)
                dve.wait_ge(S["bet_done"], i + 1)
                dve.wait_ge(x2r_in[i % 2], 16 * (i // 2 + 1))
                dve.tensor_tensor(ffn[:, t], ffn[:, t], x2r[:, i % 2], ALU.add).then_inc(S["res_done"], 1)
                dve.wait_ge(S["res_done"], i + 1)
                stats(t, 1, S["stB_done"], S["mvB_done"], i)
                dve.wait_ge(S["rsB_done"], i + 1)
                dve.tensor_scalar(ffn[:, t], ffn[:, t], mv[:, 1, 0:1], rstd[:, 1:2], ALU.subtract, ALU.mult).then_inc(S["out_done"], 1)

            dve.memset(ones[:], 1.0).then_inc(S["ones_done"], 1)
            dve.wait_ge(S["gate_hi_done"], 1)
            dve.tensor_tensor(gate_lo[:], gate_raw[:], gate_hi[:].bitcast(F32), ALU.subtract).then_inc(S["gate_lo_done"], 1)
            for k in range(KT):
                x2T_lo_out(0, k)
            dve.wait_ge(const_in, 32)
            for b in range(BATCH):
                w0 = b * WT
                split_u(w0, 0)
                split_u(w0 + 1, 1)
                route(b)
                for m in range(KL):
                    latent(b, m)
                    split_u(w0 + m + 2, m % 2)
                if b == 0:
                    with dve.Fori(0, KH // 2 - 1) as p:
                        for slot in range(2):
                            hidden(2 * p + slot, slot, 2 * p + (b * KH + slot), 2 * p + (b * KD + KL + slot))
                            split_u(2 * p + (w0 + KL + slot + 2), slot)
                else:
                    for m in range(KH - 2):
                        hidden(m, m % 2, b * KH + m, b * KD + KL + m)
                        split_u(w0 + KL + m + 2, m % 2)
                        if m % 4 == 1:
                            finish((b - 1) * BT + m // 4)
                for slot in range(2):
                    m = KH - 2 + slot
                    if slot == 0:
                        d_step(dve, b, 0, 0, "lo")
                    hidden(m, slot, b * KH + m, b * KD + KL + m)
                d_step(dve, b, 0, 1, "lo")
                for n in range(NH):
                    for k in range(2, KD + 2):
                        if k < KD:
                            d_step(dve, b, n, k, "lo")
                        elif n + 1 < NH:
                            d_step(dve, b, n + 1, k - KD, "lo")
                        if b + 1 < BATCH and n == NH - 1 and KD - KT <= k < KD:
                            x2T_lo_out(b + 1, k - (KD - KT))
            for t in range(BT):
                finish((BATCH - 1) * BT + t)

        @block.gpsimd
        def _(pool):
            for i in range(TILES):
                for slot, x in enumerate("AB"):
                    pool.wait_ge(S[f"mv{x}_done"], i + 1)
                    pool.tensor_scalar(veps[:, slot:slot + 1], mv[:, slot, 1:2], EPS, 1.0, ALU.add, ALU.mult).then_inc(S[f"ve{x}_done"], 1)
                    pool.wait_ge(S[f"ve{x}_done"], i + 1)
                    pool.tensor_tensor(rstd[:, slot:slot + 1], veps[:, slot:slot + 1], so["neg_half"][:], ALU.pow).then_inc(S[f"rs{x}_done"], 1)


def decoder(nc, args, out):
    qkv_dram = nc.dram_tensor("qkv_scratch", [3, TOKENS, GD], F32, kind="Internal").ap()
    o_dram = nc.dram_tensor("o_scratch", [TOKENS, GD], F32, kind="Internal").ap()
    x2_dram = nc.dram_tensor("x2_scratch", [TOKENS, EMB], F32, kind="Internal").ap()
    w2_dram = nc.dram_tensor("w2_scratch", [LAT, EMB], F32, kind="Internal").ap()
    with ExitStack() as ctx:
        sb = lambda name, shape, dt: ctx.enter_context(nc.sbuf_tensor(name, shape, dt))
        so = {
            "ident": sb("ident", [P, P], F32),
            "ident_bf": sb("ident_bf", [P, P], BF16),
            "ones_bf": sb("ones_bf", [P, P], BF16),
            "maskj": sb("maskj", [P, JQ], F32),
            "maskt": sb("maskt", [P, TQ], F32),
            "neg_half": sb("neg_half", [P, 1], F32),
            "unmagic": sb("unmagic", [P, 1], F32),
            "quant": sb("quant", [P, 10], F32),
        }
        with ExitStack() as inner:
            sbi = lambda name, shape, dt: inner.enter_context(nc.sbuf_tensor(name, shape, dt))
            so["w_hi"] = sbi("w_hi", [P, KT, QKV], F32R)
            so["w_lo"] = sbi("w_lo", [P, KT, QKV], F32R)
            so["bias"] = sbi("bias", [P, QKV], F32)
            prepare_weights(nc, so, args, w2_dram)
            attention_and_cross(nc, so, args, qkv_dram, o_dram, x2_dram)
        feed_forward(nc, so, args, x2_dram, w2_dram, out)


_INS = {"x": "x", "ctx_4096": "ctx", "L0_attn_Wq": "Wq", "L0_attn_bq": "bq", "L0_attn_Wk": "Wk", "L0_attn_bk": "bk",
        "L0_attn_Wv": "Wv", "L0_attn_bv": "bv", "L0_xattn_x1_scale": "x1_scale", "L0_xattn_x1_zp": "x1_zp",
        "L0_xattn_x2_scale": "x2_scale", "L0_xattn_x2_zp": "x2_zp", "L0_ffn_gate_w": "gate_w", "L0_ffn_up_w": "up_w",
        "L0_ffn_down_w": "down_w", "L0_ffn_fc1_w": "fc1_w", "L0_ffn_fc2_w": "fc2_w", "L0_ffn_expert_w": "expert_w",
        "L0_ffn_ln_gamma": "ln_gamma", "L0_ffn_ln_beta": "ln_beta"}


def kernel(**inputs):
    import numpy as _np
    import concourse.bacc as _bacc
    from concourse import mybir as _mybir
    from concourse.bass_utils import run_bass_kernel_spmd as _run

    nc = _bacc.Bacc("TRN2", target_bir_lowering=False, num_devices=1)
    arrays, args = {}, {}
    for name, short in _INS.items():
        a = _np.ascontiguousarray(inputs[name])
        arrays[f"in_{name}_dram"] = a
        args[short] = nc.dram_tensor(f"in_{name}_dram", a.shape, _mybir.dt.from_np(a.dtype), kind="ExternalInput").ap()
    out = nc.dram_tensor("out_0_dram", (BATCH, SEQ, EMB), _mybir.dt.float32, kind="ExternalOutput").ap()
    decoder(nc, args, out)
    r = _run(nc, [arrays], core_ids=[0])
    return r.results[0]["out_0_dram"]
```

```python
from contextlib import ExitStack

import concourse.bass as bass
from concourse import mybir

F32 = mybir.dt.float32
F32R = mybir.dt.float32r
BF16 = mybir.dt.bfloat16
ALU = mybir.AluOpType
ACT = mybir.ActivationFunctionType
AX = mybir.AxisListType

P = 128
BATCH, SEQ, EMB = 2, 512, 1024
TOKENS = BATCH * SEQ
TILES = TOKENS // P
HEADS, GROUPS = 32, 8
REP = HEADS // GROUPS
HD = EMB // HEADS
GD = GROUPS * HD
QKV = 3 * GD
KT = EMB // P
CTX = 1024
HID, LAT, EXPERTS = 2048, 512, 8
BANK = 512
NH = EMB // BANK
NG = P // 16
JQ = 4
TQ = 4
BT = SEQ // P
EPS = 1e-5
QMAX, QMID = 255.0, 128.0
MAGIC = 1.5 * 2.0 ** 23


def split_products(stationary, moving):
    (s_hi, s_lo), (m_hi, m_lo) = stationary, moving
    return ((s_hi, m_hi), (s_hi, m_lo), (s_lo, m_hi))


def attention_and_cross(nc, so, args, x2_dram, w2_dram):
    w_hi, w_lo, bias, ident = so["w_hi"], so["w_lo"], so["bias"], so["ident"]
    maskj, maskt, qp = so["maskj"], so["maskt"], so["quant"]
    CK = CTX // P
    XR = 3
    MT = LAT // P
    with ExitStack() as ctx:
        sb = lambda name, shape, dt: ctx.enter_context(nc.sbuf_tensor(name, shape, dt))
        ps = lambda name, shape, dt: ctx.enter_context(nc.psum_tensor(name, shape, dt))
        sem = lambda name: ctx.enter_context(nc.semaphore(name))
        x_sb = sb("x_sb", [P, 2, EMB], F32)
        xT_hi, xT_lo = sb("xT_hi", [P, 2, KT, P], F32R), sb("xT_lo", [P, 2, KT, P], F32R)
        qkv_sb = sb("qkv_sb", [P, 2, QKV], F32)
        pg = sb("pg", [P, 2, NG, 3, HD], F32)
        q_bd, k_bd = sb("q_bd", [P, 2, NG, JQ, HD], F32), sb("k_bd", [P, 2, NG, TQ, HD], F32)
        vT, v_bd = sb("vT", [P, 2, NG, HD], F32), sb("v_bd", [P, 2, NG, JQ, HD], F32)
        sm = sb("sm", [P, 2, NG * TQ, HD], F32)
        smT = sb("smT", [P, 2, NG, TQ * HD], F32)
        s_max, s_sum = sb("s_max", [P, 2, NG * TQ], F32), sb("s_sum", [P, 2, NG * TQ], F32)
        s_rec = sb("s_rec", [P, 2, NG * TQ], F32)
        o_sb = sb("o_sb", [P, 2, NG, HD], F32)
        o_tok = sb("o_tok", [P, 2, GD], F32)
        res = sb("res", [P, XR, EMB], F32)
        y_sb = sb("y_sb", [P, EMB], F32)
        q1 = sb("q1", [P, 2, EMB], BF16)
        q1T = sb("q1T", [P, 2, KT, P], BF16)
        q2 = sb("q2", [P, BATCH, CK, EMB], BF16)
        c_sb = sb("c_sb", [P, 2, EMB], F32)
        col = sb("col", [P, EMB], F32)
        xa_out = sb("xa_out", [P, EMB], F32)
        stat, mv = sb("stat", [P, 4, NH, 6], F32), sb("mv", [P, 4, 2], F32)
        veps, rstd = sb("veps", [P, 4], F32), sb("rstd", [P, 4], F32)
        rowsum, rowterm = sb("rowsum", [P, 4], F32), sb("rowterm", [P, 4], F32)
        tr_ps = ps("tr_ps", [P, KT, P], F32)
        qkv_ps = ps("qkv_ps", [P, 2 * BANK], F32)
        sc_ps = ps("sc_ps", [P, NG * TQ, HD], F32)
        xa_ps = ps("xa_ps", [P, EMB], F32)
        flat = lambda a: a.rearrange("p a n c -> p (a n c)")
        wq_slots = [res[:, i] for i in range(XR)] + [x[:, i].rearrange("p n j d -> p (n j d)") for x in (q_bd, k_bd, v_bd) for i in range(2)]
        wkv_slots = [x[:, i * 2 * GD:(i + 1) * 2 * GD] for x, slots in ((flat(smT[:]), 4), (pg[:].rearrange("p a n c d -> p (a n c d)"), 3), (flat(vT[:]), 1))
                     for i in range(slots)]
        wq_raw = lambda k: wq_slots[k]
        wkv_raw = lambda k: wkv_slots[k]
        wq_sum = lambda k: sm[:, 0].rearrange("p a e -> p (a e)")[:, (k % 4) * GD:(k % 4 + 1) * GD]
        bq_raw = sm[:, 1].rearrange("p a e -> p (a e)")
        bkv_raw = flat(o_sb[:])
        exT_hi, exT_lo = [x[:].rearrange("p a k c -> p (a k c)").rearrange("p (m l) -> p m l", m=MT) for x in (xT_hi, xT_lo)]
        fc2_hi, fc2_lo = [w[:].rearrange("p k c -> p (k c)")[:, 0:MT * EMB].rearrange("p (m n) -> p m n", m=MT) for w in (w_hi, w_lo)]
        fc2_raw = [x_sb[:, 0], x_sb[:, 1], c_sb[:, 0], c_sb[:, 1]]
        ex_raw = [x[:, 0].rearrange("p n j d -> p (n j d)")[:, h * LAT:(h + 1) * LAT] for x in (q_bd, k_bd) for h in range(2)]
        w2_sb = fc2_raw
        q1T_ps = xa_ps[:, 0:BANK].bitcast(BF16).rearrange("p (k c) -> p k c", k=KT)
        av_ps = sc_ps[:].rearrange("p (n t) d -> p n t d", n=NG)

        x_in = [sem("x_in0"), sem("x_in1")]
        c_in = [sem("c_in0"), sem("c_in1")]
        pg_in = [sem("pg_in0"), sem("pg_in1")]
        o_in = [sem("o_in0"), sem("o_in1")]
        res_in = [sem(f"res_in{i}") for i in range(XR)]
        x2_st = [sem(f"x2_st{i}") for i in range(XR)]
        names = """xT_ready xT_hi_done xT_lo_done qkv_ready qkv_evac q_bd_done k_bd_done vT_done v_bd_done
            scores_ready max_done sub_done exp_done sum_done rec_done norm_done smT_done av_ready o_part o_done
            pre_done st1_done mv1_done ve1_done rstd1_done x1_done relu_done magic_done q1_done q1T_ready q1T_done
            xa_ready xa_add rowterm_done x2pre_done st2_done mv2_done ve2_done rstd2_done x2_done
            c_relu c_magic c_done col_ready col_done xa_evac x1col_done
            wq_summed w_hi_done w_lo_done ident_zero ident_done consts_done masks_done bias_done quant_done quant2_done
            exT_ready exT_hi_done exT_lo_done fc2_hi_done fc2_lo_done w2_ready w2_evac""".split()
        S = {n: sem(n) for n in names}
        wraw_in = [sem(f"wraw_in{i}") for i in range(KT)]
        bias_in, quant_in = sem("bias_in"), sem("quant_in")
        ex_in, fc2_in, w2_stored = sem("ex_in"), [sem(f"fc2_in{i}") for i in range(MT)], sem("w2_stored")
        block = ctx.enter_context(nc.Block())
        steps = range(-1, TILES + 4)
        w2_behind = {TILES + 1: (0, 1, 2, 3), TILES + 2: (4, 5, 6, 7)}
        ctx_tiles = lambda s: (2 * s, 2 * s + 1)
        in_range = lambda t: 0 <= t < TILES

        x_tiles = args["x"].rearrange("b (t p) e -> (b t) p e", p=P)
        c_tiles = args["ctx"].rearrange("b (k p) e -> (b k) p e", p=P)
        rows16 = lambda n: slice(n * 16, (n + 1) * 16)
        part = lambda x, c0, c1: x.rearrange("p (g c d) -> p c g d", g=GROUPS, c=3)[:, c0:c1]

        @block.sync
        def _(sp):
            def load_x(t):
                if t >= 2:
                    sp.wait_ge(S["xT_ready"], t - 1)
                sp.dma_start(x_sb[:, t % 2], x_tiles[t]).then_inc(x_in[t % 2], 16)

            wq = args["Wq"].rearrange("(k p) d h -> k p (d h)", p=P)
            wk = args["Wk"].rearrange("(k p) d h -> k p (d h)", p=P)
            wv = args["Wv"].rearrange("(k p) d h -> k p (d h)", p=P)

            def load_w(k):
                sp.dma_start(wq_raw(k), wq[k]).then_inc(wraw_in[k], 16)
                sp.dma_start(wkv_raw(k)[:, 0:GD], wk[k]).then_inc(wraw_in[k], 16)
                sp.dma_start(wkv_raw(k)[:, GD:2 * GD], wv[k]).then_inc(wraw_in[k], 16)

            def store_w2(rows):
                for l in rows:
                    sp.wait_ge(S["w2_evac"], NH * (l + 1))
                    sp.dma_start(w2_dram[l * P:(l + 1) * P, :], w2_sb[l]).then_inc(w2_stored, 16)

            load_x(0)
            load_w(0)
            load_w(1)
            row = lambda a: a.rearrange("d h -> (d h)").partition_broadcast(P)
            sp.dma_start(bq_raw, row(args["bq"])).then_inc(bias_in, 16)
            sp.dma_start(bkv_raw[:, 0:GD], row(args["bk"])).then_inc(bias_in, 16)
            sp.dma_start(bkv_raw[:, GD:2 * GD], row(args["bv"])).then_inc(bias_in, 16)
            for i, name in enumerate(("x1_scale", "x1_zp", "x2_scale", "x2_zp")):
                sp.dma_start(qp[:, i:i + 1], args[name].partition_broadcast(P)).then_inc(quant_in, 16)
            for k in range(2, KT):
                load_w(k)
                if k == 4:
                    load_x(1)
            for s in range(TILES + 4):
                if in_range(s - 2):
                    t = s - 2
                    if t >= XR:
                        sp.wait_ge(x2_st[t % XR], 16 * (t // XR))
                    else:
                        sp.wait_ge(S["w_lo_done"], KT)
                    sp.dma_start(res[:, t % XR], x_tiles[t]).then_inc(res_in[t % XR], 16)
                if in_range(s + 2):
                    load_x(s + 2)
                if in_range(s - 2):
                    t = s - 2
                    sp.wait_ge(S["o_done"], t + 1)
                    if t >= 2:
                        sp.wait_ge(S["pre_done"], t - 1)
                    for n in range(NG):
                        sp.dma_start(o_tok[rows16(n), t % 2], o_sb[:, t % 2, n]).then_inc(o_in[t % 2], 16)
                if in_range(s):
                    sp.wait_ge(S["qkv_evac"], s + 1)
                    if s >= 2:
                        sp.wait_ge(S["q_bd_done"], s - 1)
                        sp.wait_ge(S["k_bd_done"], s - 1)
                        sp.wait_ge(S["vT_done"], s - 1)
                    for n in range(NG):
                        sp.dma_start(pg[:, s % 2, n], qkv_sb[rows16(n), s % 2]).then_inc(pg_in[s % 2], 16)
                if s == TILES - 1:
                    sp.wait_ge(S["scores_ready"], TILES - 1)
                    for l in range(MT):
                        sp.dma_start(ex_raw[l], args["expert_w"][l * P:(l + 1) * P, :]).then_inc(ex_in, 16)
                    sp.wait_ge(S["xT_ready"], TILES)
                    sp.wait_ge(S["c_done"], BATCH * CK)
                    for m in range(MT):
                        sp.dma_start(fc2_raw[m], args["fc2_w"][m * P:(m + 1) * P, :]).then_inc(fc2_in[m], 16)
                if s == TILES + 3:
                    store_w2(range(MT - 1))
                if in_range(s - 4):
                    t = s - 4
                    sp.wait_ge(S["x2_done"], t + 1)
                    sp.dma_start(x2_dram[t * P:(t + 1) * P, :], res[:, t % XR]).then_inc(x2_st[t % XR], 16)
            store_w2(range(MT - 1, MT))
            sp.wait_ge(w2_stored, 16 * MT)
            for i in range(XR):
                sp.wait_ge(x2_st[i], 16 * len(range(i, TILES, XR)))

        @block.tensor
        def _(pe):
            def transpose_x(t):
                pe.wait_ge(x_in[t % 2], 16 * (t // 2 + 1))
                if t >= 1:
                    pe.wait_ge(S["xT_lo_done"], t)
                for k in range(KT):
                    mm = pe.transpose(tr_ps[:, k], x_sb[:, t % 2, k * P:(k + 1) * P], ident[:])
                mm.then_inc(S["xT_ready"], 1)

            def project(t):
                pe.wait_ge(S["xT_lo_done"], t + 1)
                if t >= 1:
                    pe.wait_ge(S["qkv_evac"], t)
                for k in range(KT):
                    if t == 0:
                        pe.wait_ge(S["w_lo_done"], k + 1)
                    st = [x[:, t % 2, k] for x in (xT_hi, xT_lo)]
                    for i in range(3):
                        for c0, c1 in ((0, BANK), (BANK, QKV)):
                            s, v = split_products(st, [w[:, k, c0:c1] for w in (w_hi, w_lo)])[i]
                            mm = pe.matmul(qkv_ps[:, c0:c1], s, v, start=(k == 0 and i == 0), stop=(k == KT - 1 and i == 2))
                mm.then_inc(S["qkv_ready"], 1)

            def scores(t):
                pe.wait_ge(S["q_bd_done"], t + 1)
                pe.wait_ge(S["k_bd_done"], t + 1)
                if t >= 1:
                    pe.wait_ge(S["o_done"], t)
                for n in range(NG):
                    mm = pe.matmul(sc_ps[:, n * TQ:(n + 1) * TQ, :], q_bd[:, t % 2, n], k_bd[:, t % 2, n], start=True, stop=True)
                mm.then_inc(S["scores_ready"], 1)

            def values(t):
                pe.wait_ge(S["smT_done"], t + 1)
                pe.wait_ge(S["v_bd_done"], t + 1)
                pe.wait_ge(S["sub_done"], t + 1)
                for n in range(NG):
                    mm = pe.matmul(av_ps[:, n], v_bd[:, t % 2, n], smT[:, t % 2, n], start=True, stop=True)
                mm.then_inc(S["av_ready"], 1)

            def transpose_q1(t):
                pe.wait_ge(S["q1_done"], t + 1)
                if t >= 1:
                    pe.wait_ge(S["xa_evac"], t)
                for k in range(KT):
                    mm = pe.transpose(q1T_ps[:, k], q1[:, t % 2, k * P:(k + 1) * P], so["ident_bf"][:])
                mm.then_inc(S["q1T_ready"], 1)

            def cross(t):
                pe.wait_ge(S["q1T_done"], t + 1)
                b = t // BT
                pe.wait_ge(S["c_done"], (b + 1) * CK)
                if t % BT == 0:
                    for n in range(NH):
                        for k in range(CK):
                            mm = pe.matmul(xa_ps[:, n * BANK:(n + 1) * BANK], so["ones_bf"][:], q2[:, b, k, n * BANK:(n + 1) * BANK],
                                           start=(k == 0), stop=(k == CK - 1))
                    mm.then_inc(S["col_ready"], 1)
                    pe.wait_ge(S["col_done"], b + 1)
                for k in range(CK):
                    for n in range(NH):
                        mm = pe.matmul(xa_ps[:, n * BANK:(n + 1) * BANK], q1T[:, t % 2, k], q2[:, b, k, n * BANK:(n + 1) * BANK],
                                       start=(k == 0), stop=(k == CK - 1))
                mm.then_inc(S["xa_ready"], 1)

            def transpose_expert(m):
                pe.wait_ge(ex_in, 16 * MT)
                if m < 2:
                    pe.wait_ge(S["qkv_evac"], TILES)
                else:
                    pe.wait_ge(S["exT_lo_done"], m - 1)
                for l in range(MT):
                    mm = pe.transpose(qkv_ps[:, m % 2 * BANK + l * P:m % 2 * BANK + (l + 1) * P], ex_raw[l][:, m * P:(m + 1) * P], ident[:])
                mm.then_inc(S["exT_ready"], 1)

            def w2_product(q):
                l, n = q // NH, q % NH
                pe.wait_ge(S["exT_lo_done"], MT)
                pe.wait_ge(S["fc2_lo_done"], MT)
                if q >= 2:
                    pe.wait_ge(S["w2_evac"], q - 1)
                for m in range(MT):
                    st = [e[:, m, l * P:(l + 1) * P] for e in (exT_hi, exT_lo)]
                    mv = [f[:, m, n * BANK:(n + 1) * BANK] for f in (fc2_hi, fc2_lo)]
                    for i, (a, b) in enumerate(split_products(st, mv)):
                        mm = pe.matmul(qkv_ps[:, n * BANK:(n + 1) * BANK], a, b, start=(m == 0 and i == 0), stop=(m == MT - 1 and i == 2))
                mm.then_inc(S["w2_ready"], 1)

            pe.wait_ge(S["ident_done"], 1)
            pe.wait_ge(S["masks_done"], 3)
            pe.wait_ge(S["consts_done"], 1)
            for s in steps:
                if in_range(s):
                    project(s)
                if in_range(s + 1):
                    transpose_x(s + 1)
                if s == TILES:
                    for m in range(MT):
                        transpose_expert(m)
                if in_range(s - 2):
                    values(s - 2)
                if in_range(s - 1):
                    scores(s - 1)
                if in_range(s - 3):
                    transpose_q1(s - 3)
                    cross(s - 3)
                for q in w2_behind.get(s, ()):
                    w2_product(q)

        @block.scalar
        def _(act):
            def softmax_exp(t):
                act.wait_ge(S["sub_done"], t + 1)
                act.activation(sm[:, t % 2], sm[:, t % 2], ACT.Exp, scale=float(HD) ** -0.5).then_inc(S["exp_done"], 1)

            def query_diagonal(t):
                act.wait_ge(pg_in[t % 2], 16 * NG * (t // 2 + 1))
                if t >= 2:
                    act.wait_ge(S["scores_ready"], t - 1)
                for j in range(JQ):
                    ins = act.activation(q_bd[:, t % 2, :, j, :], pg[:, t % 2, :, 0], ACT.Copy, scale=maskj[:, j:j + 1])
                ins.then_inc(S["q_bd_done"], 1)

            def q1T_out(t):
                act.wait_ge(S["q1T_ready"], t + 1)
                if t >= 2:
                    act.wait_ge(S["xa_ready"], t - 1)
                act.activation(q1T[:, t % 2], q1T_ps, ACT.Copy).then_inc(S["q1T_done"], 1)

            def quantise_a(t):
                act.wait_ge(S["x1_done"], t + 1)
                if t >= 1:
                    act.wait_ge(S["q1_done"], t)
                act.activation(y_sb[:], res[:, t % XR], ACT.Relu, bias=qp[:, 1:2], scale=qp[:, 4:5]).then_inc(S["relu_done"], 1)

            def quantise_b(t):
                act.wait_ge(S["magic_done"], t + 1)
                if t >= 2:
                    act.wait_ge(S["q1T_ready"], t - 1)
                act.activation(q1[:, t % 2], y_sb[:], ACT.Identity, bias=so["unmagic"][:], accum_out=rowsum[:, t % 4:t % 4 + 1]).then_inc(S["q1_done"], 1)

            def xT_hi_out(t):
                act.wait_ge(S["xT_ready"], t + 1)
                if t >= 2:
                    act.wait_ge(S["qkv_ready"], t - 1)
                act.activation(xT_hi[:, t % 2], tr_ps[:], ACT.Copy).then_inc(S["xT_hi_done"], 1)

            def load_ctx(s):
                for c in ctx_tiles(s):
                    if c >= 2:
                        act.wait_ge(S["c_done"], c - 1)
                    act.dma_start(c_sb[:, c % 2], c_tiles[c]).then_inc(c_in[c % 2], 16)

            def ctx_a(c):
                act.wait_ge(c_in[c % 2], 16 * (c // 2 + 1))
                act.activation(c_sb[:, c % 2], c_sb[:, c % 2], ACT.Relu, bias=qp[:, 3:4], scale=qp[:, 5:6]).then_inc(S["c_relu"], 1)

            def ctx_b(c):
                act.wait_ge(S["c_magic"], c + 1)
                act.activation(q2[:, c // CK, c % CK], c_sb[:, c % 2], ACT.Identity, bias=so["unmagic"][:]).then_inc(S["c_done"], 1)

            def split_w(k):
                act.wait_ge(S["wq_summed"], k + 1)
                act.activation(part(w_hi[:, k], 0, 1), wq_sum(k).rearrange("p (c g d) -> p c g d", c=1, g=GROUPS), ACT.Copy)
                act.activation(part(w_hi[:, k], 1, 3),
                               wkv_raw(k).rearrange("p (c d g) -> p c g d", c=2, g=GROUPS),
                               ACT.Copy).then_inc(S["w_hi_done"], 1)

            def cross_out(t):
                act.wait_ge(S["xa_ready"], t + 1)
                act.wait_ge(S["rowterm_done"], t + 1)
                if t >= 1:
                    act.wait_ge(S["x2pre_done"], t)
                act.activation(xa_out[:], xa_ps[:], ACT.Identity, bias=rowterm[:, t % 4:t % 4 + 1], scale=qp[:, 6:7]).then_inc(S["xa_evac"], 1)

            def expert_hi(m):
                act.wait_ge(S["exT_ready"], m + 1)
                if m == 0:
                    act.wait_ge(S["qkv_ready"], TILES)
                act.activation(exT_hi[:, m], qkv_ps[:, m % 2 * BANK:(m % 2 + 1) * BANK], ACT.Copy).then_inc(S["exT_hi_done"], 1)

            def fc2_hi_out(m):
                act.wait_ge(fc2_in[m], 16)
                if m == 0:
                    act.wait_ge(S["qkv_ready"], TILES)
                act.activation(fc2_hi[:, m], fc2_raw[m], ACT.Copy).then_inc(S["fc2_hi_done"], 1)

            def w2_out(q):
                act.wait_ge(S["w2_ready"], q + 1)
                if q == 0:
                    act.wait_ge(S["fc2_lo_done"], MT)
                act.activation(w2_sb[q // NH][:, (q % NH) * BANK:(q % NH + 1) * BANK], qkv_ps[:, (q % NH) * BANK:(q % NH + 1) * BANK],
                               ACT.Copy).then_inc(S["w2_evac"], 1)

            act.wait_ge(S["masks_done"], 3)
            act.wait_ge(S["consts_done"], 1)
            for s in steps:
                if in_range(s - 4) and s < TILES + 1:
                    cross_out(s - 4)
                if in_range(s):
                    if s == 0:
                        act.wait_ge(S["quant2_done"], 1)
                    ctx_a(ctx_tiles(s)[0])
                    ctx_a(ctx_tiles(s)[1])
                    ctx_b(ctx_tiles(s)[0])
                if s == TILES:
                    for m in range(MT):
                        expert_hi(m)
                    query_diagonal(s - 1)
                if s == TILES + 2:
                    for q in range(3):
                        w2_out(q)
                if in_range(s - 3):
                    quantise_a(s - 3)
                if in_range(s - 1) and s < TILES:
                    query_diagonal(s - 1)
                if in_range(s - 3):
                    quantise_b(s - 3)
                if in_range(s + 1):
                    xT_hi_out(s + 1)
                if s == -1:
                    for k in range(KT):
                        split_w(k)
                if s == TILES + 2:
                    w2_out(3)
                if in_range(s - 3):
                    q1T_out(s - 3)
                if in_range(s):
                    ctx_b(ctx_tiles(s)[1])
                if in_range(s + 1):
                    load_ctx(s + 1)
                if in_range(s - 1):
                    softmax_exp(s - 1)
                if in_range(s - 3) and s >= TILES:
                    cross_out(s - 3)
                if s == TILES:
                    for m in range(MT):
                        fc2_hi_out(m)
            for q in range(4, NH * MT):
                w2_out(q)

        @block.vector
        def _(dve):
            def stats(t, first, st_done, mv_done):
                slot = t % 2 + (0 if first else 2)
                for n in range(NH):
                    ins = dve.bn_stats(stat[:, slot, n], res[:, t % XR, n * BANK:(n + 1) * BANK])
                ins.then_inc(st_done, 1)
                dve.wait_ge(st_done, t + 1)
                dve.bn_aggr(mv[:, slot], stat[:, slot].rearrange("p n s -> p (n s)")).then_inc(mv_done, 1)

            def normalise(t, first, rstd_done, done):
                slot = t % 2 + (0 if first else 2)
                dve.wait_ge(rstd_done, t + 1)
                dve.tensor_scalar(res[:, t % XR], res[:, t % XR], mv[:, slot, 0:1], rstd[:, slot:slot + 1],
                                  ALU.subtract, ALU.mult).then_inc(done, 1)

            def cross_residual(t):
                dve.wait_ge(S["xa_evac"], t + 1)
                dve.wait_ge(S["x1col_done"], t + 1)
                dve.tensor_tensor(res[:, t % XR], res[:, t % XR], xa_out[:], ALU.add).then_inc(S["x2pre_done"], 1)

            def last_stats(t):
                dve.wait_ge(S["x2pre_done"], t + 1)
                stats(t, False, S["st2_done"], S["mv2_done"])

            def softmax_max(t):
                dve.wait_ge(S["scores_ready"], t + 1)
                dve.tensor_reduce(s_max[:, t % 2], sc_ps[:], AX.X, ALU.max).then_inc(S["max_done"], 1)
                dve.wait_ge(S["max_done"], t + 1)
                if t >= 2:
                    dve.wait_ge(S["smT_done"], t - 1)
                dve.tensor_tensor(sm[:, t % 2], sc_ps[:], s_max[:, t % 2].unsqueeze(2).to_broadcast([P, NG * TQ, HD]),
                                  ALU.subtract).then_inc(S["sub_done"], 1)

            def values_transpose(t):
                dve.wait_ge(pg_in[t % 2], 16 * NG * (t // 2 + 1))
                if t >= 2:
                    dve.wait_ge(S["v_bd_done"], t - 1)
                dve.transpose(vT[:, t % 2], pg[:, t % 2, :, 2]).then_inc(S["vT_done"], 1)

            def collect(t):
                dve.wait_ge(S["av_ready"], t + 1)
                if t >= 2:
                    dve.wait_ge(o_in[t % 2], 16 * NG * (t // 2))
                dve.tensor_scalar(o_sb[:, t % 2], av_ps[:, :, 0, :], maskt[:, 0:1], None, ALU.mult).then_inc(S["o_part"], 1)
                for q in range(1, TQ):
                    dve.wait_ge(S["o_part"], (TQ - 1) * t + q)
                    ins = dve.scalar_tensor_tensor(out=o_sb[:, t % 2], in0=av_ps[:, :, q, :], scalar=maskt[:, q:q + 1],
                                                   in1=o_sb[:, t % 2], op0=ALU.mult, op1=ALU.add)
                    ins.then_inc(S["o_part"] if q < TQ - 1 else S["o_done"], 1)

            def first_stats(t):
                dve.wait_ge(S["pre_done"], t + 1)
                stats(t, True, S["st1_done"], S["mv1_done"])

            def prepare(k):
                dve.wait_ge(wraw_in[k], 48)
                if k >= 4:
                    dve.wait_ge(S["w_lo_done"], k - 3)
                dve.tensor_reduce(wq_sum(k).rearrange("p (g d) -> p g d", g=GROUPS),
                                  wq_raw(k).rearrange("p (d g r) -> p g d r", g=GROUPS, r=REP),
                                  AX.X, ALU.add).then_inc(S["wq_summed"], 1)

            def prepare_lo(k):
                dve.wait_ge(S["w_hi_done"], k + 1)
                dve.wait_ge(S["wq_summed"], k + 1)
                dve.tensor_tensor(part(w_lo[:, k], 0, 1), wq_sum(k).rearrange("p (c g d) -> p c g d", c=1, g=GROUPS),
                                  part(w_hi[:, k].bitcast(F32), 0, 1), ALU.subtract)
                dve.tensor_tensor(part(w_lo[:, k], 1, 3), wkv_raw(k).rearrange("p (c d g) -> p c g d", c=2, g=GROUPS),
                                  part(w_hi[:, k].bitcast(F32), 1, 3),
                                  ALU.subtract).then_inc(S["w_lo_done"], 1)

            def constants():
                dve.wait_ge(S["ident_done"], 1)
                dve.tensor_reduce(maskj[:], ident[:].rearrange("p (j r) -> p j r", j=JQ), AX.X, ALU.add).then_inc(S["masks_done"], 1)
                dve.tensor_reduce(maskt[:], ident[:].rearrange("p (j t g) -> p t j g", j=JQ, t=TQ), AX.XY, ALU.add).then_inc(S["masks_done"], 1)
                dve.tensor_copy(so["ident_bf"][:], ident[:]).then_inc(S["masks_done"], 1)

            def biases():
                dve.wait_ge(bias_in, 48)
                dve.tensor_reduce(part(bias[:], 0, 1)[:, 0],
                                  bq_raw.rearrange("p (d g r) -> p g d r", g=GROUPS, r=REP), AX.X, ALU.add)
                dve.tensor_copy(part(bias[:], 1, 3),
                                bkv_raw.rearrange("p (c d g) -> p c g d", c=2, g=GROUPS)).then_inc(S["bias_done"], 1)

            def quant_constants():
                dve.wait_ge(quant_in, 64)
                dve.reciprocal(qp[:, 4:5], qp[:, 0:1])
                dve.reciprocal(qp[:, 5:6], qp[:, 2:3])
                dve.tensor_tensor(qp[:, 6:7], qp[:, 0:1], qp[:, 2:3], ALU.mult)
                dve.tensor_scalar(qp[:, 7:8], qp[:, 1:2], -1.0, QMID, ALU.mult, ALU.add)
                dve.tensor_scalar(qp[:, 8:9], qp[:, 3:4], -1.0, QMID, ALU.mult, ALU.add).then_inc(S["quant_done"], 1)
                dve.wait_ge(S["quant_done"], 1)
                dve.tensor_scalar(qp[:, 9:10], qp[:, 8:9], float(CTX), None, ALU.mult)
                dve.tensor_tensor(qp[:, 10:11], qp[:, 8:9], qp[:, 6:7], ALU.mult)
                dve.tensor_tensor(qp[:, 11:12], qp[:, 7:8], qp[:, 6:7], ALU.mult).then_inc(S["quant2_done"], 1)

            def expert_lo(m):
                dve.wait_ge(S["exT_hi_done"], m + 1)
                dve.tensor_tensor(exT_lo[:, m], qkv_ps[:, m % 2 * BANK:(m % 2 + 1) * BANK], exT_hi[:, m].bitcast(F32), ALU.subtract).then_inc(S["exT_lo_done"], 1)

            def fc2_lo_out(m):
                dve.wait_ge(S["fc2_hi_done"], m + 1)
                dve.tensor_tensor(fc2_lo[:, m], fc2_raw[m], fc2_hi[:, m].bitcast(F32), ALU.subtract).then_inc(S["fc2_lo_done"], 1)

            def column_term(b):
                dve.wait_ge(S["col_ready"], b + 1)
                if b:
                    dve.wait_ge(S["x1col_done"], b * BT)
                dve.tensor_scalar(col[:], xa_ps[:], qp[:, 9:10], qp[:, 11:12], ALU.add, ALU.mult).then_inc(S["col_done"], 1)

            def softmax_sum(t):
                dve.wait_ge(S["exp_done"], t + 1)
                dve.tensor_reduce(s_sum[:, t % 2], sm[:, t % 2], AX.X, ALU.add).then_inc(S["sum_done"], 1)
                dve.wait_ge(S["sum_done"], t + 1)
                dve.reciprocal(s_rec[:, t % 2], s_sum[:, t % 2]).then_inc(S["rec_done"], 1)

            def magic(t):
                dve.wait_ge(S["relu_done"], t + 1)
                dve.tensor_scalar(y_sb[:], y_sb[:], QMAX, MAGIC, ALU.min, ALU.add).then_inc(S["magic_done"], 1)

            def ctx_magic(c):
                dve.wait_ge(S["c_relu"], c + 1)
                dve.tensor_scalar(c_sb[:, c % 2], c_sb[:, c % 2], QMAX, MAGIC, ALU.min, ALU.add).then_inc(S["c_magic"], 1)

            def qkv_out(t):
                dve.wait_ge(S["qkv_ready"], t + 1)
                if t >= 2:
                    dve.wait_ge(pg_in[t % 2], 16 * NG * (t // 2))
                dve.tensor_tensor(qkv_sb[:, t % 2], qkv_ps[:, 0:QKV], bias[:], ALU.add).then_inc(S["qkv_evac"], 1)

            def xT_lo_out(t):
                dve.wait_ge(S["xT_hi_done"], t + 1)
                dve.tensor_tensor(xT_lo[:, t % 2], tr_ps[:], xT_hi[:, t % 2].bitcast(F32), ALU.subtract).then_inc(S["xT_lo_done"], 1)

            def softmax_transpose(t):
                dve.wait_ge(S["norm_done"], t + 1)
                if t >= 2:
                    dve.wait_ge(S["av_ready"], t - 1)
                dve.transpose(smT[:, t % 2].rearrange("p n c -> p (n c)"), sm[:, t % 2].rearrange("p n c -> p (n c)")).then_inc(S["smT_done"], 1)

            constants()
            for s in steps:
                if in_range(s - 2):
                    softmax_sum(s - 2)
                if s == TILES:
                    for m in range(MT):
                        expert_lo(m)
                if in_range(s - 4):
                    cross_residual(s - 4)
                    last_stats(s - 4)
                if in_range(s - 2):
                    softmax_transpose(s - 2)
                if in_range(s - 3):
                    first_stats(s - 3)
                if in_range(s - 1):
                    values_transpose(s - 1)
                if in_range(s):
                    ctx_magic(ctx_tiles(s)[0])
                if in_range(s - 3):
                    normalise(s - 3, True, S["rstd1_done"], S["x1_done"])
                if in_range(s - 4):
                    normalise(s - 4, False, S["rstd2_done"], S["x2_done"])
                if in_range(s - 3):
                    magic(s - 3)
                if in_range(s - 2):
                    collect(s - 2)
                if in_range(s):
                    if s == 0:
                        dve.wait_ge(S["bias_done"], 1)
                    qkv_out(s)
                    ctx_magic(ctx_tiles(s)[1])
                if in_range(s + 1):
                    xT_lo_out(s + 1)
                if in_range(s - 1):
                    softmax_max(s - 1)
                if s == -1:
                    for k in range(KT + 1):
                        if k < KT:
                            prepare(k)
                        if k:
                            prepare_lo(k - 1)
                        if k == 2:
                            quant_constants()
                            biases()
                if in_range(s - 3) and (s - 3) % BT == 0:
                    column_term((s - 3) // BT)
                if s == TILES + 1:
                    for m in range(MT):
                        fc2_lo_out(m)

        @block.gpsimd
        def _(pool):
            def values_diagonal(t):
                pool.wait_ge(S["vT_done"], t + 1)
                if t >= 2:
                    pool.wait_ge(S["av_ready"], t - 1)
                for j in range(JQ):
                    ins = pool.tensor_scalar(v_bd[:, t % 2, :, j, :], vT[:, t % 2], maskj[:, j:j + 1], 1.0, ALU.mult, ALU.mult)
                ins.then_inc(S["v_bd_done"], 1)

            def inverse_deviation(t, first, mv_done, ve_done, rstd_done):
                slot = t % 2 + (0 if first else 2)
                pool.wait_ge(mv_done, t + 1)
                pool.tensor_scalar(veps[:, slot:slot + 1], mv[:, slot, 1:2], EPS, 1.0, ALU.add, ALU.mult).then_inc(ve_done, 1)
                pool.wait_ge(ve_done, t + 1)
                pool.tensor_tensor(rstd[:, slot:slot + 1], veps[:, slot:slot + 1], so["neg_half"][:], ALU.pow).then_inc(rstd_done, 1)

            def softmax_scale(t):
                pool.wait_ge(S["rec_done"], t + 1)
                pool.tensor_tensor(sm[:, t % 2], sm[:, t % 2], s_rec[:, t % 2].unsqueeze(2).to_broadcast([P, NG * TQ, HD]),
                                   ALU.mult).then_inc(S["norm_done"], 1)

            def row_term(t):
                pool.wait_ge(S["q1_done"], t + 1)
                pool.tensor_scalar(rowterm[:, t % 4:t % 4 + 1], rowsum[:, t % 4:t % 4 + 1], qp[:, 10:11], 1.0, ALU.mult, ALU.mult).then_inc(S["rowterm_done"], 1)

            def keys_diagonal(t):
                pool.wait_ge(pg_in[t % 2], 16 * NG * (t // 2 + 1))
                if t >= 2:
                    pool.wait_ge(S["scores_ready"], t - 1)
                for q in range(TQ):
                    ins = pool.tensor_scalar(k_bd[:, t % 2, :, q, :], pg[:, t % 2, :, 1], maskt[:, q:q + 1], 1.0, ALU.mult, ALU.mult)
                ins.then_inc(S["k_bd_done"], 1)

            def residual(t):
                pool.wait_ge(res_in[t % XR], 16 * (t // XR + 1))
                pool.wait_ge(o_in[t % 2], 16 * NG * (t // 2 + 1))
                x = res[:, t % XR].rearrange("p (d g r) -> p d g r", g=GROUPS, r=REP)
                o = o_tok[:, t % 2].rearrange("p (g d) -> p d g", g=GROUPS).unsqueeze(3).to_broadcast([P, HD, GROUPS, REP])
                pool.tensor_tensor(x, x, o, ALU.add).then_inc(S["pre_done"], 1)

            def add_column_term(t):
                if t % BT == 0:
                    pool.wait_ge(S["col_done"], t // BT + 1)
                pool.wait_ge(S["relu_done"], t + 1)
                pool.tensor_tensor(res[:, t % XR], res[:, t % XR], col[:], ALU.add).then_inc(S["x1col_done"], 1)

            pool.memset(ident[:], 0.0).then_inc(S["ident_zero"], 1)
            pool.wait_ge(S["ident_zero"], 1)
            pool.affine_select(out=ident[:], in_=ident[:], compare_op=ALU.not_equal, fill=1.0, base=0,
                               pattern=[[-1, P]], channel_multiplier=1).then_inc(S["ident_done"], 1)
            pool.memset(so["ones_bf"][:], 1.0)
            pool.memset(so["neg_half"][:], -0.5)
            pool.memset(so["unmagic"][:], -(MAGIC + QMID)).then_inc(S["consts_done"], 1)
            pool.wait_ge(S["consts_done"], 1)
            pool.wait_ge(S["masks_done"], 3)
            pool.wait_ge(S["quant2_done"], 1)
            for s in steps:
                if in_range(s - 2):
                    softmax_scale(s - 2)
                if in_range(s - 3):
                    residual(s - 3)
                if in_range(s - 1):
                    keys_diagonal(s - 1)
                if in_range(s - 4):
                    inverse_deviation(s - 4, False, S["mv2_done"], S["ve2_done"], S["rstd2_done"])
                if in_range(s - 3):
                    inverse_deviation(s - 3, True, S["mv1_done"], S["ve1_done"], S["rstd1_done"])
                if in_range(s - 1):
                    values_diagonal(s - 1)
                if in_range(s - 3):
                    row_term(s - 3)
                    add_column_term(s - 3)


KH = HID // P
KL = LAT // P
KD = KH + KL
WT = KH + KL


def feed_forward(nc, so, args, x2_dram, w2_dram, out):
    ident = so["ident"]
    with ExitStack() as ctx:
        sb = lambda name, shape, dt: ctx.enter_context(nc.sbuf_tensor(name, shape, dt))
        ps = lambda name, shape, dt: ctx.enter_context(nc.psum_tensor(name, shape, dt))
        sem = lambda name: ctx.enter_context(nc.semaphore(name))
        XS = 4
        DH = 4
        tail = lambda b, n: DH if (b, n) == (BATCH - 1, NH - 1) else DH // 2
        used_before = lambda j: sum(KD - tail(i // NH, i % NH) for i in range(j))
        XO = KD - DH - KT
        xk = sb("xk", [P, XS, BT, P], F32)
        x2T_hi, x2T_lo = sb("x2T_hi", [P, KT, SEQ], F32R), sb("x2T_lo", [P, KT, SEQ], F32R)
        h_hi, h_lo = sb("h_hi", [P, KD, SEQ], F32R), sb("h_lo", [P, KD, SEQ], F32R)
        u_raw = sb("u_raw", [P, 2, KT, P], F32)
        u_hi, u_lo = sb("u_hi", [P, 2, KT, P], F32R), sb("u_lo", [P, 2, KT, P], F32R)
        d_raw = sb("d_raw", [P, 2, BANK], F32)
        d_hi, d_lo = sb("d_hi", [P, DH, BANK], F32R), sb("d_lo", [P, DH, BANK], F32R)
        act_sb = sb("act_sb", [P, 2, SEQ], F32)
        rT = sb("rT", [P, SEQ], F32)
        lgT = rT[0:EXPERTS, :]
        gate_raw = sb("gate_raw", [P, KT, EXPERTS], F32)
        gate_hi, gate_lo = sb("gate_hi", [P, KT, EXPERTS], F32R), sb("gate_lo", [P, KT, EXPERTS], F32R)
        top = sb("top", [P, BT, 8], F32)
        r_tok, r_diag = sb("r_tok", [P, BT], F32), sb("r_diag", [P, BT, P], F32)
        ones = sb("ones", [P, P], F32)
        ffn = sb("ffn", [P, BT, EMB], F32)
        x2r_sb = sb("x2r_sb", [P, 2, EMB], F32)
        x2b = [x2r_sb[:, 0], x2r_sb[:, 1]] + [xk[:, 2 * i:2 * i + 2].rearrange("p s t c -> p (s t c)") for i in range(2)]
        gamma, beta = sb("gamma", [P, EMB], F32), sb("beta", [P, EMB], F32)
        stat, mv = sb("stat_f", [P, 2, BT, NH, 6], F32), sb("mv_f", [P, 2, BT, 2], F32)
        veps, rstd = sb("veps_f", [P, 2, BT], F32), sb("rstd_f", [P, 2, BT], F32)
        nbias = sb("nbias", [P, BT], F32)
        acc = ps("acc", [P, BT, BANK], F32)
        u_ps = ps("u_ps", [P, 2, BANK], F32)
        t_ps = ps("t_ps", [P, 2, BANK], F32)

        xk_in = [sem(f"xk_in{i}") for i in range(XS)]
        u_in, d_in = [sem("u_in0"), sem("u_in1")], [sem("d_in0"), sem("d_in1")]
        x2r_in = [sem(f"x2r_in{i}") for i in range(BT)]
        const_in, gate_in, out_st = sem("const_in"), sem("gate_in"), sem("out_st")
        names = """ones_done gate_hi_done gate_lo_done x2T_ready x2T_hi_done x2T_lo_done lgT_ready lgT_done logits_ready top_done
            r_done rdiag_done rT_ready rT_done u_hi_done u_lo_done u_ready lat_scaled act_done h_hi_done sq_done
            h_lo_done d_hi_done d_lo_done d_used acc_ready acc_evac stA_done mvA_done veA_done rsA_done
            x2b_done gam_done res_done stB_done mvB_done veB_done rsB_done out_done pow_done""".split()
        S = {n: sem("f_" + n) for n in names}
        block = ctx.enter_context(nc.Block())

        u_src = [args[w].rearrange("(k p) (m c) -> m p k c", p=P, c=P) for w in ("up_w", "fc1_w")]
        out_rows = out.rearrange("b s e -> (b s) e")
        NB = NH * KD

        @block.sync
        def _(sp):
            def load_xk(b, k):
                i = b * KT + k
                if i >= XS:
                    sp.wait_ge(S["x2T_ready"], i - XS + 1)
                src = x2_dram[b * SEQ:(b + 1) * SEQ, k * P:(k + 1) * P].rearrange("(t p) c -> p t c", p=P)
                sp.dma_start(xk[:, i % XS], src).then_inc(xk_in[i % XS], 16)

            def load_u(b, m):
                i = b * WT + m
                if i >= 2:
                    sp.wait_ge(S["u_lo_done"], i - 1)
                sp.dma_start(u_raw[:, i % 2], u_src[0][m] if m < KH else u_src[1][m - KH]).then_inc(u_in[i % 2], 16)

            def load_d(b, n, k):
                i = b * NB + n * KD + k
                if i >= 2:
                    sp.wait_ge(S["d_lo_done"], i - 1)
                rows = args["down_w"][k * P:(k + 1) * P] if k < KH else w2_dram[(k - KH) * P:(k - KH + 1) * P]
                sp.dma_start(d_raw[:, i % 2], rows[:, n * BANK:(n + 1) * BANK]).then_inc(d_in[i % 2], 16)

            sp.dma_start(gate_raw[:], args["gate_w"].rearrange("(k p) e -> p k e", p=P)).then_inc(gate_in, 16)
            for k in range(XS):
                load_xk(0, k)
            load_u(0, 0)
            load_u(0, 1)
            for k in range(XS, KT):
                load_xk(0, k)
            sp.dma_start(gamma[:], args["ln_gamma"].partition_broadcast(P)).then_inc(const_in, 16)
            sp.dma_start(beta[:], args["ln_beta"].partition_broadcast(P)).then_inc(const_in, 16)
            for b in range(BATCH):
                for m in range(2, WT):
                    load_u(b, m)
                for n in range(NH):
                    for k in range(KD):
                        load_d(b, n, k)
                        if b + 1 < BATCH and n == NH - 1:
                            if XO - XS <= k < XO:
                                load_xk(b + 1, k - (XO - XS))
                            if XO + 6 <= k < XO + 6 + KT - XS:
                                load_xk(b + 1, XS + k - (XO + 6))
                            if k >= KD - 2:
                                load_u(b + 1, k - (KD - 2))

        @block.tensor
        def _(pe):
            def transpose_x2(b, k):
                i = b * KT + k
                pe.wait_ge(xk_in[i % XS], 16 * (i // XS + 1))
                if i >= 2:
                    pe.wait_ge(S["x2T_lo_done"], i - 1)
                if b and k == 0:
                    pe.wait_ge(S["rT_done"], b)
                    pe.wait_ge(S["top_done"], b)
                for t in range(BT):
                    mm = pe.transpose(t_ps[:, i % 2, t * P:(t + 1) * P], xk[:, i % XS, t], ident[:])
                mm.then_inc(S["x2T_ready"], 1)

            def routing(b):
                pe.wait_ge(S["x2T_lo_done"], (b + 1) * KT)
                pe.wait_ge(S["gate_lo_done"], 1)
                for k in range(KT):
                    for i, (s, v) in enumerate(split_products([g[:, k] for g in (gate_hi, gate_lo)], [x[:, k] for x in (x2T_hi, x2T_lo)])):
                        mm = pe.matmul(t_ps[0:EXPERTS, 0], s, v, start=(k == 0 and i == 0), stop=(k == KT - 1 and i == 2))
                mm.then_inc(S["lgT_ready"], 1)

            def transpose_logits(b):
                pe.wait_ge(S["lgT_done"], b + 1)
                for t in range(BT):
                    mm = pe.transpose(t_ps[:, 0, t * EXPERTS:(t + 1) * EXPERTS], lgT[:, t * P:(t + 1) * P], ident[0:EXPERTS, 0:EXPERTS])
                mm.then_inc(S["logits_ready"], 1)

            def spread_r(b):
                for t in range(BT):
                    pe.wait_ge(S["rdiag_done"], b * BT + t + 1)
                    mm = pe.matmul(t_ps[:, 1, t * P:(t + 1) * P], ones[:], r_diag[:, t], start=True, stop=True)
                mm.then_inc(S["rT_ready"], 1)

            def first_product(i, slot):
                pe.wait_ge(S["u_lo_done"], i + 1)
                for k in range(KT):
                    st = [u[:, slot, k] for u in (u_hi, u_lo)]
                    for j, (s, v) in enumerate(split_products(st, [x[:, k] for x in (x2T_hi, x2T_lo)])):
                        mm = pe.matmul(u_ps[:, slot], s, v, start=(k == 0 and j == 0), stop=(k == KT - 1 and j == 2))
                mm.then_inc(S["u_ready"], 1)

            def second_product(b, n, k, t):
                i = b * NB + n * KD + k
                pe.wait_ge(S["d_lo_done"], i + 1)
                if k == 0 and b + n:
                    pe.wait_ge(S["acc_evac"], (b * NH + n - 1) * BT + t + 1)
                if n == 0:
                    pe.wait_ge(S["h_lo_done"], b * KD + k + 1)
                st = [h[:, k, t * P:(t + 1) * P] for h in (h_hi, h_lo)]
                for j, (s, v) in enumerate(split_products(st, [d[:, i % DH] for d in (d_hi, d_lo)])):
                    mm = pe.matmul(acc[:, t], s, v, start=(k == 0 and j == 0), stop=(k == KD - 1 and j == 2))
                if k == KD - 1:
                    mm.then_inc(S["acc_ready"], 1)
                elif t == BT - 1 and k < KD - tail(b, n):
                    mm.then_inc(S["d_used"], 1)

            pe.wait_ge(S["ones_done"], 1)
            for k in range(KT):
                transpose_x2(0, k)
            for b in range(BATCH):
                routing(b)
                for m in range(2):
                    if b:
                        pe.wait_ge(S["lat_scaled"], b * KL - 1 + m)
                    first_product(b * WT + m, m)
                    if m == 0:
                        transpose_logits(b)
                with pe.Fori(1, KH // 2) as p:
                    for slot in range(2):
                        pe.wait_ge(S["act_done"], 2 * p + (b * KH + slot - 1))
                        first_product(2 * p + (b * WT + slot), slot)
                spread_r(b)
                for m in range(KL):
                    if m < 2:
                        pe.wait_ge(S["act_done"], (b + 1) * KH - 1 + m)
                    else:
                        pe.wait_ge(S["lat_scaled"], b * KL + m - 1)
                    first_product(b * WT + KH + m, m % 2)
                for n in range(NH):
                    for k in range(KD - tail(b, n)):
                        for t in range(BT):
                            second_product(b, n, k, t)
                        if b + 1 < BATCH and n == NH - 1 and XO <= k < XO + KT:
                            transpose_x2(b + 1, k - XO)
                    for t in range(BT):
                        for k in range(KD - tail(b, n), KD):
                            second_product(b, n, k, t)

        def d_step(eng, b, n, k, which):
            i = b * NB + n * KD + k
            if which == "hi":
                eng.wait_ge(d_in[i % 2], 16 * (i // 2 + 1))
                if i >= DH:
                    j, kj = (i - DH) // KD, (i - DH) % KD
                    if kj >= KD - tail(j // NH, j % NH):
                        eng.wait_ge(S["acc_ready"], (j + 1) * BT)
                    else:
                        eng.wait_ge(S["d_used"], used_before(j) + kj + 1)
                eng.activation(d_hi[:, i % DH], d_raw[:, i % 2], ACT.Copy).then_inc(S["d_hi_done"], 1)
            else:
                eng.wait_ge(S["d_hi_done"], i + 1)
                eng.tensor_tensor(d_lo[:, i % DH], d_raw[:, i % 2], d_hi[:, i % DH].bitcast(F32), ALU.subtract).then_inc(S["d_lo_done"], 1)

        @block.scalar
        def _(act):
            def x2T_hi_out(b, k):
                i = b * KT + k
                act.wait_ge(S["x2T_ready"], i + 1)
                if b and k == 0:
                    act.wait_ge(S["u_ready"], b * WT)
                act.activation(x2T_hi[:, k], t_ps[:, i % 2], ACT.Copy).then_inc(S["x2T_hi_done"], 1)

            def split_u(i, slot, in_count):
                act.wait_ge(u_in[slot], in_count)
                if not (isinstance(i, int) and i < 2):
                    act.wait_ge(S["u_ready"], i - 1)
                act.activation(u_hi[:, slot], u_raw[:, slot], ACT.Copy).then_inc(S["u_hi_done"], 1)

            def hidden(m, slot, i, count):
                act.wait_ge(S["u_ready"], i + 1)
                if not (isinstance(i, int) and i < 2):
                    act.wait_ge(S["h_lo_done"], i - 1)
                act.activation(act_sb[:, slot], u_ps[:, slot], ACT.Relu).then_inc(S["act_done"], 1)
                act.wait_ge(S["act_done"], count + 1)
                act.activation(h_hi[:, m], act_sb[:, slot], ACT.Square).then_inc(S["h_hi_done"], 1)

            def latent_hi(b, m):
                act.wait_ge(S["lat_scaled"], b * KL + m + 1)
                act.activation(h_hi[:, KH + m], act_sb[:, m % 2], ACT.Copy).then_inc(S["h_hi_done"], 1)

            def logits_out(b):
                act.wait_ge(S["lgT_ready"], b + 1)
                if b:
                    act.wait_ge(S["lat_scaled"], b * KL)
                act.activation(lgT, t_ps[0:EXPERTS, 0], ACT.Copy).then_inc(S["lgT_done"], 1)

            def spread_out(b):
                act.wait_ge(S["rT_ready"], b + 1)
                act.wait_ge(S["logits_ready"], b + 1)
                act.activation(rT[:], t_ps[:, 1], ACT.Copy).then_inc(S["rT_done"], 1)

            def final_norm(i):
                act.wait_ge(S["rsB_done"], i + 1)
                act.activation(ffn[:, i % BT], ffn[:, i % BT], ACT.Identity, bias=nbias[:, i % BT:i % BT + 1],
                               scale=rstd[:, 1, i % BT:i % BT + 1]).then_inc(S["out_done"], 1)

            act.wait_ge(gate_in, 16)
            act.activation(gate_hi[:], gate_raw[:], ACT.Copy).then_inc(S["gate_hi_done"], 1)
            for k in range(KT):
                x2T_hi_out(0, k)
            for b in range(BATCH):
                w0 = b * WT
                if b == 0:
                    for slot in range(2):
                        split_u(slot, slot, 16)
                else:
                    act.wait_ge(S["acc_ready"], b * NH * BT)
                logits_out(b)
                for m in range(2):
                    hidden(m, m, w0 + m, b * KH + m)
                    split_u(w0 + m + 2, m, 16 * (w0 // 2 + 2))
                with act.Fori(1, KH // 2) as p:
                    for slot in range(2):
                        i = 2 * p + (w0 + slot)
                        hidden(2 * p + slot, slot, i, 2 * p + (b * KH + slot))
                        split_u(i + 2, slot, 16 * (p + w0 // 2 + 2))
                spread_out(b)
                for m in range(KL):
                    if m < 2:
                        latent_hi(b, m)
                        split_u(w0 + KH + m + 2, m, 16 * ((w0 + KH) // 2 + 2))
                    else:
                        d_step(act, b, 0, m - 2, "hi")
                        latent_hi(b, m)
                for n in range(NH):
                    last = b + 1 < BATCH and n == NH - 1
                    for k in range(2 if n == 0 else 0, KD):
                        d_step(act, b, n, k, "hi")
                        if last and k >= XO + DH:
                            x2T_hi_out(b + 1, k - (XO + DH))
                        if last and k >= KD - 2:
                            split_u(w0 + WT + k - (KD - 2), k - (KD - 2), 16 * ((w0 + WT) // 2 + 1))
                    for t in range(BT):
                        act.wait_ge(S["acc_ready"], (b * NH + n) * BT + t + 1)
                        if b and n == 0:
                            act.wait_ge(out_st, 16 * b * BT)
                        act.activation(ffn[:, t, n * BANK:(n + 1) * BANK], acc[:, t], ACT.Copy).then_inc(S["acc_evac"], 1)
                    if b == BATCH - 1 and n == NH - 1:
                        for t in range(BT):
                            final_norm(b * BT + t)

        @block.vector
        def _(dve):
            def x2T_lo_out(b, k):
                i = b * KT + k
                dve.wait_ge(S["x2T_hi_done"], i + 1)
                dve.tensor_tensor(x2T_lo[:, k], t_ps[:, i % 2], x2T_hi[:, k].bitcast(F32), ALU.subtract).then_inc(S["x2T_lo_done"], 1)

            def split_u(i, slot):
                dve.wait_ge(S["u_hi_done"], i + 1)
                dve.tensor_tensor(u_lo[:, slot], u_raw[:, slot], u_hi[:, slot].bitcast(F32), ALU.subtract).then_inc(S["u_lo_done"], 1)

            def hidden(m, slot, i, count):
                dve.wait_ge(S["h_hi_done"], i + 1)
                dve.tensor_tensor(act_sb[:, slot], act_sb[:, slot], act_sb[:, slot], ALU.mult).then_inc(S["sq_done"], 1)
                dve.wait_ge(S["sq_done"], count + 1)
                dve.tensor_tensor(h_lo[:, m], act_sb[:, slot], h_hi[:, m].bitcast(F32), ALU.subtract).then_inc(S["h_lo_done"], 1)

            def route(b):
                dve.wait_ge(S["logits_ready"], b + 1)
                for t in range(BT):
                    ins = dve.max(top[:, t], t_ps[:, 0, t * EXPERTS:(t + 1) * EXPERTS])
                ins.then_inc(S["top_done"], 1)
                dve.wait_ge(S["top_done"], b + 1)
                for t in range(BT):
                    dve.tensor_tensor(r_tok[:, t:t + 1], top[:, t, 0:1], top[:, t, 1:2], ALU.add).then_inc(S["r_done"], 1)
                dve.wait_ge(S["r_done"], (b + 1) * BT)
                for t in range(BT):
                    dve.tensor_scalar(r_diag[:, t], ident[:], r_tok[:, t:t + 1], None, ALU.mult).then_inc(S["rdiag_done"], 1)

            def latent(b, m):
                i = b * WT + KH + m
                dve.wait_ge(S["u_ready"], i + 1)
                dve.wait_ge(S["rT_done"], b + 1)
                dve.wait_ge(S["h_lo_done"], i - 1)
                dve.tensor_tensor(act_sb[:, m % 2], u_ps[:, m % 2], rT[:], ALU.mult).then_inc(S["lat_scaled"], 1)
                dve.wait_ge(S["h_hi_done"], i + 1)
                dve.tensor_tensor(h_lo[:, KH + m], act_sb[:, m % 2], h_hi[:, KH + m].bitcast(F32), ALU.subtract).then_inc(S["h_lo_done"], 1)

            def half_stats(i, n):
                dve.wait_ge(S["acc_evac"], (i // BT * NH + n) * BT + i % BT + 1)
                dve.bn_stats(stat[:, 0, i % BT, n], ffn[:, i % BT, n * BANK:(n + 1) * BANK]).then_inc(S["stA_done"], 1)

            def row_stats(i):
                dve.wait_ge(S["stA_done"], NH * (i // BT) * BT + BT + i % BT + 1)
                dve.bn_aggr(mv[:, 0, i % BT], stat[:, 0, i % BT].rearrange("p n s -> p (n s)")).then_inc(S["mvA_done"], 1)

            def scale_and_add(i):
                t = i % BT
                dve.wait_ge(S["mvA_done"], i + 1)
                dve.scalar_tensor_tensor(out=ffn[:, t], in0=ffn[:, t], scalar=mv[:, 0, t, 0:1], in1=gamma[:],
                                         op0=ALU.subtract, op1=ALU.mult).then_inc(S["gam_done"], 1)
                dve.wait_ge(S["gam_done"], i + 1)
                dve.wait_ge(S["rsA_done"], i + 1)
                dve.wait_ge(S["x2b_done"], i + 1)
                dve.scalar_tensor_tensor(out=ffn[:, t], in0=ffn[:, t], scalar=rstd[:, 0, t:t + 1], in1=x2b[t],
                                         op0=ALU.mult, op1=ALU.add).then_inc(S["res_done"], 1)

            def last_stats(i):
                t = i % BT
                dve.wait_ge(S["res_done"], i + 1)
                for n in range(NH):
                    ins = dve.bn_stats(stat[:, 1, t, n], ffn[:, t, n * BANK:(n + 1) * BANK])
                ins.then_inc(S["stB_done"], 1)
                dve.wait_ge(S["stB_done"], i + 1)
                dve.bn_aggr(mv[:, 1, t], stat[:, 1, t].rearrange("p n s -> p (n s)")).then_inc(S["mvB_done"], 1)

            def last_norm(i):
                t = i % BT
                dve.wait_ge(S["rsB_done"], i + 1)
                dve.tensor_scalar(ffn[:, t], ffn[:, t], mv[:, 1, t, 0:1], rstd[:, 1, t:t + 1], ALU.subtract, ALU.mult).then_inc(S["out_done"], 1)

            dve.memset(ones[:], 1.0).then_inc(S["ones_done"], 1)
            dve.wait_ge(S["gate_hi_done"], 1)
            dve.tensor_tensor(gate_lo[:], gate_raw[:], gate_hi[:].bitcast(F32), ALU.subtract).then_inc(S["gate_lo_done"], 1)
            for k in range(KT):
                x2T_lo_out(0, k)
            dve.wait_ge(const_in, 32)
            for b in range(BATCH):
                w0 = b * WT
                if b == 0:
                    split_u(0, 0)
                    split_u(1, 1)
                route(b)
                if b == 0:
                    with dve.Fori(0, KH // 2) as p:
                        for slot in range(2):
                            hidden(2 * p + slot, slot, 2 * p + slot, 2 * p + slot)
                            split_u(2 * p + (slot + 2), slot)
                else:
                    for m in range(KH):
                        hidden(m, m % 2, w0 + m, b * KH + m)
                        split_u(w0 + m + 2, m % 2)
                        i = (b - 1) * BT + m // 3
                        if m < 3 * BT:
                            if m % 3 == 0:
                                half_stats(i, 1)
                                row_stats(i)
                            elif m % 3 == 1:
                                scale_and_add(i)
                            else:
                                last_stats(i)
                        if m % 3 == 0 and 0 < m <= 3 * BT:
                            last_norm(i - 1)
                for m in range(KL):
                    if m < 2:
                        latent(b, m)
                        split_u(w0 + KH + m + 2, m)
                    else:
                        d_step(dve, b, 0, m - 2, "lo")
                        latent(b, m)
                for n in range(NH):
                    last = b + 1 < BATCH and n == NH - 1
                    for k in range(2 if n == 0 else 0, KD):
                        d_step(dve, b, n, k, "lo")
                        if last and k >= XO + DH:
                            x2T_lo_out(b + 1, k - (XO + DH))
                        if last and k >= KD - 2:
                            split_u(w0 + WT + k - (KD - 2), k - (KD - 2))
                        if n == NH - 1 and 6 <= k < 6 + BT:
                            half_stats(b * BT + k - 6, 0)
            for t in range(BT):
                i = (BATCH - 1) * BT + t
                half_stats(i, 1)
                row_stats(i)
                scale_and_add(i)
                last_stats(i)

        @block.gpsimd
        def _(pool):
            def load_x2(i):
                if i == 0:
                    pool.wait_ge(S["x2T_ready"], BATCH * KT)
                if i >= BT:
                    pool.wait_ge(S["res_done"], i - BT + 1)
                pool.dma_start(x2b[i % BT], x2_dram[i * P:(i + 1) * P, :]).then_inc(x2r_in[i % BT], 16)

            def add_beta(i):
                pool.wait_ge(x2r_in[i % BT], 16 * (i // BT + 1))
                pool.tensor_tensor(x2b[i % BT], x2b[i % BT], beta[:], ALU.add).then_inc(S["x2b_done"], 1)

            def inverse_deviation(i, which, x):
                t = i % BT
                pool.wait_ge(S[f"mv{x}_done"], i + 1)
                pool.tensor_scalar(veps[:, which, t:t + 1], mv[:, which, t, 1:2], EPS, 1.0, ALU.add, ALU.mult).then_inc(S[f"ve{x}_done"], 1)
                pool.wait_ge(S[f"ve{x}_done"], i + 1)
                ins = pool.tensor_tensor(rstd[:, which, t:t + 1], veps[:, which, t:t + 1], so["neg_half"][:], ALU.pow)
                if x == "B" and i >= TILES - BT:
                    ins.then_inc(S["pow_done"], 1)
                    pool.wait_ge(S["pow_done"], i - (TILES - BT) + 1)
                    ins = pool.tensor_scalar(nbias[:, t:t + 1], mv[:, 1, t, 0:1], rstd[:, 1, t:t + 1], -1.0, ALU.mult, ALU.mult)
                ins.then_inc(S[f"rs{x}_done"], 1)

            def store(i):
                pool.wait_ge(S["out_done"], i + 1)
                pool.dma_start(out_rows[i * P:(i + 1) * P, :], ffn[:, i % BT]).then_inc(out_st, 16)

            pool.wait_ge(const_in, 32)
            for b in range(BATCH):
                if b == 0:
                    for t in range(BT):
                        load_x2(t)
                    for t in range(BT):
                        add_beta(t)
                for t in range(BT):
                    i = b * BT + t
                    inverse_deviation(i, 0, "A")
                    inverse_deviation(i, 1, "B")
                    if b + 1 < BATCH:
                        store(i)
                        load_x2(i + BT)
                    elif t:
                        store(i - 1)
                if b + 1 < BATCH:
                    for t in range(BT):
                        add_beta((b + 1) * BT + t)
            store(TILES - 1)
            pool.wait_ge(out_st, 16 * TILES)


def decoder(nc, args, out):
    x2_dram = nc.dram_tensor("x2_scratch", [TOKENS, EMB], F32, kind="Internal").ap()
    w2_dram = nc.dram_tensor("w2_scratch", [LAT, EMB], F32, kind="Internal").ap()
    with ExitStack() as ctx:
        sb = lambda name, shape, dt: ctx.enter_context(nc.sbuf_tensor(name, shape, dt))
        so = {
            "ident": sb("ident", [P, P], F32),
            "ident_bf": sb("ident_bf", [P, P], BF16),
            "ones_bf": sb("ones_bf", [P, P], BF16),
            "maskj": sb("maskj", [P, JQ], F32),
            "maskt": sb("maskt", [P, TQ], F32),
            "neg_half": sb("neg_half", [P, 1], F32),
            "unmagic": sb("unmagic", [P, 1], F32),
            "quant": sb("quant", [P, 12], F32),
        }
        with ExitStack() as inner:
            sbi = lambda name, shape, dt: inner.enter_context(nc.sbuf_tensor(name, shape, dt))
            so["w_hi"] = sbi("w_hi", [P, KT, QKV], F32R)
            so["w_lo"] = sbi("w_lo", [P, KT, QKV], F32R)
            so["bias"] = sbi("bias", [P, QKV], F32)
            attention_and_cross(nc, so, args, x2_dram, w2_dram)
        feed_forward(nc, so, args, x2_dram, w2_dram, out)


_INS = {"x": "x", "ctx_4096": "ctx", "L0_attn_Wq": "Wq", "L0_attn_bq": "bq", "L0_attn_Wk": "Wk", "L0_attn_bk": "bk",
        "L0_attn_Wv": "Wv", "L0_attn_bv": "bv", "L0_xattn_x1_scale": "x1_scale", "L0_xattn_x1_zp": "x1_zp",
        "L0_xattn_x2_scale": "x2_scale", "L0_xattn_x2_zp": "x2_zp", "L0_ffn_gate_w": "gate_w", "L0_ffn_up_w": "up_w",
        "L0_ffn_down_w": "down_w", "L0_ffn_fc1_w": "fc1_w", "L0_ffn_fc2_w": "fc2_w", "L0_ffn_expert_w": "expert_w",
        "L0_ffn_ln_gamma": "ln_gamma", "L0_ffn_ln_beta": "ln_beta"}


def kernel(**inputs):
    import numpy as _np
    import concourse.bacc as _bacc
    from concourse import mybir as _mybir
    from concourse.bass_utils import run_bass_kernel_spmd as _run

    nc = _bacc.Bacc("TRN2", target_bir_lowering=False, num_devices=1)
    arrays, args = {}, {}
    for name, short in _INS.items():
        a = _np.ascontiguousarray(inputs[name])
        arrays[f"in_{name}_dram"] = a
        args[short] = nc.dram_tensor(f"in_{name}_dram", a.shape, _mybir.dt.from_np(a.dtype), kind="ExternalInput").ap()
    out = nc.dram_tensor("out_0_dram", (BATCH, SEQ, EMB), _mybir.dt.float32, kind="ExternalOutput").ap()
    decoder(nc, args, out)
    r = _run(nc, [arrays], core_ids=[0])
    return r.results[0]["out_0_dram"]
```

```python
from contextlib import ExitStack

import concourse.bass as bass
from concourse import mybir

F32 = mybir.dt.float32
F32R = mybir.dt.float32r
BF16 = mybir.dt.bfloat16
ALU = mybir.AluOpType
ACT = mybir.ActivationFunctionType
AX = mybir.AxisListType

P = 128
BATCH, SEQ, EMB = 2, 512, 1024
TOKENS = BATCH * SEQ
TILES = TOKENS // P
HEADS, GROUPS = 32, 8
REP = HEADS // GROUPS
HD = EMB // HEADS
GD = GROUPS * HD
QKV = 3 * GD
KT = EMB // P
CTX = 1024
HID, LAT, EXPERTS = 2048, 512, 8
BANK = 512
NH = EMB // BANK
NG = P // 16
JQ = 4
TQ = 4
BT = SEQ // P
EPS = 1e-5
QMAX, QMID = 255.0, 128.0
XS = 4
XR = 3
MT = LAT // P
MAGIC = 1.5 * 2.0 ** 23


def split_products(stationary, moving):
    (s_hi, s_lo), (m_hi, m_lo) = stationary, moving
    return ((s_hi, m_hi), (s_hi, m_lo), (s_lo, m_hi))


def attention_and_cross(nc, so, args, x2_dram, w2_dram):
    w_hi, w_lo, ident = so["w_hi"], so["w_lo"], so["ident"]
    maskj, maskt, qp = so["maskj"], so["maskt"], so["quant"]
    CK = CTX // P
    with ExitStack() as ctx:
        sb = lambda name, shape, dt: ctx.enter_context(nc.sbuf_tensor(name, shape, dt))
        ps = lambda name, shape, dt: ctx.enter_context(nc.psum_tensor(name, shape, dt))
        sem = lambda name: ctx.enter_context(nc.semaphore(name))
        x_sb = sb("x_sb", [P, 2, EMB], F32)
        xT_hi, xT_lo = sb("xT_hi", [P, 2, KT, P], F32R), sb("xT_lo", [P, 2, KT, P], F32R)
        qkv_sb = sb("qkv_sb", [P, 2, QKV], F32)
        pg = sb("pg", [P, 2, NG, 3, HD], F32)
        bias = sb("bias", [P, QKV], F32)
        q_bd, smT = so["q_bd"], so["smT"]
        k_bd = sb("k_bd", [P, 2, NG, TQ, HD], F32)
        vT, v_bd = sb("vT", [P, 2, NG, HD], F32), sb("v_bd", [P, 2, NG, JQ, HD], F32)
        sm = so["u_raw"][:].rearrange("p (a n e) -> p a n e", a=2, e=HD)
        s_max, s_sum = sb("s_max", [P, 2, NG * TQ], F32), sb("s_sum", [P, 2, NG * TQ], F32)
        s_rec = sb("s_rec", [P, 2, NG * TQ], F32)
        o_sb = sb("o_sb", [P, 2, NG, HD], F32)
        o_tok = sb("o_tok", [P, 2, GD], F32)
        res = sb("res", [P, XR, EMB], F32)
        y_sb = sb("y_sb", [P, EMB], F32)
        q1 = sb("q1", [P, 2, EMB], BF16)
        q1T = sb("q1T", [P, 2, KT, P], BF16)
        with nc.sbuf_tensor("q2", [P, BATCH, CK, EMB], BF16) as q2:
            pass
        fc2_hi = sb("fc2_hi", [P, MT, EMB], F32R)
        sb("q2_second", [P, CK, EMB], BF16)
        c_sb = sb("c_sb", [P, 2, EMB], F32)
        col = sb("col", [P, EMB], F32)
        xa_out = sb("xa_out", [P, EMB], F32)
        stat, mv = sb("stat", [P, 4, NH, 6], F32), sb("mv", [P, 4, 2], F32)
        veps, rstd = sb("veps", [P, 4], F32), sb("rstd", [P, 4], F32)
        rowsum, rowterm = sb("rowsum", [P, 4], F32), sb("rowterm", [P, 4], F32)
        tr_ps = ps("tr_ps", [P, KT, P], F32)
        qkv_ps = ps("qkv_ps", [P, 2 * BANK], F32)
        sc_ps = ps("sc_ps", [P, NG * TQ, HD], F32)
        xa_ps = ps("xa_ps", [P, EMB], F32)
        flat = lambda a: a.rearrange("p a n c -> p (a n c)")
        wq_slots = [res[:, i] for i in range(XR)] + [x[:, i].rearrange("p n j d -> p (n j d)") for x in (q_bd, k_bd, v_bd) for i in range(2)]
        wkv_slots = [x[:, i * 2 * GD:(i + 1) * 2 * GD] for x, slots in ((flat(smT[:]), 4), (pg[:].rearrange("p a n c d -> p (a n c d)"), 3), (flat(vT[:]), 1))
                     for i in range(slots)]
        wq_raw = lambda k: wq_slots[k]
        wkv_raw = lambda k: wkv_slots[k]
        wq_sum = lambda k: sm[:, 0].rearrange("p a e -> p (a e)")[:, (k % 4) * GD:(k % 4 + 1) * GD]
        bq_raw = sm[:, 1].rearrange("p a e -> p (a e)")
        bkv_raw = flat(o_sb[:])
        exT_hi, exT_lo = [x[:].rearrange("p a k c -> p (a k c)").rearrange("p (m l) -> p m l", m=MT) for x in (xT_hi, xT_lo)]
        fc2_lo = [so[x][:, i] for x in ("fc2_lo_a", "fc2_lo_b") for i in range(2)]
        fc2_raw = [x_sb[:, 0], x_sb[:, 1], c_sb[:, 0], c_sb[:, 1]]
        ex_raw = [x[:, 0].rearrange("p n j d -> p (n j d)")[:, h * LAT:(h + 1) * LAT] for x in (q_bd, k_bd) for h in range(2)]
        x2T_hi, x2T_lo = so["x2T_hi"], so["x2T_lo"]
        xk_slots = [qkv_sb[:].rearrange("p a c -> p (a c)")[:, i * BT * P:(i + 1) * BT * P] for i in range(3)] + [bias[:, 0:BT * P]]
        xk = [x.rearrange("p (t c) -> p t c", t=BT) for x in xk_slots]
        gate_raw = bias[:, BT * P:BT * P + KT * EXPERTS].rearrange("p (k e) -> p k e", k=KT)
        x2T_ps = [tr_ps[:, BT * i:BT * (i + 1)].rearrange("p t c -> p (t c)") for i in range(2)]
        u_raw = so["u_raw"][:].rearrange("p (i k c) -> p i k c", i=2, k=KT)
        w2_sb = fc2_raw
        q1T_ps = xa_ps[:, 0:BANK].bitcast(BF16).rearrange("p (k c) -> p k c", k=KT)
        av_ps = sc_ps[:].rearrange("p (n t) d -> p n t d", n=NG)

        x_in = [sem("x_in0"), sem("x_in1")]
        c_in = [sem("c_in0"), sem("c_in1")]
        pg_in = [sem("pg_in0"), sem("pg_in1")]
        o_in = [sem("o_in0"), sem("o_in1")]
        res_in = [sem(f"res_in{i}") for i in range(XR)]
        x2_st = so["x2_st"]
        xk_in, u_in, gate_in = [sem(f"xk_in{i}") for i in range(4)], so["u_in"], sem("gate_in")
        names = """xT_ready xT_hi_done xT_lo_done qkv_ready qkv_evac q_bd_done k_bd_done vT_done v_bd_done
            scores_ready max_done sub_done exp_done sum_done rec_done norm_done smT_done av_ready o_part o_done
            pre_done st1_done mv1_done ve1_done rstd1_done x1_done relu_done magic_done q1_done q1T_ready q1T_done
            xa_ready rowterm_done x2pre_done st2_done mv2_done ve2_done rstd2_done x2_done
            c_relu c_magic c_done col_ready col_done xa_evac x1col_done
            wq_summed w_hi_done wq_lo_done wkv_lo_done ident_zero ident_done consts_done masks_done bias_done quant_done quant2_done
            exT_ready exT_hi_done exT_lo_done fc2_hi_done fc2_lo_done w2_ready w2_evac""".split()
        S = {**so["sem"], **{n: sem(n) for n in names}}
        wraw_in = [sem(f"wraw_in{i}") for i in range(KT)]
        bias_in, quant_in = sem("bias_in"), sem("quant_in")
        ex_in, fc2_in, w2_stored = sem("ex_in"), [sem(f"fc2_in{i}") for i in range(MT)], so["w2_stored"]
        block = ctx.enter_context(nc.Block())
        steps = range(-1, TILES + 4)
        w2_ahead = {TILES + 1: (0, 1, 2, 3), TILES + 2: (4, 5)}
        w2_behind = {TILES + 2: (6, 7)}
        ctx_tiles = lambda s: (2 * s, 2 * s + 1)
        in_range = lambda t: 0 <= t < TILES

        x_tiles = args["x"].rearrange("b (t p) e -> (b t) p e", p=P)
        c_tiles = args["ctx"].rearrange("b (k p) e -> (b k) p e", p=P)
        rows16 = lambda n: slice(n * 16, (n + 1) * 16)
        part = lambda x, c0, c1: x.rearrange("p (g c d) -> p c g d", g=GROUPS, c=3)[:, c0:c1]

        @block.sync
        def _(sp):
            def load_x(t):
                if t >= 2:
                    sp.wait_ge(S["xT_ready"], t - 1)
                sp.dma_start(x_sb[:, t % 2], x_tiles[t]).then_inc(x_in[t % 2], 16)

            wq = args["Wq"].rearrange("(k p) d h -> k p (d h)", p=P)
            wk = args["Wk"].rearrange("(k p) d h -> k p (d h)", p=P)
            wv = args["Wv"].rearrange("(k p) d h -> k p (d h)", p=P)

            def load_w(k):
                sp.dma_start(wq_raw(k), wq[k]).then_inc(wraw_in[k], 16)
                sp.dma_start(wkv_raw(k)[:, 0:GD], wk[k]).then_inc(wraw_in[k], 16)
                sp.dma_start(wkv_raw(k)[:, GD:2 * GD], wv[k]).then_inc(wraw_in[k], 16)

            def store_w2(rows):
                for l in rows:
                    sp.wait_ge(S["w2_evac"], NH * (l + 1))
                    sp.dma_start(w2_dram[l * P:(l + 1) * P, :], w2_sb[l]).then_inc(w2_stored, 16)

            def load_xk(k):
                if k == 0:
                    for i in range(XR):
                        sp.wait_ge(x2_st[i], 16 * len(range(i, BT, XR)))
                    sp.wait_ge(S["qkv_evac"], TILES)
                    for i in range(2):
                        sp.wait_ge(pg_in[i], 16 * NG * TILES // 2)
                if k >= 4:
                    sp.wait_ge(S["x2T_ready"], k - 3)
                sp.dma_start(xk[k % 4], x2_dram[0:SEQ, k * P:(k + 1) * P].rearrange("(t p) c -> p t c", p=P)).then_inc(xk_in[k % 4], 16)

            load_x(0)
            for k in range(KT):
                load_w(k)
            load_x(1)
            row = lambda a: a.rearrange("d h -> (d h)").partition_broadcast(P)
            sp.dma_start(bq_raw, row(args["bq"])).then_inc(bias_in, 16)
            sp.dma_start(bkv_raw[:, 0:GD], row(args["bk"])).then_inc(bias_in, 16)
            sp.dma_start(bkv_raw[:, GD:2 * GD], row(args["bv"])).then_inc(bias_in, 16)
            for i, name in enumerate(("x1_scale", "x1_zp", "x2_scale", "x2_zp")):
                sp.dma_start(qp[:, i:i + 1], args[name].partition_broadcast(P)).then_inc(quant_in, 16)
            for s in range(TILES + 4):
                if in_range(s - 2):
                    t = s - 2
                    if t >= XR:
                        sp.wait_ge(x2_st[t % XR], 16 * (t // XR))
                    else:
                        sp.wait_ge(S["wq_lo_done"], KT)
                    sp.dma_start(res[:, t % XR], x_tiles[t]).then_inc(res_in[t % XR], 16)
                if in_range(s + 2):
                    load_x(s + 2)
                if s == TILES:
                    for k in range(4):
                        load_xk(k)
                    sp.dma_start(gate_raw, args["gate_w"].rearrange("(k p) e -> p k e", p=P)).then_inc(gate_in, 16)
                if s == TILES + 1:
                    for k in range(4, KT):
                        load_xk(k)
                if s == TILES + 2:
                    sp.wait_ge(S["smT_done"], TILES)
                    for i in range(2):
                        sp.dma_start(u_raw[:, i], args["up_w"][:, i * P:(i + 1) * P].rearrange("(k p) c -> p k c", p=P)).then_inc(u_in[i], 16)
                if in_range(s - 2):
                    t = s - 2
                    sp.wait_ge(S["o_done"], t + 1)
                    if t >= 2:
                        sp.wait_ge(S["pre_done"], t - 1)
                    for n in range(NG):
                        sp.dma_start(o_tok[rows16(n), t % 2], o_sb[:, t % 2, n]).then_inc(o_in[t % 2], 16)
                if in_range(s):
                    sp.wait_ge(S["qkv_evac"], s + 1)
                    if s >= 2:
                        sp.wait_ge(S["q_bd_done"], s - 1)
                        sp.wait_ge(S["k_bd_done"], s - 1)
                        sp.wait_ge(S["vT_done"], s - 1)
                    for n in range(NG):
                        sp.dma_start(pg[:, s % 2, n], qkv_sb[rows16(n), s % 2]).then_inc(pg_in[s % 2], 16)
                if s == TILES - 1:
                    sp.wait_ge(S["scores_ready"], TILES - 1)
                    for l in range(MT):
                        sp.dma_start(ex_raw[l], args["expert_w"][l * P:(l + 1) * P, :]).then_inc(ex_in, 16)
                    sp.wait_ge(S["xT_ready"], TILES)
                    sp.wait_ge(S["c_done"], BATCH * CK)
                    for m in range(MT):
                        sp.dma_start(fc2_raw[m], args["fc2_w"][m * P:(m + 1) * P, :]).then_inc(fc2_in[m], 16)
                if s == TILES + 3:
                    store_w2(range(MT - 1))
                if in_range(s - 4):
                    t = s - 4
                    sp.wait_ge(S["x2_done"], t + 1)
                    sp.dma_start(x2_dram[t * P:(t + 1) * P, :], res[:, t % XR]).then_inc(x2_st[t % XR], 16)
            store_w2(range(MT - 1, MT))

        @block.tensor
        def _(pe):
            def transpose_x(t):
                pe.wait_ge(x_in[t % 2], 16 * (t // 2 + 1))
                if t >= 1:
                    pe.wait_ge(S["xT_lo_done"], t)
                for k in range(KT):
                    mm = pe.transpose(tr_ps[:, k], x_sb[:, t % 2, k * P:(k + 1) * P], ident[:])
                mm.then_inc(S["xT_ready"], 1)

            def project(t):
                pe.wait_ge(S["xT_lo_done"], t + 1)
                if t >= 1:
                    pe.wait_ge(S["qkv_evac"], t)
                for k in range(KT):
                    if t == 0:
                        pe.wait_ge(S["wq_lo_done"], k + 1)
                        pe.wait_ge(S["wkv_lo_done"], k + 1)
                    st = [x[:, t % 2, k] for x in (xT_hi, xT_lo)]
                    for i in range(3):
                        for c0, c1 in ((0, BANK), (BANK, QKV)):
                            s, v = split_products(st, [w[:, k, c0:c1] for w in (w_hi, w_lo)])[i]
                            mm = pe.matmul(qkv_ps[:, c0:c1], s, v, start=(k == 0 and i == 0), stop=(k == KT - 1 and i == 2))
                mm.then_inc(S["qkv_ready"], 1)

            def scores(t):
                pe.wait_ge(S["q_bd_done"], t + 1)
                pe.wait_ge(S["k_bd_done"], t + 1)
                if t >= 1:
                    pe.wait_ge(S["o_done"], t)
                for n in range(NG):
                    mm = pe.matmul(sc_ps[:, n * TQ:(n + 1) * TQ, :], q_bd[:, t % 2, n], k_bd[:, t % 2, n], start=True, stop=True)
                mm.then_inc(S["scores_ready"], 1)

            def values(t):
                pe.wait_ge(S["smT_done"], t + 1)
                pe.wait_ge(S["v_bd_done"], t + 1)
                pe.wait_ge(S["sub_done"], t + 1)
                for n in range(NG):
                    mm = pe.matmul(av_ps[:, n], v_bd[:, t % 2, n], smT[:, t % 2, n], start=True, stop=True)
                mm.then_inc(S["av_ready"], 1)

            def transpose_q1(t):
                pe.wait_ge(S["q1_done"], t + 1)
                if t >= 1:
                    pe.wait_ge(S["xa_evac"], t)
                for k in range(KT):
                    mm = pe.transpose(q1T_ps[:, k], q1[:, t % 2, k * P:(k + 1) * P], so["ident_bf"][:])
                mm.then_inc(S["q1T_ready"], 1)

            def cross(t):
                pe.wait_ge(S["q1T_done"], t + 1)
                b = t // BT
                pe.wait_ge(S["c_done"], (b + 1) * CK)
                if t % BT == 0:
                    for n in range(NH):
                        for k in range(CK):
                            mm = pe.matmul(xa_ps[:, n * BANK:(n + 1) * BANK], so["ones_bf"][:], q2[:, b, k, n * BANK:(n + 1) * BANK],
                                           start=(k == 0), stop=(k == CK - 1))
                    mm.then_inc(S["col_ready"], 1)
                    pe.wait_ge(S["col_done"], b + 1)
                for k in range(CK):
                    for n in range(NH):
                        mm = pe.matmul(xa_ps[:, n * BANK:(n + 1) * BANK], q1T[:, t % 2, k], q2[:, b, k, n * BANK:(n + 1) * BANK],
                                       start=(k == 0), stop=(k == CK - 1))
                mm.then_inc(S["xa_ready"], 1)

            def transpose_x2(k):
                pe.wait_ge(xk_in[k % 4], 16 * (k // 4 + 1))
                if k >= 2:
                    pe.wait_ge(S["x2T_lo_done"], k - 1)
                for t in range(BT):
                    mm = pe.transpose(tr_ps[:, k % 2 * BT + t], xk[k % 4][:, t], ident[:])
                mm.then_inc(S["x2T_ready"], 1)

            def transpose_expert(m):
                pe.wait_ge(ex_in, 16 * MT)
                if m < 2:
                    pe.wait_ge(S["qkv_evac"], TILES)
                else:
                    pe.wait_ge(S["exT_lo_done"], m - 1)
                for l in range(MT):
                    mm = pe.transpose(qkv_ps[:, m % 2 * BANK + l * P:m % 2 * BANK + (l + 1) * P], ex_raw[l][:, m * P:(m + 1) * P], ident[:])
                mm.then_inc(S["exT_ready"], 1)

            def w2_product(q):
                l, n = q // NH, q % NH
                pe.wait_ge(S["exT_lo_done"], MT)
                pe.wait_ge(S["fc2_lo_done"], MT)
                if q >= 2:
                    pe.wait_ge(S["w2_evac"], q - 1)
                for m in range(MT):
                    st = [e[:, m, l * P:(l + 1) * P] for e in (exT_hi, exT_lo)]
                    mv = [f[:, n * BANK:(n + 1) * BANK] for f in (fc2_hi[:, m], fc2_lo[m])]
                    for i, (a, b) in enumerate(split_products(st, mv)):
                        mm = pe.matmul(qkv_ps[:, n * BANK:(n + 1) * BANK], a, b, start=(m == 0 and i == 0), stop=(m == MT - 1 and i == 2))
                mm.then_inc(S["w2_ready"], 1)

            pe.wait_ge(S["ident_done"], 1)
            pe.wait_ge(S["masks_done"], 3)
            pe.wait_ge(S["consts_done"], 1)
            for s in steps:
                if in_range(s):
                    project(s)
                if s == TILES:
                    transpose_expert(0)
                    transpose_expert(1)
                if s == TILES + 1:
                    transpose_x2(4)
                    transpose_x2(5)
                if in_range(s - 2):
                    values(s - 2)
                if s == TILES:
                    transpose_expert(2)
                    transpose_expert(3)
                    transpose_x2(0)
                    transpose_x2(1)
                if s == TILES + 1:
                    transpose_x2(6)
                    transpose_x2(7)
                if in_range(s + 1):
                    transpose_x(s + 1)
                for q in w2_ahead.get(s, ()):
                    w2_product(q)
                if in_range(s - 3) and s < TILES:
                    transpose_q1(s - 3)
                if in_range(s - 1):
                    scores(s - 1)
                if s == TILES:
                    transpose_x2(2)
                    transpose_x2(3)
                if in_range(s - 3):
                    if s >= TILES:
                        transpose_q1(s - 3)
                    cross(s - 3)
                for q in w2_behind.get(s, ()):
                    w2_product(q)

        @block.scalar
        def _(act):
            def softmax_exp(t):
                act.wait_ge(S["sub_done"], t + 1)
                act.activation(sm[:, t % 2], sm[:, t % 2], ACT.Exp, scale=float(HD) ** -0.5).then_inc(S["exp_done"], 1)

            def query_diagonal(t):
                act.wait_ge(pg_in[t % 2], 16 * NG * (t // 2 + 1))
                if t >= 2:
                    act.wait_ge(S["scores_ready"], t - 1)
                for j in range(JQ):
                    ins = act.activation(q_bd[:, t % 2, :, j, :], pg[:, t % 2, :, 0], ACT.Copy, scale=maskj[:, j:j + 1])
                ins.then_inc(S["q_bd_done"], 1)

            def q1T_out(t):
                act.wait_ge(S["q1T_ready"], t + 1)
                if t >= 2:
                    act.wait_ge(S["xa_ready"], t - 1)
                act.activation(q1T[:, t % 2], q1T_ps, ACT.Copy).then_inc(S["q1T_done"], 1)

            def quantise_a(t):
                act.wait_ge(S["x1_done"], t + 1)
                if t >= 1:
                    act.wait_ge(S["q1_done"], t)
                act.activation(y_sb[:], res[:, t % XR], ACT.Relu, bias=qp[:, 1:2], scale=qp[:, 4:5]).then_inc(S["relu_done"], 1)

            def quantise_b(t):
                act.wait_ge(S["magic_done"], t + 1)
                if t >= 2:
                    act.wait_ge(S["q1T_ready"], t - 1)
                act.activation(q1[:, t % 2], y_sb[:], ACT.Identity, bias=so["unmagic"][:], accum_out=rowsum[:, t % 4:t % 4 + 1]).then_inc(S["q1_done"], 1)

            def xT_hi_out(t):
                act.wait_ge(S["xT_ready"], t + 1)
                if t >= 2:
                    act.wait_ge(S["qkv_ready"], t - 1)
                act.activation(xT_hi[:, t % 2], tr_ps[:], ACT.Copy).then_inc(S["xT_hi_done"], 1)

            def load_ctx(s):
                for c in ctx_tiles(s):
                    if c >= 2:
                        act.wait_ge(S["c_done"], c - 1)
                    act.dma_start(c_sb[:, c % 2], c_tiles[c]).then_inc(c_in[c % 2], 16)

            def ctx_a(c):
                act.wait_ge(c_in[c % 2], 16 * (c // 2 + 1))
                act.activation(c_sb[:, c % 2], c_sb[:, c % 2], ACT.Relu, bias=qp[:, 3:4], scale=qp[:, 5:6]).then_inc(S["c_relu"], 1)

            def ctx_b(c):
                act.wait_ge(S["c_magic"], c + 1)
                act.activation(q2[:, c // CK, c % CK], c_sb[:, c % 2], ACT.Identity, bias=so["unmagic"][:]).then_inc(S["c_done"], 1)

            def split_w(k):
                act.wait_ge(S["wq_summed"], k + 1)
                act.activation(part(w_hi[:, k], 0, 1), wq_sum(k).rearrange("p (c g d) -> p c g d", c=1, g=GROUPS), ACT.Copy)
                act.activation(part(w_hi[:, k], 1, 3),
                               wkv_raw(k).rearrange("p (c d g) -> p c g d", c=2, g=GROUPS),
                               ACT.Copy).then_inc(S["w_hi_done"], 1)

            def cross_out(t):
                act.wait_ge(S["xa_ready"], t + 1)
                act.wait_ge(S["rowterm_done"], t + 1)
                if t >= 1:
                    act.wait_ge(S["x2pre_done"], t)
                act.activation(xa_out[:], xa_ps[:], ACT.Identity, bias=rowterm[:, t % 4:t % 4 + 1], scale=qp[:, 6:7]).then_inc(S["xa_evac"], 1)

            def x2T_hi_out(k):
                act.wait_ge(S["x2T_ready"], k + 1)
                if k == 0:
                    act.wait_ge(S["qkv_ready"], TILES)
                act.activation(x2T_hi[:, k], x2T_ps[k % 2], ACT.Copy).then_inc(S["x2T_hi_done"], 1)

            def split_u(i):
                act.wait_ge(u_in[i], 16)
                act.wait_ge(S["av_ready"], TILES)
                act.activation(so["u_hi"][:, i], u_raw[:, i], ACT.Copy).then_inc(S["u_hi_done"], 1)

            def expert_hi(m):
                act.wait_ge(S["exT_ready"], m + 1)
                if m == 0:
                    act.wait_ge(S["qkv_ready"], TILES)
                act.activation(exT_hi[:, m], qkv_ps[:, m % 2 * BANK:(m % 2 + 1) * BANK], ACT.Copy).then_inc(S["exT_hi_done"], 1)

            def fc2_hi_out(m):
                act.wait_ge(fc2_in[m], 16)
                if m == 0:
                    act.wait_ge(S["xa_ready"], BT)
                act.activation(fc2_hi[:, m], fc2_raw[m], ACT.Copy).then_inc(S["fc2_hi_done"], 1)

            def w2_out(q):
                act.wait_ge(S["w2_ready"], q + 1)
                if q == 0:
                    act.wait_ge(S["fc2_lo_done"], MT)
                act.activation(w2_sb[q // NH][:, (q % NH) * BANK:(q % NH + 1) * BANK], qkv_ps[:, (q % NH) * BANK:(q % NH + 1) * BANK],
                               ACT.Copy).then_inc(S["w2_evac"], 1)

            act.wait_ge(S["masks_done"], 3)
            act.wait_ge(S["consts_done"], 1)
            for s in steps:
                if in_range(s - 4) and s < TILES + 1:
                    cross_out(s - 4)
                if s == 0:
                    xT_hi_out(1)
                    act.wait_ge(S["quant2_done"], 1)
                if in_range(s):
                    ctx_a(ctx_tiles(s)[0])
                    ctx_a(ctx_tiles(s)[1])
                if s == TILES:
                    query_diagonal(s - 1)
                    expert_hi(0)
                    expert_hi(1)
                if s == TILES + 1:
                    x2T_hi_out(6)
                    x2T_hi_out(7)
                    w2_out(0)
                    w2_out(1)
                if in_range(s - 3):
                    quantise_a(s - 3)
                if in_range(s - 3):
                    quantise_b(s - 3)
                if in_range(s - 1) and s < TILES:
                    query_diagonal(s - 1)
                if in_range(s - 3) and s < TILES:
                    q1T_out(s - 3)
                if in_range(s + 1) and s:
                    xT_hi_out(s + 1)
                if in_range(s):
                    ctx_b(ctx_tiles(s)[0])
                if s == -1:
                    for k in range(KT):
                        split_w(k)
                if s > TILES:
                    for q in w2_ahead.get(s, ())[-2:]:
                        w2_out(q)
                if s == TILES:
                    expert_hi(2)
                    expert_hi(3)
                    for k in range(4):
                        x2T_hi_out(k)
                    act.wait_ge(gate_in, 16)
                    act.activation(so["gate_hi"][:], gate_raw, ACT.Copy).then_inc(S["gate_hi_done"], 1)
                if in_range(s - 3) and s >= TILES:
                    q1T_out(s - 3)
                if s == TILES + 2:
                    for i in range(2):
                        split_u(i)
                if in_range(s):
                    ctx_b(ctx_tiles(s)[1])
                if in_range(s - 1):
                    softmax_exp(s - 1)
                if in_range(s + 1):
                    load_ctx(s + 1)
                if s == TILES:
                    for m in range(MT):
                        fc2_hi_out(m)
                if in_range(s - 3) and s >= TILES:
                    cross_out(s - 3)
                if s == TILES:
                    x2T_hi_out(4)
                    x2T_hi_out(5)
            for q in w2_behind[TILES + 2]:
                w2_out(q)

        @block.vector
        def _(dve):
            def stats(t, first, st_done, mv_done):
                slot = t % 2 + (0 if first else 2)
                for n in range(NH):
                    ins = dve.bn_stats(stat[:, slot, n], res[:, t % XR, n * BANK:(n + 1) * BANK])
                ins.then_inc(st_done, 1)
                dve.wait_ge(st_done, t + 1)
                dve.bn_aggr(mv[:, slot], stat[:, slot].rearrange("p n s -> p (n s)")).then_inc(mv_done, 1)

            def normalise(t, first, rstd_done, done):
                slot = t % 2 + (0 if first else 2)
                dve.wait_ge(rstd_done, t + 1)
                dve.tensor_scalar(res[:, t % XR], res[:, t % XR], mv[:, slot, 0:1], rstd[:, slot:slot + 1],
                                  ALU.subtract, ALU.mult).then_inc(done, 1)

            def cross_residual(t):
                dve.wait_ge(S["xa_evac"], t + 1)
                dve.wait_ge(S["x1col_done"], t + 1)
                dve.tensor_tensor(res[:, t % XR], res[:, t % XR], xa_out[:], ALU.add).then_inc(S["x2pre_done"], 1)

            def last_stats(t):
                dve.wait_ge(S["x2pre_done"], t + 1)
                stats(t, False, S["st2_done"], S["mv2_done"])

            def softmax_max(t):
                dve.wait_ge(S["scores_ready"], t + 1)
                dve.tensor_reduce(s_max[:, t % 2], sc_ps[:], AX.X, ALU.max).then_inc(S["max_done"], 1)
                dve.wait_ge(S["max_done"], t + 1)
                if t >= 2:
                    dve.wait_ge(S["smT_done"], t - 1)
                dve.tensor_tensor(sm[:, t % 2], sc_ps[:], s_max[:, t % 2].unsqueeze(2).to_broadcast([P, NG * TQ, HD]),
                                  ALU.subtract).then_inc(S["sub_done"], 1)

            def values_transpose(t):
                dve.wait_ge(pg_in[t % 2], 16 * NG * (t // 2 + 1))
                if t >= 2:
                    dve.wait_ge(S["v_bd_done"], t - 1)
                dve.transpose(vT[:, t % 2], pg[:, t % 2, :, 2]).then_inc(S["vT_done"], 1)

            def collect(t):
                dve.wait_ge(S["av_ready"], t + 1)
                if t >= 2:
                    dve.wait_ge(o_in[t % 2], 16 * NG * (t // 2))
                dve.tensor_scalar(o_sb[:, t % 2], av_ps[:, :, 0, :], maskt[:, 0:1], None, ALU.mult).then_inc(S["o_part"], 1)
                for q in range(1, TQ):
                    dve.wait_ge(S["o_part"], (TQ - 1) * t + q)
                    ins = dve.scalar_tensor_tensor(out=o_sb[:, t % 2], in0=av_ps[:, :, q, :], scalar=maskt[:, q:q + 1],
                                                   in1=o_sb[:, t % 2], op0=ALU.mult, op1=ALU.add)
                    ins.then_inc(S["o_part"] if q < TQ - 1 else S["o_done"], 1)

            def residual(t):
                dve.wait_ge(res_in[t % XR], 16 * (t // XR + 1))
                dve.wait_ge(o_in[t % 2], 16 * NG * (t // 2 + 1))
                x = res[:, t % XR].rearrange("p (d g r) -> p d g r", g=GROUPS, r=REP)
                o = o_tok[:, t % 2].rearrange("p (g d) -> p d g", g=GROUPS).unsqueeze(3).to_broadcast([P, HD, GROUPS, REP])
                dve.tensor_tensor(x, x, o, ALU.add).then_inc(S["pre_done"], 1)

            def first_stats(t):
                dve.wait_ge(S["pre_done"], t + 1)
                stats(t, True, S["st1_done"], S["mv1_done"])

            def prepare(k):
                dve.wait_ge(wraw_in[k], 48)
                if k >= 4:
                    dve.wait_ge(S["wq_lo_done"], k - 3)
                dve.tensor_reduce(wq_sum(k).rearrange("p (g d) -> p g d", g=GROUPS),
                                  wq_raw(k).rearrange("p (d g r) -> p g d r", g=GROUPS, r=REP),
                                  AX.X, ALU.add).then_inc(S["wq_summed"], 1)

            def prepare_lo(k):
                dve.wait_ge(S["w_hi_done"], k + 1)
                dve.wait_ge(S["wq_summed"], k + 1)
                dve.tensor_tensor(part(w_lo[:, k], 0, 1), wq_sum(k).rearrange("p (c g d) -> p c g d", c=1, g=GROUPS),
                                  part(w_hi[:, k].bitcast(F32), 0, 1), ALU.subtract).then_inc(S["wq_lo_done"], 1)

            def constants():
                dve.wait_ge(S["ident_done"], 1)
                dve.tensor_reduce(maskj[:], ident[:].rearrange("p (j r) -> p j r", j=JQ), AX.X, ALU.add).then_inc(S["masks_done"], 1)
                dve.tensor_reduce(maskt[:], ident[:].rearrange("p (j t g) -> p t j g", j=JQ, t=TQ), AX.XY, ALU.add).then_inc(S["masks_done"], 1)
                dve.tensor_copy(so["ident_bf"][:], ident[:]).then_inc(S["masks_done"], 1)

            def biases():
                dve.wait_ge(bias_in, 48)
                dve.tensor_reduce(part(bias[:], 0, 1)[:, 0],
                                  bq_raw.rearrange("p (d g r) -> p g d r", g=GROUPS, r=REP), AX.X, ALU.add)
                dve.tensor_copy(part(bias[:], 1, 3),
                                bkv_raw.rearrange("p (c d g) -> p c g d", c=2, g=GROUPS)).then_inc(S["bias_done"], 1)

            def quant_constants():
                dve.wait_ge(quant_in, 64)
                dve.reciprocal(qp[:, 4:5], qp[:, 0:1])
                dve.reciprocal(qp[:, 5:6], qp[:, 2:3])
                dve.tensor_tensor(qp[:, 6:7], qp[:, 0:1], qp[:, 2:3], ALU.mult)
                dve.tensor_scalar(qp[:, 7:8], qp[:, 1:2], -1.0, QMID, ALU.mult, ALU.add)
                dve.tensor_scalar(qp[:, 8:9], qp[:, 3:4], -1.0, QMID, ALU.mult, ALU.add).then_inc(S["quant_done"], 1)
                dve.wait_ge(S["quant_done"], 1)
                dve.tensor_scalar(qp[:, 9:10], qp[:, 8:9], float(CTX), None, ALU.mult)
                dve.tensor_tensor(qp[:, 10:11], qp[:, 8:9], qp[:, 6:7], ALU.mult)
                dve.tensor_tensor(qp[:, 11:12], qp[:, 7:8], qp[:, 6:7], ALU.mult).then_inc(S["quant2_done"], 1)

            def x2T_lo_out(k):
                dve.wait_ge(S["x2T_hi_done"], k + 1)
                dve.tensor_tensor(x2T_lo[:, k], x2T_ps[k % 2], x2T_hi[:, k].bitcast(F32), ALU.subtract).then_inc(S["x2T_lo_done"], 1)

            def split_u(i):
                dve.wait_ge(S["u_hi_done"], i + 1)
                dve.wait_ge(S["scores_ready"], TILES)
                dve.wait_ge(S["exT_ready"], MT)
                dve.tensor_tensor(so["u_lo"][:, i], u_raw[:, i], so["u_hi"][:, i].bitcast(F32), ALU.subtract).then_inc(S["u_lo_done"], 1)

            def expert_lo(m):
                dve.wait_ge(S["exT_hi_done"], m + 1)
                dve.tensor_tensor(exT_lo[:, m], qkv_ps[:, m % 2 * BANK:(m % 2 + 1) * BANK], exT_hi[:, m].bitcast(F32), ALU.subtract).then_inc(S["exT_lo_done"], 1)

            def fc2_lo_out(m):
                dve.wait_ge(S["fc2_hi_done"], m + 1)
                dve.tensor_tensor(fc2_lo[m], fc2_raw[m], fc2_hi[:, m].bitcast(F32), ALU.subtract).then_inc(S["fc2_lo_done"], 1)

            def column_term(b):
                dve.wait_ge(S["col_ready"], b + 1)
                if b:
                    dve.wait_ge(S["x1col_done"], b * BT)
                dve.tensor_scalar(col[:], xa_ps[:], qp[:, 9:10], qp[:, 11:12], ALU.add, ALU.mult).then_inc(S["col_done"], 1)

            def softmax_sum(t):
                dve.wait_ge(S["exp_done"], t + 1)
                dve.tensor_reduce(s_sum[:, t % 2], sm[:, t % 2], AX.X, ALU.add).then_inc(S["sum_done"], 1)
                dve.wait_ge(S["sum_done"], t + 1)
                dve.reciprocal(s_rec[:, t % 2], s_sum[:, t % 2]).then_inc(S["rec_done"], 1)

            def magic(t):
                dve.wait_ge(S["relu_done"], t + 1)
                dve.tensor_scalar(y_sb[:], y_sb[:], QMAX, MAGIC, ALU.min, ALU.add).then_inc(S["magic_done"], 1)

            def ctx_magic(c):
                dve.wait_ge(S["c_relu"], c + 1)
                dve.tensor_scalar(c_sb[:, c % 2], c_sb[:, c % 2], QMAX, MAGIC, ALU.min, ALU.add).then_inc(S["c_magic"], 1)

            def qkv_out(t):
                dve.wait_ge(S["qkv_ready"], t + 1)
                if t >= 2:
                    dve.wait_ge(pg_in[t % 2], 16 * NG * (t // 2))
                dve.tensor_tensor(qkv_sb[:, t % 2], qkv_ps[:, 0:QKV], bias[:], ALU.add).then_inc(S["qkv_evac"], 1)

            def xT_lo_out(t):
                dve.wait_ge(S["xT_hi_done"], t + 1)
                dve.tensor_tensor(xT_lo[:, t % 2], tr_ps[:], xT_hi[:, t % 2].bitcast(F32), ALU.subtract).then_inc(S["xT_lo_done"], 1)

            def softmax_transpose(t):
                dve.wait_ge(S["norm_done"], t + 1)
                if t >= 2:
                    dve.wait_ge(S["av_ready"], t - 1)
                dve.transpose(smT[:, t % 2].rearrange("p n c -> p (n c)"), sm[:, t % 2].rearrange("p n c -> p (n c)")).then_inc(S["smT_done"], 1)

            constants()
            for s in steps:
                if in_range(s - 2):
                    softmax_sum(s - 2)
                if in_range(s - 3):
                    residual(s - 3)
                if in_range(s - 3) and s < TILES:
                    first_stats(s - 3)
                if in_range(s - 2) and s < TILES:
                    softmax_transpose(s - 2)
                if in_range(s - 3) and s < TILES:
                    normalise(s - 3, True, S["rstd1_done"], S["x1_done"])
                if s == TILES + 1:
                    fc2_lo_out(0)
                    fc2_lo_out(1)
                    softmax_transpose(s - 2)
                    x2T_lo_out(4)
                    x2T_lo_out(5)
                    fc2_lo_out(2)
                    fc2_lo_out(3)
                    collect(s - 2)
                    x2T_lo_out(6)
                    x2T_lo_out(7)
                if s == TILES + 2:
                    first_stats(s - 3)
                    normalise(s - 3, True, S["rstd1_done"], S["x1_done"])
                    magic(s - 3)
                if in_range(s - 4):
                    cross_residual(s - 4)
                if in_range(s - 3) and s < TILES:
                    magic(s - 3)
                if in_range(s - 4):
                    last_stats(s - 4)
                if s == TILES:
                    softmax_transpose(s - 2)
                if s == TILES:
                    expert_lo(0)
                    expert_lo(1)
                if s in (TILES, TILES + 1):
                    first_stats(s - 3)
                if in_range(s - 1):
                    values_transpose(s - 1)
                if in_range(s - 2) and s < TILES:
                    collect(s - 2)
                if in_range(s) and s:
                    ctx_magic(ctx_tiles(s)[0])
                if s in (TILES, TILES + 1):
                    normalise(s - 3, True, S["rstd1_done"], S["x1_done"])
                if in_range(s - 4):
                    normalise(s - 4, False, S["rstd2_done"], S["x2_done"])
                if s in (TILES, TILES + 1):
                    magic(s - 3)
                if s == TILES:
                    collect(s - 2)
                if s == TILES:
                    expert_lo(2)
                    expert_lo(3)
                    x2T_lo_out(0)
                    x2T_lo_out(1)
                if in_range(s):
                    if s == 0:
                        dve.wait_ge(S["bias_done"], 1)
                    qkv_out(s)
                if in_range(s) and s:
                    ctx_magic(ctx_tiles(s)[1])
                if s == -1:
                    prepare(0)
                if in_range(s + 1):
                    xT_lo_out(s + 1)
                for c in ctx_tiles(s) if s == 0 else ():
                    ctx_magic(c)
                if in_range(s - 1):
                    softmax_max(s - 1)
                if s == TILES:
                    x2T_lo_out(2)
                    x2T_lo_out(3)
                    dve.wait_ge(S["gate_hi_done"], 1)
                    dve.tensor_tensor(so["gate_lo"][:], gate_raw, so["gate_hi"][:].bitcast(F32), ALU.subtract).then_inc(S["gate_lo_done"], 1)
                if s == TILES + 2:
                    for i in range(2):
                        split_u(i)
                if s == -1:
                    for k in range(1, KT + 1):
                        if k < KT:
                            prepare(k)
                        prepare_lo(k - 1)
                    quant_constants()
                    biases()
                if in_range(s - 3) and (s - 3) % BT == 0:
                    column_term((s - 3) // BT)

        @block.gpsimd
        def _(pool):
            def keys_values_lo(k):
                pool.wait_ge(wraw_in[k], 48)
                pool.wait_ge(S["w_hi_done"], k + 1)
                pool.tensor_tensor(part(w_lo[:, k], 1, 3), wkv_raw(k).rearrange("p (c d g) -> p c g d", c=2, g=GROUPS),
                                   part(w_hi[:, k].bitcast(F32), 1, 3), ALU.subtract).then_inc(S["wkv_lo_done"], 1)

            def values_diagonal(t):
                pool.wait_ge(S["vT_done"], t + 1)
                if t >= 2:
                    pool.wait_ge(S["av_ready"], t - 1)
                for j in range(JQ):
                    ins = pool.tensor_scalar(v_bd[:, t % 2, :, j, :], vT[:, t % 2], maskj[:, j:j + 1], 1.0, ALU.mult, ALU.mult)
                ins.then_inc(S["v_bd_done"], 1)

            def inverse_deviation(t, first, mv_done, ve_done, rstd_done):
                slot = t % 2 + (0 if first else 2)
                pool.wait_ge(mv_done, t + 1)
                pool.tensor_scalar(veps[:, slot:slot + 1], mv[:, slot, 1:2], EPS, 1.0, ALU.add, ALU.mult).then_inc(ve_done, 1)
                pool.wait_ge(ve_done, t + 1)
                pool.tensor_tensor(rstd[:, slot:slot + 1], veps[:, slot:slot + 1], so["neg_half"][:], ALU.pow).then_inc(rstd_done, 1)

            def softmax_scale(t):
                pool.wait_ge(S["rec_done"], t + 1)
                pool.tensor_tensor(sm[:, t % 2], sm[:, t % 2], s_rec[:, t % 2].unsqueeze(2).to_broadcast([P, NG * TQ, HD]),
                                   ALU.mult).then_inc(S["norm_done"], 1)

            def row_term(t):
                pool.wait_ge(S["q1_done"], t + 1)
                pool.tensor_scalar(rowterm[:, t % 4:t % 4 + 1], rowsum[:, t % 4:t % 4 + 1], qp[:, 10:11], 1.0, ALU.mult, ALU.mult).then_inc(S["rowterm_done"], 1)

            def keys_diagonal(t):
                pool.wait_ge(pg_in[t % 2], 16 * NG * (t // 2 + 1))
                if t >= 2:
                    pool.wait_ge(S["scores_ready"], t - 1)
                for q in range(TQ):
                    ins = pool.tensor_scalar(k_bd[:, t % 2, :, q, :], pg[:, t % 2, :, 1], maskt[:, q:q + 1], 1.0, ALU.mult, ALU.mult)
                ins.then_inc(S["k_bd_done"], 1)

            def add_column_term(t):
                if t % BT == 0:
                    pool.wait_ge(S["col_done"], t // BT + 1)
                pool.wait_ge(S["relu_done"], t + 1)
                pool.tensor_tensor(res[:, t % XR], res[:, t % XR], col[:], ALU.add).then_inc(S["x1col_done"], 1)

            pool.memset(ident[:], 0.0).then_inc(S["ident_zero"], 1)
            pool.wait_ge(S["ident_zero"], 1)
            pool.affine_select(out=ident[:], in_=ident[:], compare_op=ALU.not_equal, fill=1.0, base=0,
                               pattern=[[-1, P]], channel_multiplier=1).then_inc(S["ident_done"], 1)
            pool.memset(so["ones_bf"][:], 1.0)
            pool.memset(so["neg_half"][:], -0.5)
            pool.memset(so["unmagic"][:], -(MAGIC + QMID)).then_inc(S["consts_done"], 1)
            pool.wait_ge(S["consts_done"], 1)
            pool.wait_ge(S["masks_done"], 3)
            for k in range(KT):
                keys_values_lo(k)
            pool.wait_ge(S["quant2_done"], 1)
            for s in steps:
                if in_range(s - 2):
                    softmax_scale(s - 2)
                if in_range(s - 1) and s >= TILES:
                    keys_diagonal(s - 1)
                if s in (TILES, TILES + 1):
                    inverse_deviation(s - 4, False, S["mv2_done"], S["ve2_done"], S["rstd2_done"])
                if in_range(s - 3):
                    inverse_deviation(s - 3, True, S["mv1_done"], S["ve1_done"], S["rstd1_done"])
                if in_range(s - 1) and s < TILES:
                    keys_diagonal(s - 1)
                if in_range(s - 4) and s not in (TILES, TILES + 1):
                    inverse_deviation(s - 4, False, S["mv2_done"], S["ve2_done"], S["rstd2_done"])
                if in_range(s - 1):
                    values_diagonal(s - 1)
                if in_range(s - 3):
                    row_term(s - 3)
                    add_column_term(s - 3)


KH = HID // P
KL = LAT // P
KD = KH + KL
WT = KH + KL


def feed_forward(nc, so, args, x2_dram, w2_dram, out):
    ident = so["ident"]
    with ExitStack() as ctx:
        sb = lambda name, shape, dt: ctx.enter_context(nc.sbuf_tensor(name, shape, dt))
        ps = lambda name, shape, dt: ctx.enter_context(nc.psum_tensor(name, shape, dt))
        sem = lambda name: ctx.enter_context(nc.semaphore(name))
        DH = 4
        tail = lambda b, n: 2 * DH if (b, n) == (BATCH - 1, NH - 1) else DH // 2
        used_before = lambda j: sum(KD - tail(i // NH, i % NH) for i in range(j))
        XO = KD - DH - KT
        x2T_hi, x2T_lo = so["x2T_hi"], so["x2T_lo"]
        xk, x2r_sb = so["xk"], so["x2r"]
        h_hi, h_lo = sb("h_hi", [P, KD, SEQ], F32R), sb("h_lo", [P, KD, SEQ], F32R)
        u_raw = so["u_raw"][:].rearrange("p (i k c) -> p i k c", i=2, k=KT)
        u_hi, u_lo = so["u_hi"], so["u_lo"]
        d_raw = sb("d_raw", [P, 2, BANK], F32)
        d_hi, d_lo = sb("d_hi", [P, DH, BANK], F32R), sb("d_lo", [P, DH, BANK], F32R)
        act_sb = sb("act_sb", [P, 2, SEQ], F32)
        TD = BATCH * NH * KD - 2 * DH
        d_more = [u[:].rearrange("p i k c -> p (i k c)").rearrange("p (s c) -> p s c", s=DH) for u in (u_hi, u_lo)]

        def d_slot(which, i):
            if TD <= i < TD + DH:
                return d_more[which][:, i % DH]
            return (d_hi, d_lo)[which][:, i % DH]

        rT = sb("rT", [P, SEQ], F32)
        lgT = rT[0:EXPERTS, :]
        gate_hi, gate_lo = so["gate_hi"], so["gate_lo"]
        top = sb("top", [P, BT, 8], F32)
        r_tok, r_diag = sb("r_tok", [P, BT], F32), sb("r_diag", [P, BT, P], F32)
        ones = sb("ones", [P, P], F32)
        ffn = sb("ffn", [P, BT, EMB], F32)
        x2b = [x2r_sb[:, 0], x2r_sb[:, 1]] + [xk[:, 2 * i:2 * i + 2].rearrange("p s t c -> p (s t c)") for i in range(2)]
        gamma, beta = sb("gamma", [P, EMB], F32), sb("beta", [P, EMB], F32)
        stat, mv = sb("stat_f", [P, 2, BT, NH, 6], F32), sb("mv_f", [P, 2, BT, 2], F32)
        veps, rstd = sb("veps_f", [P, 2, BT], F32), sb("rstd_f", [P, 2, BT], F32)
        nbias = sb("nbias", [P, BT], F32)
        acc = ps("acc", [P, BT, BANK], F32)
        u_ps = ps("u_ps", [P, 2, BANK], F32)
        t_ps = ps("t_ps", [P, 2, BANK], F32)

        xk_in = [sem(f"f_xk_in{i}") for i in range(XS)]
        u_in, d_in = so["u_in"], [sem("d_in0"), sem("d_in1")]
        x2r_in = [sem(f"x2r_in{i}") for i in range(BT)]
        const_in, out_st, last_st = sem("const_in"), sem("out_st"), sem("last_st")
        names = """ones_done lgT_ready lgT_done logits_ready top_done
            r_done rdiag_done rT_ready rT_done u_ready lat_scaled act_done h_hi_done sq_done
            h_lo_done d_hi_done d_lo_done d_used acc_ready acc_evac stA_done mvA_done veA_done rsA_done
            x2b_done gam_done res_done stB_done mvB_done veB_done rsB_done out_done pow_done""".split()
        S = {**so["sem"], **{n: sem("f_" + n) for n in names}}
        block = ctx.enter_context(nc.Block())

        u_src = [args[w].rearrange("(k p) (m c) -> m p k c", p=P, c=P) for w in ("up_w", "fc1_w")]
        out_rows = out.rearrange("b s e -> (b s) e")
        NB = NH * KD

        def block1_stored(eng):
            for n in range(XR):
                eng.wait_ge(so["x2_st"][n], 16 * len(range(n, TILES, XR)))
            eng.wait_ge(so["w2_stored"], 16 * MT)

        @block.sync
        def _(sp):
            def load_xk(b, k):
                if k >= XS:
                    sp.wait_ge(S["x2T_ready"], b * KT + k - XS + 1)
                src = x2_dram[b * SEQ:(b + 1) * SEQ, k * P:(k + 1) * P].rearrange("(t p) c -> p t c", p=P)
                sp.dma_start(xk[:, k % XS], src).then_inc(xk_in[k % XS], 16)

            def load_u(b, m):
                i = b * WT + m
                if i >= 2:
                    sp.wait_ge(S["u_lo_done"], i - 1)
                sp.dma_start(u_raw[:, i % 2], u_src[0][m] if m < KH else u_src[1][m - KH]).then_inc(u_in[i % 2], 16)

            def load_d(b, n, k):
                i = b * NB + n * KD + k
                if i >= 2:
                    sp.wait_ge(S["d_lo_done"], i - 1)
                rows = args["down_w"][k * P:(k + 1) * P] if k < KH else w2_dram[(k - KH) * P:(k - KH + 1) * P]
                sp.dma_start(d_raw[:, i % 2], rows[:, n * BANK:(n + 1) * BANK]).then_inc(d_in[i % 2], 16)

            load_u(0, 2)
            block1_stored(sp)
            sp.dma_start(gamma[:], args["ln_gamma"].partition_broadcast(P)).then_inc(const_in, 16)
            sp.dma_start(beta[:], args["ln_beta"].partition_broadcast(P)).then_inc(const_in, 16)
            for b in range(BATCH):
                for m in range(2 if b else 3, WT):
                    load_u(b, m)
                for n in range(NH):
                    for k in range(KD):
                        load_d(b, n, k)
                        if b + 1 < BATCH and n == NH - 1:
                            if XO - XS <= k < XO:
                                load_xk(b + 1, k - (XO - XS))
                            if XO + 6 <= k < XO + 6 + KT - XS:
                                load_xk(b + 1, XS + k - (XO + 6))
                            if k >= KD - 2:
                                load_u(b + 1, k - (KD - 2))

            for i in range(TILES - BT, TILES):
                sp.wait_ge(S["out_done"], i + 1)
                sp.dma_start(out_rows[i * P:(i + 1) * P, :], ffn[:, i % BT]).then_inc(last_st, 16)
            sp.wait_ge(last_st, 16 * BT)

        @block.tensor
        def _(pe):
            def transpose_x2(b, k):
                i = b * KT + k
                pe.wait_ge(xk_in[k % XS], 16 * (k // XS + 1))
                if k >= 2:
                    pe.wait_ge(S["x2T_lo_done"], i - 1)
                if k == 0:
                    pe.wait_ge(S["rT_done"], b)
                    pe.wait_ge(S["top_done"], b)
                for t in range(BT):
                    mm = pe.transpose(t_ps[:, i % 2, t * P:(t + 1) * P], xk[:, k % XS, t], ident[:])
                mm.then_inc(S["x2T_ready"], 1)

            def routing(b):
                pe.wait_ge(S["x2T_lo_done"], (b + 1) * KT)
                pe.wait_ge(S["gate_lo_done"], 1)
                for k in range(KT):
                    for i, (s, v) in enumerate(split_products([g[:, k] for g in (gate_hi, gate_lo)], [x[:, k] for x in (x2T_hi, x2T_lo)])):
                        mm = pe.matmul(t_ps[0:EXPERTS, 0], s, v, start=(k == 0 and i == 0), stop=(k == KT - 1 and i == 2))
                mm.then_inc(S["lgT_ready"], 1)

            def transpose_logits(b):
                pe.wait_ge(S["lgT_done"], b + 1)
                for t in range(BT):
                    mm = pe.transpose(t_ps[:, 0, t * EXPERTS:(t + 1) * EXPERTS], lgT[:, t * P:(t + 1) * P], ident[0:EXPERTS, 0:EXPERTS])
                mm.then_inc(S["logits_ready"], 1)

            def spread_r(b):
                pe.wait_ge(S["ones_done"], 1)
                for t in range(BT):
                    pe.wait_ge(S["rdiag_done"], b * BT + t + 1)
                    mm = pe.matmul(t_ps[:, 1, t * P:(t + 1) * P], ones[:], r_diag[:, t], start=True, stop=True)
                mm.then_inc(S["rT_ready"], 1)

            def first_product(i, slot):
                pe.wait_ge(S["u_lo_done"], i + 1)
                for k in range(KT):
                    st = [u[:, slot, k] for u in (u_hi, u_lo)]
                    for j, (s, v) in enumerate(split_products(st, [x[:, k] for x in (x2T_hi, x2T_lo)])):
                        mm = pe.matmul(u_ps[:, slot], s, v, start=(k == 0 and j == 0), stop=(k == KT - 1 and j == 2))
                mm.then_inc(S["u_ready"], 1)

            def second_product(b, n, k, t):
                i = b * NB + n * KD + k
                pe.wait_ge(S["d_lo_done"], i + 1)
                if k == 0 and b + n:
                    pe.wait_ge(S["acc_evac"], (b * NH + n - 1) * BT + t + 1)
                if n == 0:
                    pe.wait_ge(S["h_lo_done"], b * KD + k + 1)
                st = [h[:, k, t * P:(t + 1) * P] for h in (h_hi, h_lo)]
                for j, (s, v) in enumerate(split_products(st, [d_slot(which, i) for which in range(2)])):
                    mm = pe.matmul(acc[:, t], s, v, start=(k == 0 and j == 0), stop=(k == KD - 1 and j == 2))
                if k == KD - 1:
                    mm.then_inc(S["acc_ready"], 1)
                elif t == BT - 1 and k < KD - tail(b, n):
                    mm.then_inc(S["d_used"], 1)

            for b in range(BATCH):
                routing(b)
                for m in range(2):
                    if b:
                        pe.wait_ge(S["lat_scaled"], b * KL - 1 + m)
                    first_product(b * WT + m, m)
                    if m == 0:
                        transpose_logits(b)
                with pe.Fori(1, KH // 2) as p:
                    for slot in range(2):
                        pe.wait_ge(S["act_done"], 2 * p + (b * KH + slot - 1))
                        first_product(2 * p + (b * WT + slot), slot)
                spread_r(b)
                for m in range(KL):
                    if m < 2:
                        pe.wait_ge(S["act_done"], (b + 1) * KH - 1 + m)
                    else:
                        pe.wait_ge(S["lat_scaled"], b * KL + m - 1)
                    first_product(b * WT + KH + m, m % 2)
                for n in range(NH):
                    for k in range(KD - tail(b, n)):
                        for t in range(BT):
                            second_product(b, n, k, t)
                        if b + 1 < BATCH and n == NH - 1 and XO <= k < XO + KT:
                            transpose_x2(b + 1, k - XO)
                    for t in range(BT):
                        for k in range(KD - tail(b, n), KD):
                            second_product(b, n, k, t)

        def d_step(eng, b, n, k, which):
            i = b * NB + n * KD + k
            if which == "hi":
                eng.wait_ge(d_in[i % 2], 16 * (i // 2 + 1))
                if TD <= i < TD + DH:
                    eng.wait_ge(S["u_ready"], BATCH * WT)
                elif i >= DH:
                    last = i - DH if i < TD else i - 2 * DH
                    j, kj = last // KD, last % KD
                    if kj >= KD - tail(j // NH, j % NH):
                        eng.wait_ge(S["acc_ready"], (j + 1) * BT)
                    else:
                        eng.wait_ge(S["d_used"], used_before(j) + kj + 1)
                eng.activation(d_slot(0, i), d_raw[:, i % 2], ACT.Copy).then_inc(S["d_hi_done"], 1)
            else:
                eng.wait_ge(S["d_hi_done"], i + 1)
                eng.tensor_tensor(d_slot(1, i), d_raw[:, i % 2], d_slot(0, i).bitcast(F32), ALU.subtract).then_inc(S["d_lo_done"], 1)

        @block.scalar
        def _(act):
            def x2T_hi_out(b, k):
                i = b * KT + k
                act.wait_ge(S["x2T_ready"], i + 1)
                if b and k == 0:
                    act.wait_ge(S["u_ready"], b * WT)
                act.activation(x2T_hi[:, k], t_ps[:, i % 2], ACT.Copy).then_inc(S["x2T_hi_done"], 1)

            def split_u(i, slot, in_count):
                act.wait_ge(u_in[slot], in_count)
                if not (isinstance(i, int) and i < 2):
                    act.wait_ge(S["u_ready"], i - 1)
                act.activation(u_hi[:, slot], u_raw[:, slot], ACT.Copy).then_inc(S["u_hi_done"], 1)

            def hidden(m, slot, i, count):
                act.wait_ge(S["u_ready"], i + 1)
                if not (isinstance(i, int) and i < 2):
                    act.wait_ge(S["h_lo_done"], i - 1)
                act.activation(act_sb[:, slot], u_ps[:, slot], ACT.Relu).then_inc(S["act_done"], 1)
                act.wait_ge(S["act_done"], count + 1)
                act.activation(h_hi[:, m], act_sb[:, slot], ACT.Square).then_inc(S["h_hi_done"], 1)

            def latent_hi(b, m):
                act.wait_ge(S["lat_scaled"], b * KL + m + 1)
                act.activation(h_hi[:, KH + m], act_sb[:, m % 2], ACT.Copy).then_inc(S["h_hi_done"], 1)

            def logits_out(b):
                act.wait_ge(S["lgT_ready"], b + 1)
                if b:
                    act.wait_ge(S["lat_scaled"], b * KL)
                act.activation(lgT, t_ps[0:EXPERTS, 0], ACT.Copy).then_inc(S["lgT_done"], 1)

            def spread_out(b):
                act.wait_ge(S["rT_ready"], b + 1)
                act.wait_ge(S["logits_ready"], b + 1)
                act.activation(rT[:], t_ps[:, 1], ACT.Copy).then_inc(S["rT_done"], 1)

            def final_norm(i):
                act.wait_ge(S["rsB_done"], i + 1)
                act.activation(ffn[:, i % BT], ffn[:, i % BT], ACT.Identity, bias=nbias[:, i % BT:i % BT + 1],
                               scale=rstd[:, 1, i % BT:i % BT + 1]).then_inc(S["out_done"], 1)

            block1_stored(act)
            for b in range(BATCH):
                w0 = b * WT
                if b:
                    act.wait_ge(S["acc_ready"], b * NH * BT)
                logits_out(b)
                for m in range(2):
                    hidden(m, m, w0 + m, b * KH + m)
                    split_u(w0 + m + 2, m, 16 * (w0 // 2 + 2))
                with act.Fori(1, KH // 2) as p:
                    for slot in range(2):
                        i = 2 * p + (w0 + slot)
                        hidden(2 * p + slot, slot, i, 2 * p + (b * KH + slot))
                        split_u(i + 2, slot, 16 * (p + w0 // 2 + 2))
                spread_out(b)
                for m in range(KL):
                    if m < 2:
                        latent_hi(b, m)
                        split_u(w0 + KH + m + 2, m, 16 * ((w0 + KH) // 2 + 2))
                    else:
                        d_step(act, b, 0, m - 2, "hi")
                        latent_hi(b, m)
                for n in range(NH):
                    last = b + 1 < BATCH and n == NH - 1
                    for k in range(2, KD):
                        d_step(act, b, n, k, "hi")
                        if last and k >= XO + DH:
                            x2T_hi_out(b + 1, k - (XO + DH))
                        if last and k >= KD - 2:
                            split_u(w0 + WT + k - (KD - 2), k - (KD - 2), 16 * ((w0 + WT) // 2 + 1))
                    if n + 1 < NH:
                        for k in range(2):
                            d_step(act, b, n + 1, k, "hi")
                    for t in range(BT):
                        act.wait_ge(S["acc_ready"], (b * NH + n) * BT + t + 1)
                        if b and n == 0:
                            act.wait_ge(out_st, 16 * b * BT)
                        act.activation(ffn[:, t, n * BANK:(n + 1) * BANK], acc[:, t], ACT.Copy).then_inc(S["acc_evac"], 1)
                        if b == BATCH - 1 and n == NH - 1 and t:
                            final_norm(b * BT + t - 1)
            final_norm(TILES - 1)

        @block.vector
        def _(dve):
            def x2T_lo_out(b, k):
                i = b * KT + k
                dve.wait_ge(S["x2T_hi_done"], i + 1)
                dve.tensor_tensor(x2T_lo[:, k], t_ps[:, i % 2], x2T_hi[:, k].bitcast(F32), ALU.subtract).then_inc(S["x2T_lo_done"], 1)

            def split_u(i, slot):
                dve.wait_ge(S["u_hi_done"], i + 1)
                dve.tensor_tensor(u_lo[:, slot], u_raw[:, slot], u_hi[:, slot].bitcast(F32), ALU.subtract).then_inc(S["u_lo_done"], 1)

            def hidden(m, slot, i, count):
                dve.wait_ge(S["h_hi_done"], i + 1)
                dve.tensor_tensor(act_sb[:, slot], act_sb[:, slot], act_sb[:, slot], ALU.mult).then_inc(S["sq_done"], 1)
                dve.wait_ge(S["sq_done"], count + 1)
                dve.tensor_tensor(h_lo[:, m], act_sb[:, slot], h_hi[:, m].bitcast(F32), ALU.subtract).then_inc(S["h_lo_done"], 1)

            def route(b):
                dve.wait_ge(S["logits_ready"], b + 1)
                for t in range(BT):
                    ins = dve.max(top[:, t], t_ps[:, 0, t * EXPERTS:(t + 1) * EXPERTS])
                ins.then_inc(S["top_done"], 1)
                dve.wait_ge(S["top_done"], b + 1)
                for t in range(BT):
                    dve.tensor_tensor(r_tok[:, t:t + 1], top[:, t, 0:1], top[:, t, 1:2], ALU.add).then_inc(S["r_done"], 1)
                dve.wait_ge(S["r_done"], (b + 1) * BT)
                for t in range(BT):
                    dve.tensor_scalar(r_diag[:, t], ident[:], r_tok[:, t:t + 1], None, ALU.mult).then_inc(S["rdiag_done"], 1)

            def latent(b, m):
                i = b * WT + KH + m
                dve.wait_ge(S["u_ready"], i + 1)
                dve.wait_ge(S["rT_done"], b + 1)
                dve.wait_ge(S["h_lo_done"], i - 1)
                dve.tensor_tensor(act_sb[:, m % 2], u_ps[:, m % 2], rT[:], ALU.mult).then_inc(S["lat_scaled"], 1)
                dve.wait_ge(S["h_hi_done"], i + 1)
                dve.tensor_tensor(h_lo[:, KH + m], act_sb[:, m % 2], h_hi[:, KH + m].bitcast(F32), ALU.subtract).then_inc(S["h_lo_done"], 1)

            def half_stats(i, n):
                dve.wait_ge(S["acc_evac"], (i // BT * NH + n) * BT + i % BT + 1)
                dve.bn_stats(stat[:, 0, i % BT, n], ffn[:, i % BT, n * BANK:(n + 1) * BANK]).then_inc(S["stA_done"], 1)

            def row_stats(i):
                dve.wait_ge(S["stA_done"], NH * (i // BT) * BT + BT + i % BT + 1)
                dve.bn_aggr(mv[:, 0, i % BT], stat[:, 0, i % BT].rearrange("p n s -> p (n s)")).then_inc(S["mvA_done"], 1)

            def scale_and_add(i):
                t = i % BT
                dve.wait_ge(S["mvA_done"], i + 1)
                dve.scalar_tensor_tensor(out=ffn[:, t], in0=ffn[:, t], scalar=mv[:, 0, t, 0:1], in1=gamma[:],
                                         op0=ALU.subtract, op1=ALU.mult).then_inc(S["gam_done"], 1)
                dve.wait_ge(S["gam_done"], i + 1)
                dve.wait_ge(S["rsA_done"], i + 1)
                dve.wait_ge(S["x2b_done"], i + 1)
                dve.scalar_tensor_tensor(out=ffn[:, t], in0=ffn[:, t], scalar=rstd[:, 0, t:t + 1], in1=x2b[t],
                                         op0=ALU.mult, op1=ALU.add).then_inc(S["res_done"], 1)

            def last_stats(i):
                t = i % BT
                dve.wait_ge(S["res_done"], i + 1)
                for n in range(NH):
                    ins = dve.bn_stats(stat[:, 1, t, n], ffn[:, t, n * BANK:(n + 1) * BANK])
                ins.then_inc(S["stB_done"], 1)
                dve.wait_ge(S["stB_done"], i + 1)
                dve.bn_aggr(mv[:, 1, t], stat[:, 1, t].rearrange("p n s -> p (n s)")).then_inc(S["mvB_done"], 1)

            def last_norm(i):
                t = i % BT
                dve.wait_ge(S["rsB_done"], i + 1)
                dve.tensor_scalar(ffn[:, t], ffn[:, t], mv[:, 1, t, 0:1], rstd[:, 1, t:t + 1], ALU.subtract, ALU.mult).then_inc(S["out_done"], 1)

            block1_stored(dve)
            dve.memset(ones[:], 1.0).then_inc(S["ones_done"], 1)
            dve.wait_ge(const_in, 32)
            for b in range(BATCH):
                w0 = b * WT
                route(b)
                if b == 0:
                    with dve.Fori(0, KH // 2) as p:
                        for slot in range(2):
                            hidden(2 * p + slot, slot, 2 * p + slot, 2 * p + slot)
                            split_u(2 * p + (slot + 2), slot)
                else:
                    for m in range(KH):
                        hidden(m, m % 2, w0 + m, b * KH + m)
                        split_u(w0 + m + 2, m % 2)
                        i = (b - 1) * BT + m // 3
                        if m < 3 * BT:
                            if m % 3 == 0:
                                half_stats(i, 1)
                                row_stats(i)
                            elif m % 3 == 1:
                                scale_and_add(i)
                            else:
                                last_stats(i)
                        if m % 3 == 0 and 0 < m <= 3 * BT:
                            last_norm(i - 1)
                for m in range(KL):
                    if m < 2:
                        latent(b, m)
                        split_u(w0 + KH + m + 2, m)
                    else:
                        d_step(dve, b, 0, m - 2, "lo")
                        latent(b, m)
                for n in range(NH):
                    last = b + 1 < BATCH and n == NH - 1
                    for k in range(2, KD):
                        d_step(dve, b, n, k, "lo")
                        if last and k >= XO + DH:
                            x2T_lo_out(b + 1, k - (XO + DH))
                        if last and k >= KD - 2:
                            split_u(w0 + WT + k - (KD - 2), k - (KD - 2))
                        if n == NH - 1 and 6 <= k < 6 + BT:
                            half_stats(b * BT + k - 6, 0)
                    if n + 1 < NH:
                        for k in range(2):
                            d_step(dve, b, n + 1, k, "lo")
            for t in range(BT):
                i = (BATCH - 1) * BT + t
                half_stats(i, 1)
                row_stats(i)
                scale_and_add(i)
                last_stats(i)

        @block.gpsimd
        def _(pool):
            def load_x2(i):
                if i == 0:
                    pool.wait_ge(S["x2T_ready"], BATCH * KT)
                if i >= BT:
                    pool.wait_ge(S["res_done"], i - BT + 1)
                pool.dma_start(x2b[i % BT], x2_dram[i * P:(i + 1) * P, :]).then_inc(x2r_in[i % BT], 16)

            def add_beta(i):
                pool.wait_ge(x2r_in[i % BT], 16 * (i // BT + 1))
                pool.tensor_tensor(x2b[i % BT], x2b[i % BT], beta[:], ALU.add).then_inc(S["x2b_done"], 1)

            def inverse_deviation(i, which, x):
                t = i % BT
                pool.wait_ge(S[f"mv{x}_done"], i + 1)
                pool.tensor_scalar(veps[:, which, t:t + 1], mv[:, which, t, 1:2], EPS, 1.0, ALU.add, ALU.mult).then_inc(S[f"ve{x}_done"], 1)
                pool.wait_ge(S[f"ve{x}_done"], i + 1)
                ins = pool.tensor_tensor(rstd[:, which, t:t + 1], veps[:, which, t:t + 1], so["neg_half"][:], ALU.pow)
                if x == "B" and i >= TILES - BT:
                    ins.then_inc(S["pow_done"], 1)
                    pool.wait_ge(S["pow_done"], i - (TILES - BT) + 1)
                    ins = pool.tensor_scalar(nbias[:, t:t + 1], mv[:, 1, t, 0:1], rstd[:, 1, t:t + 1], -1.0, ALU.mult, ALU.mult)
                ins.then_inc(S[f"rs{x}_done"], 1)

            def store(i):
                pool.wait_ge(S["out_done"], i + 1)
                pool.dma_start(out_rows[i * P:(i + 1) * P, :], ffn[:, i % BT]).then_inc(out_st, 16)

            block1_stored(pool)
            pool.wait_ge(const_in, 32)
            for t in range(BT):
                load_x2(t)
            for t in range(BT):
                add_beta(t)
            for b in range(BATCH):
                for t in range(BT):
                    i = b * BT + t
                    inverse_deviation(i, 0, "A")
                    inverse_deviation(i, 1, "B")
                    if b + 1 < BATCH:
                        store(i)
                        load_x2(i + BT)
                if b + 1 < BATCH:
                    for t in range(BT):
                        add_beta((b + 1) * BT + t)
            pool.wait_ge(out_st, 16 * (TILES - BT))


def decoder(nc, args, out):
    x2_dram = nc.dram_tensor("x2_scratch", [TOKENS, EMB], F32, kind="Internal").ap()
    w2_dram = nc.dram_tensor("w2_scratch", [LAT, EMB], F32, kind="Internal").ap()
    with ExitStack() as ctx:
        sb = lambda name, shape, dt: ctx.enter_context(nc.sbuf_tensor(name, shape, dt))
        so = {
            "ident": sb("ident", [P, P], F32),
            "ident_bf": sb("ident_bf", [P, P], BF16),
            "ones_bf": sb("ones_bf", [P, P], BF16),
            "maskj": sb("maskj", [P, JQ], F32),
            "maskt": sb("maskt", [P, TQ], F32),
            "neg_half": sb("neg_half", [P, 1], F32),
            "unmagic": sb("unmagic", [P, 1], F32),
            "quant": sb("quant", [P, 12], F32),
            "gate_hi": sb("gate_hi", [P, KT, EXPERTS], F32R),
            "gate_lo": sb("gate_lo", [P, KT, EXPERTS], F32R),
        }

        def passing(name, shape, dt):
            with nc.sbuf_tensor(name, shape, dt) as x:
                so[name] = x

        def staying(name, shape, dt):
            so[name] = sb(name, shape, dt)

        passing("w_hi", [P, KT, QKV], F32R)
        staying("x2T_hi", [P, KT, SEQ], F32R)
        passing("fc2_lo_a", [P, 2, EMB], F32R)
        staying("xk", [P, XS, BT, P], F32)
        passing("w_lo", [P, KT, QKV], F32R)
        staying("x2T_lo", [P, KT, SEQ], F32R)
        passing("fc2_lo_b", [P, 2, EMB], F32R)
        staying("x2r", [P, 2, EMB], F32)
        passing("smT", [P, 2, NG, TQ * HD], F32)
        staying("u_hi", [P, 2, KT, P], F32R)
        passing("q_bd", [P, 2, NG, JQ, HD], F32)
        staying("u_lo", [P, 2, KT, P], F32R)
        so["u_raw"] = sb("u_raw", [P, 2 * EMB], F32)
        names = "x2T_ready x2T_hi_done x2T_lo_done u_hi_done u_lo_done gate_hi_done gate_lo_done".split()
        so["sem"] = {n: ctx.enter_context(nc.semaphore(n)) for n in names}
        so["u_in"] = [ctx.enter_context(nc.semaphore(f"u_in{i}")) for i in range(2)]
        so["x2_st"] = [ctx.enter_context(nc.semaphore(f"x2_st{i}")) for i in range(XR)]
        so["w2_stored"] = ctx.enter_context(nc.semaphore("w2_stored"))
        attention_and_cross(nc, so, args, x2_dram, w2_dram)
        feed_forward(nc, so, args, x2_dram, w2_dram, out)


_INS = {"x": "x", "ctx_4096": "ctx", "L0_attn_Wq": "Wq", "L0_attn_bq": "bq", "L0_attn_Wk": "Wk", "L0_attn_bk": "bk",
        "L0_attn_Wv": "Wv", "L0_attn_bv": "bv", "L0_xattn_x1_scale": "x1_scale", "L0_xattn_x1_zp": "x1_zp",
        "L0_xattn_x2_scale": "x2_scale", "L0_xattn_x2_zp": "x2_zp", "L0_ffn_gate_w": "gate_w", "L0_ffn_up_w": "up_w",
        "L0_ffn_down_w": "down_w", "L0_ffn_fc1_w": "fc1_w", "L0_ffn_fc2_w": "fc2_w", "L0_ffn_expert_w": "expert_w",
        "L0_ffn_ln_gamma": "ln_gamma", "L0_ffn_ln_beta": "ln_beta"}


def kernel(**inputs):
    import numpy as _np
    import concourse.bacc as _bacc
    from concourse import mybir as _mybir
    from concourse.bass_utils import run_bass_kernel_spmd as _run

    nc = _bacc.Bacc("TRN2", target_bir_lowering=False, num_devices=1)
    arrays, args = {}, {}
    for name, short in _INS.items():
        a = _np.ascontiguousarray(inputs[name])
        arrays[f"in_{name}_dram"] = a
        args[short] = nc.dram_tensor(f"in_{name}_dram", a.shape, _mybir.dt.from_np(a.dtype), kind="ExternalInput").ap()
    out = nc.dram_tensor("out_0_dram", (BATCH, SEQ, EMB), _mybir.dt.float32, kind="ExternalOutput").ap()
    decoder(nc, args, out)
    r = _run(nc, [arrays], core_ids=[0])
    return r.results[0]["out_0_dram"]
```
